# Optimizing a Trainium2 kernel written in Bass

```python
import numpy as np
import jax
import jax.numpy as jnp

def _softmax(x, axis=-1):
    return jax.nn.softmax(x, axis=axis)

def _gelu(x):
    return jax.nn.gelu(x, approximate=True)

def _silu(x):
    return jax.nn.silu(x)

def _sigmoid(x):
    return jax.nn.sigmoid(x)

def _layernorm(x, axis=-1, eps=1e-05):
    m = jnp.mean(x, axis=axis, keepdims=True)
    v = jnp.var(x, axis=axis, keepdims=True)
    return (x - m) / jnp.sqrt(v + eps)

def _scatter_add(tgt, idx, src, axis=0):
    return tgt.at[idx].add(src)

def _segment_sum(src, seg, n):
    return jax.ops.segment_sum(src, seg, n)
kernel_name = 'mk_vit_tower_cls_d1_tok_img768_r4_7d6f1a'

def setup_inputs(seed: int=0):
    np.random.seed(seed)
    _w = jnp.asarray

    def _rec_inputs():
        import jax
        import jax.numpy as jnp
        _rk = jax.random.key(seed)
        x = -9.30917e-05 + 1.0002 * jax.random.normal(jax.random.fold_in(_rk, 1), (16, 3, 96, 96), jnp.float32)
        cls_tok = 0.02 * jax.random.normal(jax.random.fold_in(_rk, 5), (1, 1, 192), jnp.float32)
        return (x, cls_tok)
    x, cls_tok = _rec_inputs()

    def _L0_tok_setup():
        import jax, jax.numpy as jnp
        import numpy as np
        PATCH = 16
        EPS = 1e-05

        def _shift(x, pad_spec):
            l, r, t, b = pad_spec
            H, W = (x.shape[2], x.shape[3])
            xp = jnp.pad(x, ((0, 0), (0, 0), (max(t, 0), max(b, 0)), (max(l, 0), max(r, 0))))
            h0 = -t if t < 0 else 0
            w0 = -l if l < 0 else 0
            return xp[:, :, h0:h0 + H, w0:w0 + W]
        key = jax.random.key(seed)
        k1, k2 = jax.random.split(key)
        B, C, H, Wd = (32, 3, 224, 224)
        patch_dim = PATCH * PATCH * 5 * C
        dim = 192
        x = jax.random.normal(k1, (B, C, H, Wd), dtype=jnp.float32)
        ln_gamma = jnp.ones((patch_dim,), dtype=jnp.float32)
        ln_beta = jnp.zeros((patch_dim,), dtype=jnp.float32)
        W = jax.random.normal(k2, (patch_dim, dim), dtype=jnp.float32) * patch_dim ** (-0.5)
        b = jnp.zeros((dim,), dtype=jnp.float32)
        return {'x': x, 'ln_gamma': ln_gamma, 'ln_beta': ln_beta, 'W': W, 'b': b}
    _L0_tok_all = _L0_tok_setup()
    _L0_tok_in = {k: v for k, v in _L0_tok_all.items() if k in ('ln_gamma', 'ln_beta', 'W', 'b')}
    del _L0_tok_all

    def _L0_attn_setup():
        import jax, jax.numpy as jnp
        import numpy as np
        B, T, D, H, MAX_REL = (4, 512, 192, 12, 128)
        HD = D // H
        key = jax.random.key(seed)
        ks = jax.random.split(key, 10)
        s = 0.02
        return {'x': jax.random.normal(ks[0], (B, T, D), dtype=jnp.float32), 'w_q': jax.random.normal(ks[1], (D, D), dtype=jnp.float32) * s, 'b_q': jnp.zeros((D,), dtype=jnp.float32), 'w_k': jax.random.normal(ks[2], (D, D), dtype=jnp.float32) * s, 'b_k': jnp.zeros((D,), dtype=jnp.float32), 'w_v': jax.random.normal(ks[3], (D, D), dtype=jnp.float32) * s, 'b_v': jnp.zeros((D,), dtype=jnp.float32), 'w_o': jax.random.normal(ks[4], (D, D), dtype=jnp.float32) * s, 'b_o': jnp.zeros((D,), dtype=jnp.float32), 'bias_table': jax.random.normal(ks[5], (2 * MAX_REL + 1, H), dtype=jnp.float32) * s}
    _L0_attn_all = _L0_attn_setup()
    _L0_attn_in = {k: v for k, v in _L0_attn_all.items() if k in ('w_q', 'b_q', 'w_k', 'b_k', 'w_v', 'b_v', 'w_o', 'b_o', 'bias_table')}
    del _L0_attn_all

    def _L0_ffn_setup():
        import jax, jax.numpy as jnp
        import numpy as np
        B, S, D = (4, 256, 192)
        E = 8
        H = 192
        HS = 768
        TOPK_ROUTED = 2
        key = jax.random.key(seed)
        ks = jax.random.split(key, 10)
        w = lambda k, shape: jax.random.normal(k, shape, dtype=jnp.float32) * 0.02
        return {'x': jax.random.normal(ks[0], (B, S, D), dtype=jnp.float32), 'router_w': w(ks[1], (D, E)), 'w_gate': w(ks[2], (E, D, H)), 'w_up': w(ks[3], (E, D, H)), 'w_down': w(ks[4], (E, H, D)), 'ws_gate': w(ks[5], (D, HS)), 'ws_up': w(ks[6], (D, HS)), 'ws_down': w(ks[7], (HS, D)), 'sg_w': w(ks[8], (D, 1)), 'sg_b': jnp.zeros((1,), jnp.float32)}
    _L0_ffn_all = _L0_ffn_setup()
    _L0_ffn_in = {k: v for k, v in _L0_ffn_all.items() if k in ('router_w', 'w_gate', 'w_up', 'w_down', 'ws_gate', 'ws_up', 'ws_down', 'sg_w', 'sg_b')}
    del _L0_ffn_all
    return {'x': x, 'cls_tok': cls_tok, 'L0_tok_ln_gamma': _L0_tok_in['ln_gamma'], 'L0_tok_ln_beta': _L0_tok_in['ln_beta'], 'L0_tok_W': _L0_tok_in['W'], 'L0_tok_b': _L0_tok_in['b'], 'L0_attn_w_q': _L0_attn_in['w_q'], 'L0_attn_b_q': _L0_attn_in['b_q'], 'L0_attn_w_k': _L0_attn_in['w_k'], 'L0_attn_b_k': _L0_attn_in['b_k'], 'L0_attn_w_v': _L0_attn_in['w_v'], 'L0_attn_b_v': _L0_attn_in['b_v'], 'L0_attn_w_o': _L0_attn_in['w_o'], 'L0_attn_b_o': _L0_attn_in['b_o'], 'L0_attn_bias_table': _L0_attn_in['bias_table'], 'L0_ffn_router_w': _L0_ffn_in['router_w'], 'L0_ffn_w_gate': _L0_ffn_in['w_gate'], 'L0_ffn_w_up': _L0_ffn_in['w_up'], 'L0_ffn_w_down': _L0_ffn_in['w_down'], 'L0_ffn_ws_gate': _L0_ffn_in['ws_gate'], 'L0_ffn_ws_up': _L0_ffn_in['ws_up'], 'L0_ffn_ws_down': _L0_ffn_in['ws_down'], 'L0_ffn_sg_w': _L0_ffn_in['sg_w'], 'L0_ffn_sg_b': _L0_ffn_in['sg_b']}

def reference(x, cls_tok, L0_tok_ln_gamma, L0_tok_ln_beta, L0_tok_W, L0_tok_b, L0_attn_w_q, L0_attn_b_q, L0_attn_w_k, L0_attn_b_k, L0_attn_w_v, L0_attn_b_v, L0_attn_w_o, L0_attn_b_o, L0_attn_bias_table, L0_ffn_router_w, L0_ffn_w_gate, L0_ffn_w_up, L0_ffn_w_down, L0_ffn_ws_gate, L0_ffn_ws_up, L0_ffn_ws_down, L0_ffn_sg_w, L0_ffn_sg_b):
    import jax
    import jax.numpy as jnp

    def _L0_tok_ref(x, ln_gamma, ln_beta, W, b):
        import jax, jax.numpy as jnp
        import numpy as np
        PATCH = 16
        EPS = 1e-05

        def _shift(x, pad_spec):
            l, r, t, b = pad_spec
            H, W = (x.shape[2], x.shape[3])
            xp = jnp.pad(x, ((0, 0), (0, 0), (max(t, 0), max(b, 0)), (max(l, 0), max(r, 0))))
            h0 = -t if t < 0 else 0
            w0 = -l if l < 0 else 0
            return xp[:, :, h0:h0 + H, w0:w0 + W]
        shifts = [(1, -1, 0, 0), (-1, 1, 0, 0), (0, 0, 1, -1), (0, 0, -1, 1)]
        xs = jnp.concatenate([x] + [_shift(x, s) for s in shifts], axis=1)
        B, C5, H, Wd = xs.shape
        h, w = (H // PATCH, Wd // PATCH)
        t = xs.reshape(B, C5, h, PATCH, w, PATCH)
        t = t.transpose(0, 2, 4, 3, 5, 1)
        t = t.reshape(B, h * w, PATCH * PATCH * C5)
        mu = jnp.mean(t, axis=-1, keepdims=True)
        var = jnp.var(t, axis=-1, keepdims=True)
        tn = (t - mu) * jax.lax.rsqrt(var + EPS) * ln_gamma + ln_beta
        return jnp.einsum('bnp,pd->bnd', tn, W) + b

    def _L0_attn_ref(x, w_q, b_q, w_k, b_k, w_v, b_v, w_o, b_o, bias_table):
        import jax, jax.numpy as jnp
        import numpy as np
        B, T, D, H, MAX_REL = (4, 512, 192, 12, 128)
        HD = D // H
        Bn, Tn, Dn = x.shape
        max_rel = (bias_table.shape[0] - 1) // 2
        idx = jnp.arange(Tn)[:, None] - jnp.arange(Tn)[None, :]
        idx = jnp.clip(idx, -max_rel, max_rel) + max_rel
        mask = bias_table[idx].mean(-1)
        q = (x @ w_q.T + b_q).reshape(Bn, Tn, H, HD)
        k = (x @ w_k.T + b_k).reshape(Bn, Tn, H, HD)
        v = (x @ w_v.T + b_v).reshape(Bn, Tn, H, HD)
        scale = 1.0 / jnp.sqrt(jnp.asarray(HD, dtype=x.dtype))
        scores = jnp.einsum('bqhd,bkhd->bhqk', q, k) * scale + mask[None, None]
        attn = jax.nn.softmax(scores, axis=-1)
        ctx = jnp.einsum('bhqk,bkhd->bqhd', attn, v).reshape(Bn, Tn, Dn)
        return ctx @ w_o.T + b_o

    def _L0_ffn_ref(x, router_w, w_gate, w_up, w_down, ws_gate, ws_up, ws_down, sg_w, sg_b):
        import jax, jax.numpy as jnp
        import numpy as np
        B, S, D = (4, 256, 192)
        E = 8
        H = 192
        HS = 768
        TOPK_ROUTED = 2
        probs = jax.nn.softmax(x @ router_w, axis=-1)
        gates, idx = jax.lax.top_k(probs, TOPK_ROUTED)
        gates = gates / jnp.sum(gates, axis=-1, keepdims=True)
        n_exp = router_w.shape[1]
        dense_g = jnp.sum(jax.nn.one_hot(idx, n_exp, dtype=x.dtype) * gates[..., None], axis=-2)
        g = jax.nn.silu(jnp.einsum('bsd,edh->bseh', x, w_gate))
        u = jnp.einsum('bsd,edh->bseh', x, w_up)
        expert_out = jnp.einsum('bseh,ehd->bsed', g * u, w_down)
        routed = jnp.einsum('bse,bsed->bsd', dense_g, expert_out)
        shared = jax.nn.silu(x @ ws_gate) * (x @ ws_up) @ ws_down
        alpha = jax.nn.sigmoid(x @ sg_w + sg_b)
        return alpha * shared + (1.0 - alpha) * routed
    h = _L0_tok_ref(x, L0_tok_ln_gamma, L0_tok_ln_beta, L0_tok_W, L0_tok_b)
    h = jnp.concatenate([jnp.broadcast_to(cls_tok, (h.shape[0], 1, h.shape[2])), h], axis=1)
    h = h + _L0_attn_ref(_layernorm(h, axis=-1), L0_attn_w_q, L0_attn_b_q, L0_attn_w_k, L0_attn_b_k, L0_attn_w_v, L0_attn_b_v, L0_attn_w_o, L0_attn_b_o, L0_attn_bias_table)
    h = h + _L0_ffn_ref(_layernorm(h, axis=-1), L0_ffn_router_w, L0_ffn_w_gate, L0_ffn_w_up, L0_ffn_w_down, L0_ffn_ws_gate, L0_ffn_ws_up, L0_ffn_ws_down, L0_ffn_sg_w, L0_ffn_sg_b)
    return h

_drawn_inputs = setup_inputs


def setup_inputs(seed=0):
    import zlib

    import numpy as np

    out = dict(_drawn_inputs(seed))
    spreads = {'L0_tok_ln_gamma': (1.0, 0.2),
     'L0_tok_ln_beta': (0.0, 0.1),
     'L0_tok_b': (0.0, 0.1),
     'L0_attn_b_q': (0.0, 0.8),
     'L0_attn_b_k': (0.0, 0.8),
     'L0_attn_b_v': (0.0, 0.279),
     'L0_attn_b_o': (0.0, 0.1)}
    factors = {'cls_tok': 8.0,
     'L0_attn_w_q': 8.0,
     'L0_attn_w_k': 8.0,
     'L0_attn_w_v': 3.985,
     'L0_attn_bias_table': 8.0,
     'L0_ffn_router_w': 8.0,
     'L0_ffn_w_gate': 8.0,
     'L0_ffn_w_up': 8.0,
     'L0_ffn_w_down': 8.0,
     'L0_ffn_ws_gate': 5.576,
     'L0_ffn_ws_up': 5.551,
     'L0_ffn_ws_down': 5.555,
     'L0_ffn_sg_w': 8.0}
    for name, (base, spread) in spreads.items():
        noise = np.random.default_rng([zlib.crc32(name.encode()), seed]).standard_normal(out[name].shape)
        drawn = base * np.exp(spread * noise) if base else spread * noise
        out[name] = jnp.asarray(drawn.astype(out[name].dtype))
    for name, factor in factors.items():
        out[name] = (out[name] * factor).astype(out[name].dtype)
    return out
```

```python
from contextlib import ExitStack

import concourse.bass as bass
from concourse import mybir

F32 = mybir.dt.float32
F16 = mybir.dt.float16
ALU = mybir.AluOpType
ACT = mybir.ActivationFunctionType
AX = mybir.AxisListType

P = 128
IMAGES, POSITIONS, D = 16, 37, 192
N = IMAGES * POSITIONS
HALF = N // 2
TILES = 5
NPAD = TILES * P
REST = N - 4 * P
PATCH_DIM = 16 * 16 * 15
EPS = 1e-5

INNER, RING, RK = 6, 2, 96
CHUNKS = INNER + RING
SHIFTS = 5

HEADS, HD = 12, 16
GROUPS, LANES = 3, 4
BLOCK = GROUPS * POSITIONS
QROWS = 64 + POSITIONS
PAIRS = IMAGES // 2
VW = GROUPS * HD + GROUPS

QC, KC, VC, OC, RC = 0, 384, 768, 960, 1152
AW = RC + 9
CROWS = 97

EXPERTS, HID, SHARED = 8, 192, 768
FT = (SHARED + EXPERTS * HID) // P
ST = SHARED // P
FCOLS = FT * P
PIECES = 3
PT_ = FT // PIECES

SX, SW, SPIX, SPW, SK, SQ, SP_, SV, SCTX, SH, SG = 64.0, 64.0, 16.0, 256.0, 16.0, 4.0, 256.0, 16.0, 16.0, 16.0, 256.0
XW = SX * SW

CONSTS = 128 + CHUNKS + 1 + D + GROUPS + EXPERTS
VAR_READY = (4, 9, 14)


def f_expert(f):
    pair, k = divmod(f - ST, 3)
    return (2 * pair, 2 * pair + 1) if k == 2 else (2 * pair + k, 2 * pair + k)


def two_experts(f):
    return f >= ST and (f - ST) % 3 == 2


def vit_kernel(nc, x_inner, x_ring, w_inner, w_ring, gb, consts, j_rev, ind, tok_b, cls, tab,
               aw_a, aw_b, aw_c, f_a, f_b, f_d, out):
    with ExitStack() as ctx:
        def sb(name, shape, dt=F32):
            return ctx.enter_context(nc.sbuf_tensor(name, shape, dt))

        def sem(name):
            return ctx.enter_context(nc.semaphore(name))

        PS = ctx.enter_context(nc.psum_tensor("PS", [P, 8, 512], F32))

        xs = sb("xs", [P, CHUNKS * N])
        xsv = xs[:, :].rearrange("p (c n) -> p c n", c=CHUNKS)
        slab = sb("slab", [P, SHIFTS * INNER * D])
        slabv = slab[:, :].rearrange("p (s c d) -> p s c d", s=SHIFTS, c=INNER)
        wring = sb("wring", [P, RING, D])
        xsq = sb("xsq", [P, 9 * N])
        xsqv = xsq[:, 0:CHUNKS * N].rearrange("p (c n) -> p c n", c=CHUNKS)
        gbs = sb("gbs", [P, 2, SHIFTS * INNER + RING])
        cst = sb("cst", [P, CONSTS])
        ident = cst[:, 0:128]
        cnt = cst[:, 128:136]
        negm = cst[:, 136:137]
        bmask = cst[:, 137:329]
        bones = cst[:, 329:332]
        cst_rank = cst[:, 332:340]
        jrev = sb("jrev", [POSITIONS, POSITIONS])
        inds = sb("inds", [2, NPAD])
        tokb = sb("tokb", [1, D])
        biasrow = sb("biasrow", [2, D])
        tabs = sb("tabs", [POSITIONS, POSITIONS, HEADS])
        one = sb("one", [1, 1])
        xhl = sb("xhl", [P, CHUNKS * NPAD])
        xhlv = xhl[:, :].bitcast(F16).rearrange("p (k c n) -> p k c n", k=2, c=CHUNKS)
        xh, xl = xhlv[:, 0], xhlv[:, 1]
        wef = sb("we", [P, CHUNKS * D])
        we = wef[:, :].rearrange("p (c d) -> p c d", c=CHUNKS)
        whl = sb("whl", [P, CHUNKS * (2 * D + 1) // 2])
        WHC = CHUNKS * (D + 1) // 2
        wh = whl[:, 0:WHC].bitcast(F16).rearrange("p (c d) -> p c d", c=CHUNKS)
        wl = whl[:, WHC:].bitcast(F16).rearrange("p (c d) -> p c d", c=CHUNKS)
        ones16 = sb("ones16", [P, P], F16)
        ident16 = sb("ident16", [P, P], F16)
        jrep = sb("jrep", [POSITIONS, HEADS, POSITIONS], F16)
        mkf = sb("mkf", [POSITIONS, QROWS])
        mksum = sb("mksum", [POSITIONS, POSITIONS])
        mkh = sb("mkh", [POSITIONS, QROWS], F16)
        mkl = sb("mkl", [POSITIONS, QROWS], F16)
        ssrow = xsq[0:1, 9 * N - NPAD:9 * N]
        csum = sb("csum", [P, D])
        small = sb("small", [P, 48, TILES])
        t1 = sb("t1", [P, TILES, D])
        h1 = sb("h1", [P, TILES, D])
        h2 = sb("h2", [P, TILES, D])
        hn = sb("hn", [P, TILES, 256])
        bst = sb("bst", [P, TILES, 6])
        mv = sb("mv", [P, TILES, 2])
        XAh, XAl, XB = (sb(n, [P, NPAD], F16) for n in ("XAh", "XAl", "XB"))
        XC = sb("XC", [CROWS, NPAD], F16)
        ctxv = wef[:, 0:2 * NPAD].bitcast(F16).rearrange("p (k n) -> p k n", k=4)
        CAh, CAl, CB, CC = ctxv[:, 0], ctxv[:, 1], ctxv[:, 2], ctxv[0:CROWS, 3]
        awst = sb("awst", [P, 3, AW])
        WAh, WAl, WB = (sb(n, [P, AW], F16) for n in ("WAh", "WAl", "WB"))
        WC = sb("WC", [CROWS, AW], F16)
        KFC = 2 * LANES * 4 * BLOCK
        kf = slab[:, KFC:KFC + GROUPS * N].rearrange("p (g n) -> p g n", g=GROUPS)
        kh = xsq[:, KFC:KFC + GROUPS * N // 2].bitcast(F16).rearrange("p (g n) -> p g n", g=GROUPS)
        kq = sb("kq", [P, 3 * GROUPS * N // 2 + 192])
        kqv = kq[:, 0:3 * GROUPS * N // 2].bitcast(F16).rearrange("p (k g n) -> p k g n", k=3, g=GROUPS)
        KK, Q1, Q2 = kqv[:, 0], kqv[:, 1], kqv[:, 2]
        vm = xs[0:BLOCK, 0:IMAGES * D].rearrange("p (b d) -> p b d", b=IMAGES)
        vhl = sb("vhl", [P, IMAGES * LANES * VW])
        vhlv = vhl[0:BLOCK, :].bitcast(F16).rearrange("p (k b r c) -> p k b r c", k=2, b=IMAGES, r=LANES)
        vh, vl = vhlv[:, 0], vhlv[:, 1]
        SCOLS = 4 * BLOCK
        sdif = slab[0:QROWS, 0:2 * LANES * SCOLS].rearrange("p (u r c) -> p u r c", u=2, r=LANES)
        prob = xsq[0:QROWS, 0:2 * LANES * SCOLS].rearrange("p (u r c) -> p u r c", u=2, r=LANES)
        repv = slab[:, 0:2 * LANES * SCOLS].bitcast(F16).rearrange("p (k n) -> p k n", k=4)
        RAh, RAl, RB, RC_ = repv[:, 0], repv[:, 1], repv[:, 2], repv[0:CROWS, 3]
        mx = sb("mx", [QROWS, 2, LANES, 12])
        ptv = xhl[0:BLOCK, 0:PAIRS * LANES * QROWS].bitcast(F16).rearrange(
            "p (k b r q) -> p k b r q", k=2, b=PAIRS, r=LANES)
        PTh, PTl = ptv[:, 0], ptv[:, 1]
        rden = sb("rden", [QROWS, PAIRS, LANES, GROUPS])
        cn = awst[0:QROWS, :, :].rearrange("p a b -> p (a b)")[:, 0:PAIRS * 256].rearrange(
            "p (b d) -> p b d", b=PAIRS)
        PC = PT_ * P
        stage = sb("stage", [P, 4 * PC + PT_ * D])
        piece0 = sb("piece0", [P, 3 * PC + PT_ * D])

        def stages(p):
            r = (stage, xhl)[p % 2]
            ab = r[:, 0:4 * PC].rearrange("p (k g c) -> p k g c", k=2, g=2)
            return ab[:, 0], ab[:, 1], r[:, 4 * PC:4 * PC + PT_ * D].rearrange("p (f d) -> p f d", f=PT_)

        def split(p):
            r = (piece0, slab, xsq)[p]
            up = r[:, 0:3 * PC].bitcast(F16).rearrange("p (k g c) -> p k g c", k=3, g=2)
            dn = r[:, 3 * PC:3 * PC + PT_ * D].bitcast(F16).rearrange("p (k f d) -> p k f d", k=2, f=PT_)
            return up[:, 0], up[:, 1], up[:, 2], dn[:, 0], dn[:, 1]

        Gb = xs[:, 0:EXPERTS * N].rearrange("p (e n) -> p e n", e=EXPERTS)
        g8 = whl[:, 0:480].rearrange("p (k t e) -> p k t e", k=12, t=TILES)
        lg = whl[:, 480:525].rearrange("p (t e) -> p t e", t=TILES)
        Gf = whl[:, 525:565].rearrange("p (t e) -> p t e", t=TILES)
        Gh = sb("Gh", [P, TILES, EXPERTS], F16)
        Gl = sb("Gl", [P, TILES, EXPERTS], F16)
        work = vhl[:, 0:7 * HALF].rearrange("p (k n) -> p k n", k=7)
        silu, sgate, hf = work[:, 0:2], work[:, 2:4], work[:, 4:7]
        ABUF = 3
        ahlv = kq[:, 0:ABUF * NPAD].bitcast(F16).rearrange("p (k b n) -> p k b n", k=2, b=ABUF)
        ah, al = ahlv[:, 0], ahlv[:, 1]
        acc = t1
        fin = hn

        d_x = [sem(f"d_x{i}") for i in range(4)]
        d_w = [sem(f"d_w{i}") for i in range(SHIFTS + 1)]
        d_gb, d_cst, d_rows, d_tab, d_aw = sem("d_gb"), sem("d_cst"), sem("d_rows"), sem("d_tab"), sem("d_aw")
        d_f = [sem(f"d_f{i}") for i in range(PIECES)]
        d_out = sem("d_out")
        names = """p_ss p_bw p_main p_bias p_t p_k p_q p_v p_s p_pt p_av p_ct p_wo p_r p_gb p_gu p_dn
                   a_xh a_xsq a_ss a_bw a_cs a_aw a_wh a_sqrt a_hi a_kf a_q1 a_vh a_exp a_pth a_chi a_e a_sig a_gb
                   a_fw a_silu a_ah
                   v_one v_cst v_pad v_jm v_xl v_fold v_wl v_awl v_mk v_stat v_h v_hn v_lo v_kh v_kk v_q2 v_vm v_xr v_sg v_max v_sub
                   v_ptl v_cn v_rd v_clo v_lg v_gate v_gx v_fw v_hf v_acc v_fin v_bn
                   g_pad g_vl g_sg g_al g_dup""".split()
        S = {n: sem(n) for n in names}

        def bank(b, rows=P):
            return PS[0:rows, b, :]

        def xparts(cols, kc=CROWS):
            return [XAh[:, cols], XAl[:, cols], XAh[:, cols], XB[:, cols], XC[0:kc, cols]]

        def cparts(cols):
            return [CAh[:, cols], CAl[:, cols], CAh[:, cols], CB[:, cols], CC[:, cols]]

        def wparts(c0, c1):
            return [WAh[:, c0:c1], WAh[:, c0:c1], WAl[:, c0:c1], WB[:, c0:c1], WC[:, c0:c1]]

        def pair_cols(C, p, rows):
            c0 = 2 * p * POSITIONS
            return C[0:rows, c0:c0 + 2 * POSITIONS].rearrange("p (b q) -> p b q", b=2)

        def pair_queries(b, pr, k, rows):
            c0 = (2 * pr + k) * QROWS
            return PS[0:rows, b, c0:c0 + 2 * 64].rearrange("p (b q) -> p b q", b=2)[:, :, 0:POSITIONS]

        block = ctx.enter_context(nc.Block())

        @block.sync
        def _(sp):
            sp.dma_start(cst[:, :], consts).then_inc(d_cst, 16)
            for i in range(3):
                sp.dma_start(xsv[:, 2 * i:2 * i + 2, :], x_inner[:, 2 * i:2 * i + 2, :]).then_inc(d_x[i], 16)
            sp.dma_start(xsv[0:RK, INNER:CHUNKS, :], x_ring).then_inc(d_x[3], 16)
            sp.dma_start(gbs[:, :, :], gb).then_inc(d_gb, 16)
            for s in range(SHIFTS):
                sp.dma_start(slabv[:, s], w_inner[s]).then_inc(d_w[s], 16)
                if s == 0:
                    sp.dma_start(wring[0:RK, :, :], w_ring).then_inc(d_w[SHIFTS], 16)
                    sp.dma_start(tokb[:, :], tok_b).then_inc(d_rows, 16)
                    sp.dma_start(biasrow[1:2, :], cls).then_inc(d_rows, 16)
                    sp.dma_start(inds[:, :], ind).then_inc(d_rows, 16)
            sp.dma_start(tabs[:, :, :], tab).then_inc(d_tab, 16)
            sp.dma_start(jrev[:, :], j_rev).then_inc(d_tab, 16)
            sp.dma_start(awst[:, 0, :], aw_a).then_inc(d_aw, 16)
            sp.dma_start(awst[:, 1, :], aw_b).then_inc(d_aw, 16)
            sp.dma_start(awst[0:CROWS, 2, :], aw_c).then_inc(d_aw, 16)
            for p in range(PIECES):
                if p == 1:
                    sp.wait_ge(S["p_av"], PAIRS)
                if p == 2:
                    sp.wait_ge(S["a_fw"], 3)
                    sp.wait_ge(S["v_fw"], 3)
                cols = slice(p * PC, (p + 1) * PC)
                sa, sbb, sd = stages(p)
                sp.dma_start(sa, f_a[:, :, cols]).then_inc(d_f[p], 16)
                sp.dma_start(sbb, f_b[:, :, cols]).then_inc(d_f[p], 16)
                sp.dma_start(sd, f_d[:, p * PT_:(p + 1) * PT_, :]).then_inc(d_f[p], 16)
            for t in range(TILES):
                rows = min(P, N - t * P)
                sp.wait_ge(S["v_fin"], t + 1)
                sp.dma_start(out[t * P:t * P + rows, :], fin[0:rows, t, 0:D]).then_inc(d_out, 16)
            sp.wait_ge(d_out, 16 * TILES)

        @block.tensor
        def _(pe):
            mm = nc.tensor.matmul

            pe.wait_ge(d_cst, 16)
            for i in range(4):
                pe.wait_ge(S["a_xsq"], i + 1)
                for j in (2 * i, 2 * i + 1):
                    K = P if j < INNER else RK
                    for half in range(2):
                        last = mm(PS[0:1, half, 0:HALF], cnt[0:K, j:j + 1], xsqv[0:K, j, half * HALF:(half + 1) * HALF],
                                  start=(j == 0), stop=(j == CHUNKS - 1))
            last.then_inc(S["p_ss"], 1)
            pe.wait_ge(d_gb, 16)
            for s in range(SHIFTS):
                pe.wait_ge(d_w[s], 16)
                for j in range(INNER):
                    mm(PS[0:1, 2, 0:D], gbs[:, 1, s * INNER + j:s * INNER + j + 1], slabv[:, s, j, :],
                       start=(s == 0 and j == 0), stop=False)
            pe.wait_ge(d_w[SHIFTS], 16)
            for j in range(RING):
                mm(PS[0:1, 2, 0:D], gbs[0:RK, 1, 30 + j:31 + j], wring[0:RK, j, :], start=False, stop=False)
            pe.wait_ge(d_rows, 48)
            pe.wait_ge(S["v_one"], 1)
            mm(PS[0:1, 2, 0:D], one[:, :], tokb[:, :], start=False, stop=True).then_inc(S["p_bw"], 1)

            pe.wait_ge(S["v_pad"], 1)
            pe.wait_ge(S["a_cs"], 1)
            for j in range(CHUNKS):
                K = P if j < INNER else RK
                pe.wait_ge(S["a_xh"], j // 2 + 1)
                pe.wait_ge(S["v_xl"], j // 2 + 1)
                pe.wait_ge(S["a_wh"], j // 2 + 1)
                pe.wait_ge(S["v_wl"], j // 2 + 1)
                for t in range(TILES):
                    tok = slice(t * P, (t + 1) * P)
                    o = PS[:, 3 + t // 2, 200 * (t % 2):200 * (t % 2) + D + 1]
                    mm(o, xh[0:K, j, tok], wh[0:K, j, :], start=(j == 0 and t % 2 == 0), stop=False,
                       skip_group_check=True)
                    mm(o, xl[0:K, j, tok], wh[0:K, j, :], start=False, stop=False, skip_group_check=True)
                    mm(o[:, 0:D], xh[0:K, j, tok], wl[0:K, j, :], start=False, stop=(j == CHUNKS - 1),
                       skip_group_check=True)
                for w in (wh, wl):
                    last = mm(PS[:, 5, 200:200 + D], ones16[0:K, :], w[0:K, j, 0:D], start=False,
                              stop=(j == CHUNKS - 1), skip_group_check=True)
            last.then_inc(S["p_main"], 1)
            pe.wait_ge(S["a_ss"], 1)
            pe.wait_ge(S["a_bw"], 1)
            for t in range(TILES):
                tok = slice(t * P, (t + 1) * P)
                mm(PS[:, 2, t:t + 1], ssrow[:, tok], one[:, :], start=(t == 0), stop=True, skip_group_check=True)
                mm(PS[:, (6, 6, 7, 7, 0)[t], D * (t % 2):D * (t % 2) + D], inds[:, tok], biasrow[:, :],
                   start=(t % 2 == 0), stop=True, skip_group_check=True).then_inc(S["p_bias"], 1)

            def transposes(n0, ba, bb, bc):
                for t in range(TILES):
                    pe.wait_ge(S["v_hn"], n0 + t + 1)
                    oa = PS[:, ba, t * P:(t + 1) * P] if t < 4 else PS[:, bc, 0:P]
                    ob = PS[:, bb, t * P:(t + 1) * P] if t < 4 else PS[:, bc, P:2 * P]
                    nc.tensor.transpose(oa, hn[:, t, 0:P], ident)
                    nc.tensor.transpose(ob, hn[:, t, P:2 * P], ident).then_inc(S["p_t"], 1)

            transposes(0, 1, 2, 0)

            pe.wait_ge(S["a_aw"], 3)
            pe.wait_ge(S["v_awl"], 3)
            pe.wait_ge(S["a_hi"], 4)
            pe.wait_ge(S["v_lo"], 4)
            for f in range(12):
                g, half = divmod(f % 6, 2)
                c0 = (KC if f < 6 else QC) + g * P
                if 4 <= f:
                    if f - 4 < 6:
                        pe.wait_ge(S["a_kf"], f - 3)
                    else:
                        pe.wait_ge(S["v_q2"], f - 9)
                cols = slice(half * HALF, (half + 1) * HALF)
                for i, (w, x) in enumerate(zip(wparts(c0, c0 + P), xparts(cols))):
                    last = mm(PS[:, 3 + f % 4, 0:HALF], w, x, start=(i == 0), stop=(i == 4))
                last.then_inc(S["p_k" if f < 6 else "p_q"], 1)

            pe.wait_ge(S["v_xr"], 4)
            for i in range(PAIRS):
                if i >= 4:
                    pe.wait_ge(S["v_vm"], i - 3)
                for b in (0, 1):
                    xr = [x[:, (2 * i + b) * BLOCK:(2 * i + b + 1) * BLOCK] for x in (RAh, RAl, RAh, RB, RC_)]
                    for k, (w, x) in enumerate(zip(wparts(VC, VC + D), xr)):
                        last = mm(PS[0:BLOCK, (7, 0, 1, 2)[i % 4], b * D:(b + 1) * D], x, w,
                                  start=(k == 0 and b == 0), stop=(k == 4), skip_group_check=True)
                last.then_inc(S["p_v"], 1)

            pe.wait_ge(S["v_mk"], 1)
            for u in range(2):
                banks = ((3, 4, 5, 6), (7, 0, 1, 2))[u]
                if u == 0:
                    pe.wait_ge(S["v_kk"], GROUPS)
                    pe.wait_ge(S["v_q2"], 6)
                else:
                    pe.wait_ge(S["v_vm"], PAIRS)
                for r in range(LANES):
                    for w in (mkh, mkl):
                        mm(PS[0:QROWS, banks[r], 0:SCOLS], w[:, :], jrep[:, :, :].rearrange("p h k -> p (h k)"),
                           start=(w is mkh), stop=False, skip_group_check=True)
                for pair in range(4):
                    for bi in (0, 1):
                        b = 2 * (4 * u + pair) + bi
                        tok = slice(b * POSITIONS, (b + 1) * POSITIONS)
                        for g in range(GROUPS):
                            for Q in (Q1, Q2):
                                for r in range(LANES):
                                    rows = slice(32 * r, 32 * r + 32)
                                    col = pair * BLOCK + g * POSITIONS
                                    last = mm(PS[64 * bi:64 * bi + POSITIONS, banks[r], col:col + POSITIONS],
                                              Q[rows, g, tok], KK[rows, g, tok], start=False, stop=(Q is Q2),
                                              skip_group_check=True)
                last.then_inc(S["p_s"], 1)

            def pt(p):
                u, pair = divmod(p, 4)
                pe.wait_ge(S["a_exp"], 4 * u + 4)
                if p >= 2:
                    pe.wait_ge(S["v_ptl"], p - 1)
                for r in range(LANES):
                    last = nc.tensor.transpose(PS[0:BLOCK, 3 + p % 2, r * QROWS:(r + 1) * QROWS],
                                               prob[:, u, r, pair * BLOCK:(pair + 1) * BLOCK],
                                               ident[0:QROWS, 0:QROWS])
                last.then_inc(S["p_pt"], 1)

            def av(p):
                pe.wait_ge(S["a_pth"], p + 1)
                pe.wait_ge(S["v_ptl"], p + 1)
                if p == 0:
                    pe.wait_ge(S["a_vh"], PAIRS + 1)
                    pe.wait_ge(S["g_vl"], PAIRS)
                if p % 2 == 0 and p >= 4:
                    pe.wait_ge(S["v_cn"], p - 2)
                for bi in (0, 1):
                    q0, q1 = (0, 64) if bi == 0 else (64, QROWS)
                    for r in range(LANES):
                        c0 = (p % 2) * LANES * VW + r * VW
                        o = PS[q0:q1, 5 + (p // 2) % 2, c0:c0 + VW]
                        for k, (a, v) in enumerate(((PTh, vh), (PTl, vh), (PTh, vl))):
                            last = mm(o, a[:, p, r, q0:q1], v[:, 2 * p + bi, r, :],
                                      start=(p % 2 == 0 and r == 0 and k == 0), stop=(k == 2),
                                      skip_group_check=True)
                last.then_inc(S["p_av"], 1)

            def ct(p):
                pe.wait_ge(S["v_cn"], p + 1)
                pe.wait_ge(S["g_dup"], p + 1)
                if p == 0:
                    pe.wait_ge(S["v_sub"], 2 * LANES)
                if p >= 4 and p % 2 == 0:
                    pe.wait_ge(S["v_clo"], p - 2)
                    pe.wait_ge(S["a_chi"], p - 2)
                c0 = (p % 2) * 2 * QROWS
                b = (7, 0)[(p // 2) % 2]
                nc.tensor.transpose(PS[:, b, c0:c0 + QROWS], cn[:, p, 0:P], ident[0:QROWS, 0:QROWS])
                nc.tensor.transpose(PS[:, b, c0 + QROWS:c0 + 2 * QROWS], cn[:, p, P:2 * P],
                                    ident[0:QROWS, 0:QROWS]).then_inc(S["p_ct"], 1)

            def wo(t):
                need = min(2 * (t + 1), PAIRS)
                pe.wait_ge(S["a_chi"], need)
                pe.wait_ge(S["v_clo"], need)
                tok = slice(t * P, (t + 1) * P)
                for k, (x, w) in enumerate(zip(cparts(tok), wparts(OC, OC + D))):
                    last = mm(PS[:, (1, 1, 2, 2, 3)[t], D * (t % 2):D * (t % 2) + D], x, w,
                              start=(k == 0 and t % 2 == 0), stop=(k == 4), skip_group_check=True)
                last.then_inc(S["p_wo"], 1)

            for p in range(PAIRS + 2):
                if p < PAIRS:
                    pt(p)
                if 1 <= p <= PAIRS:
                    av(p - 1)
                if p >= 3 and p % 2 == 1:
                    ct(p - 3)
                    ct(p - 2)
            for t in range(TILES):
                wo(t)

            transposes(TILES, 4, 5, 6)

            pe.wait_ge(S["a_hi"], 8)
            pe.wait_ge(S["v_lo"], 8)
            for t in range(TILES):
                tok = slice(t * P, (t + 1) * P)
                for k, (x, w) in enumerate(zip(xparts(tok), wparts(RC, RC + 9))):
                    last = mm(PS[:, 7, 9 * t:9 * t + 9], x, w, start=(t == 0 and k == 0), stop=(k == 4),
                              skip_group_check=True)
            last.then_inc(S["p_r"], 1)

            def gu(i):
                f, half = divmod(i, 2)
                if i % (2 * PT_) == 0:
                    pe.wait_ge(S["a_fw"], 3 * (f // PT_) + 3)
                    pe.wait_ge(S["v_fw"], 3 * (f // PT_) + 3)
                if i >= 2:
                    pe.wait_ge(S["v_hf"], i - 1)
                cols = slice(half * HALF, (half + 1) * HALF)
                Ah, Al, Bw, _, _ = split(f // PT_)
                fc = slice(f % PT_ * P, (f % PT_ + 1) * P)
                for m in range(2):
                    w5 = (Ah[:, m, fc], Ah[:, m, fc], Al[:, m, fc], Bw[:, m, fc], Bw[0:64, m, fc])
                    for k, (w, x) in enumerate(zip(w5, xparts(cols, 64))):
                        last = mm(PS[:, 3 + 2 * (i % 2) + m, 0:HALF], w, x, start=(k == 0), stop=(k == 4))
                last.then_inc(S["p_gu"], 1)

            def gates(k):
                if k == 0:
                    pe.wait_ge(S["v_gx"], 1)
                if k >= 1:
                    pe.wait_ge(S["a_gb"], k)
                for e, t, c0, n in ([(k, t, t * P, P) for t in range(4)] if k < EXPERTS else
                                    [(4 * (k - EXPERTS) + i, 4, i * REST, REST) for i in range(4)]):
                    for G in (Gh, Gl):
                        last = mm(PS[:, 7, c0:c0 + n], G[:, t, e:e + 1].to_broadcast([P, P]), ident16[:, 0:n],
                                  start=(c0 == 0 and G is Gh), stop=(G is Gl), skip_group_check=True)
                last.then_inc(S["p_gb"], 1)

            def down(f):
                pe.wait_ge(S["a_ah"], 2 * f + 2)
                pe.wait_ge(S["g_al"], 2 * f + 2)
                if f == 0:
                    pe.wait_ge(S["v_pad"], 2)
                if f == ST:
                    pe.wait_ge(S["v_acc"], TILES)
                Dh, Dl = split(f // PT_)[3:]
                for t in range(TILES):
                    tok = slice(t * P, (t + 1) * P)
                    o = PS[:, t // 2, D * (t % 2):D * (t % 2) + D]
                    for k, (a, w) in enumerate(((ah, Dh), (al, Dh), (ah, Dl))):
                        last = mm(o, a[:, f % ABUF, tok], w[:, f % PT_, :], start=(f in (0, ST) and t % 2 == 0 and k == 0),
                                  stop=(f in (ST - 1, FT - 1) and k == 2), skip_group_check=True)
                last.then_inc(S["p_dn"], 1)

            for f in range(FT + 1):
                for half in range(2):
                    if f < FT:
                        gu(2 * f + half)
                    k = 2 * (f - 1) + half
                    if 0 <= k < EXPERTS + 2:
                        gates(k)
                if f >= 1:
                    down(f - 1)

        @block.scalar
        def _(act):
            A = nc.scalar.activation
            for i in range(4):
                act.wait_ge(d_x[i], 16)
                K = P if i < 3 else RK
                src = xsv[0:K, 2 * i:2 * i + 2, :]
                A(xsqv[0:K, 2 * i:2 * i + 2, :], src, ACT.Square).then_inc(S["a_xsq"], 1)
                A(xh[0:K, 2 * i:2 * i + 2, 0:N], src, ACT.Copy, scale=SPIX).then_inc(S["a_xh"], 1)
            act.wait_ge(d_cst, 16)
            A(wh[:, :, D:D + 1].rearrange("p c o -> p (c o)"), cnt, ACT.Copy).then_inc(S["a_cs"], 1)
            act.wait_ge(S["p_ss"], 1)
            act.wait_ge(S["v_pad"], 1)
            A(ssrow[:, 0:N].rearrange("p (b n) -> p b n", b=2), PS[0:1, 0:2, 0:HALF], ACT.Copy).then_inc(S["a_ss"], 1)
            for i in range(4):
                K = P if i < 3 else RK
                act.wait_ge(S["v_fold"], (SHIFTS - 1) * INNER + 2 * i + 2)
                A(wh[0:K, 2 * i:2 * i + 2, 0:D], we[0:K, 2 * i:2 * i + 2, :], ACT.Copy, scale=SPW).then_inc(S["a_wh"], 1)
            act.wait_ge(S["p_bw"], 1)
            act.wait_ge(d_rows, 48)
            A(biasrow[0:1, :], PS[0:1, 2, 0:D], ACT.Copy).then_inc(S["a_bw"], 1)
            act.wait_ge(d_aw, 48)
            A(WAh[:, :], awst[:, 0, :], ACT.Copy, scale=SW).then_inc(S["a_aw"], 1)
            A(WB[:, :], awst[:, 1, :], ACT.Copy, scale=SW).then_inc(S["a_aw"], 1)
            A(WC[:, :], awst[0:CROWS, 2, :], ACT.Copy, scale=SW).then_inc(S["a_aw"], 1)

            def ffn_weights(p):
                act.wait_ge(d_f[p], 48)
                Ah, _, Bw, Dh, _ = split(p)
                for W, st in zip((Ah, Bw, Dh), stages(p)):
                    A(W, st, ACT.Copy, scale=SW).then_inc(S["a_fw"], 1)

            act.wait_ge(S["p_main"], 1)
            A(csum[:, :], PS[:, 5, 200:200 + D], ACT.Copy).then_inc(S["a_cs"], 1)

            def root(k):
                act.wait_ge(S["v_stat"], VAR_READY[k])
                A(small[:, 10 * k + 1, :], small[:, 10 * k, :], ACT.Sqrt).then_inc(S["a_sqrt"], 1)

            def high_parts(n, ba, bb, bc):
                for k, (dst, src, need) in enumerate((
                        (XAh[:, 0:512], PS[:, ba, :], 4), (XB[:, 0:512], PS[:, bb, :], 4),
                        (XAh[:, 512:NPAD], PS[:, bc, 0:P], 5), (XB[:, 512:NPAD], PS[:, bc, P:2 * P], 5))):
                    act.wait_ge(S["p_t"], TILES * n + need)
                    if n == 1 and k == 0:
                        act.wait_ge(S["p_v"], PAIRS)
                    A(dst, src, ACT.Copy, scale=SX).then_inc(S["a_hi"], 1)

            root(0)
            root(1)
            high_parts(0, 1, 2, 0)
            for f in range(6):
                g, half = divmod(f, 2)
                act.wait_ge(S["p_k"], f + 1)
                A(kf[:, g, half * HALF:(half + 1) * HALF], PS[:, 3 + f % 4, 0:HALF], ACT.Copy,
                  scale=SK / XW).then_inc(S["a_kf"], 1)
            for f in range(6):
                g, half = divmod(f, 2)
                act.wait_ge(S["p_q"], f + 1)
                A(Q1[:, g, half * HALF:(half + 1) * HALF], PS[:, 3 + (f + 6) % 4, 0:HALF], ACT.Copy,
                  scale=SQ / XW).then_inc(S["a_q1"], 1)
            act.wait_ge(S["g_pad"], 1)
            A(vh[:, :, :, GROUPS * HD:VW].rearrange("p b r o -> p (b r) o"),
              bones[0:BLOCK, :].unsqueeze(1).to_broadcast([BLOCK, IMAGES * LANES, GROUPS]),
              ACT.Copy).then_inc(S["a_vh"], 1)
            for i in range(PAIRS):
                act.wait_ge(S["v_vm"], i + 1)
                A(vh[:, 2 * i:2 * i + 2, :, 0:GROUPS * HD],
                  vm[:, 2 * i:2 * i + 2, :].rearrange("p b (r c) -> p b r c", r=LANES),
                  ACT.Copy).then_inc(S["a_vh"], 1)
            for u in range(2):
                for r in range(LANES):
                    act.wait_ge(S["v_sub"], 4 * u + r + 1)
                    A(prob[:, u, r, :], sdif[:, u, r, :], ACT.Exp, scale=1.0 / (SK * SQ * 4)).then_inc(S["a_exp"], 1)

            def ctx_high(i):
                act.wait_ge(S["p_ct"], 2 * i + 2)
                b = (7, 0)[i % 2]
                for k, C in enumerate((CAh, CB)):
                    for pr in (0, 1):
                        last = A(pair_cols(C, 2 * i + pr, P), pair_queries(b, pr, k, P), ACT.Copy)
                last.then_inc(S["a_chi"], 2)

            for p in range(PAIRS + 3):
                if p < PAIRS:
                    act.wait_ge(S["p_pt"], p + 1)
                    A(PTh[:, p].rearrange("p r q -> p (r q)"), PS[0:BLOCK, 3 + p % 2, 0:LANES * QROWS], ACT.Copy,
                      scale=SP_).then_inc(S["a_pth"], 1)
                if p >= 3 and p % 2 == 0:
                    ctx_high(p // 2 - 2)
            ffn_weights(0)
            root(2)
            high_parts(1, 4, 5, 6)
            act.wait_ge(S["v_gate"], 1)
            A(g8[:, 1], g8[:, 0], ACT.Exp).then_inc(S["a_e"], 1)
            act.wait_ge(S["v_lg"], 1)
            A(small[:, 30, :], lg[:, :, 8], ACT.Sigmoid).then_inc(S["a_sig"], 1)
            A(small[:, 31, :], lg[:, :, 8], ACT.Sigmoid, scale=-1.0).then_inc(S["a_sig"], 1)

            def silu_step(i):
                act.wait_ge(S["p_gu"], i + 1)
                if i >= 2:
                    act.wait_ge(S["v_hf"], i - 1)
                A(silu[:, i % 2, :], PS[:, 3 + 2 * (i % 2), 0:HALF], ACT.Silu, scale=1.0 / XW).then_inc(S["a_silu"], 1)

            def act_high(i):
                f, half = divmod(i, 2)
                act.wait_ge(S["v_hf"], i + 1)
                if half == 0 and f >= ABUF:
                    act.wait_ge(S["p_dn"], f - ABUF + 1)
                A(ah[:, f % ABUF, half * HALF:(half + 1) * HALF], hf[:, i % 3, :], ACT.Copy).then_inc(S["a_ah"], 1)

            def gate_copy(k):
                act.wait_ge(S["p_gb"], k + 1)
                if k < EXPERTS:
                    dst, n = Gb[:, k, 0:512], 512
                    A(dst, PS[:, 7, 0:512], ACT.Copy, scale=1.0 / SG).then_inc(S["a_gb"], 1)
                else:
                    e = 4 * (k - EXPERTS)
                    A(Gb[:, e:e + 4, 512:N], PS[:, 7, 0:4 * REST].rearrange("p (e n) -> p e n", e=4), ACT.Copy,
                      scale=1.0 / SG).then_inc(S["a_gb"], 1)

            for i in range(2 * FT + 1):
                if i < 2 * FT:
                    silu_step(i)
                if i >= 1:
                    act_high(i - 1)
                if i == 5:
                    ffn_weights(1)
                if i == 17:
                    ffn_weights(2)
                k = i - 3
                if 0 <= k < EXPERTS + 2:
                    gate_copy(k)

        @block.gpsimd
        def _(pool):
            G = nc.gpsimd
            G.memset(vl[:, :, :, :].rearrange("p b r c -> p (b r c)"), 0.0).then_inc(S["g_pad"], 1)
            pool.wait_ge(S["g_pad"], 1)
            for i in range(PAIRS):
                pool.wait_ge(S["a_vh"], i + 2)
                G.tensor_tensor(vl[:, 2 * i:2 * i + 2, :, 0:GROUPS * HD],
                                vm[:, 2 * i:2 * i + 2, :].rearrange("p b (r c) -> p b r c", r=LANES),
                                vh[:, 2 * i:2 * i + 2, :, 0:GROUPS * HD], ALU.subtract).then_inc(S["g_vl"], 1)
            for p in range(PAIRS):
                pool.wait_ge(S["v_cn"], p + 1)
                G.tensor_copy(cn[:, p, D:256], cn[:, p, P:D]).then_inc(S["g_dup"], 1)

            def gated(i):
                f, half = divmod(i, 2)
                n = i - 2 * ST
                if n == 0:
                    pool.wait_ge(S["a_gb"], EXPERTS + 2)
                pool.wait_ge(S["a_silu"], i + 1)
                if n >= 2:
                    pool.wait_ge(S["v_hf"], i - 1)
                cols = slice(half * HALF, (half + 1) * HALF)
                G.tensor_tensor(sgate[:, i % 2, :], silu[:, i % 2, :], Gb[:, f_expert(f)[0], cols],
                                ALU.mult).then_inc(S["g_sg"], 1)

            def act_low(i):
                f, half = divmod(i, 2)
                cols = slice(half * HALF, (half + 1) * HALF)
                pool.wait_ge(S["a_ah"], i + 1)
                if half == 0 and f >= ABUF:
                    pool.wait_ge(S["p_dn"], f - ABUF + 1)
                G.tensor_tensor(al[:, f % ABUF, cols], hf[:, i % 3, :], ah[:, f % ABUF, cols],
                                ALU.subtract).then_inc(S["g_al"], 1)

            for i in range(2 * FT + 1):
                if 2 * ST <= i < 2 * FT and not two_experts(i // 2):
                    gated(i)
                if i >= 1:
                    act_low(i - 1)

        @block.vector
        def _(dve):
            V = nc.vector
            V.memset(one[:, :], 1.0).then_inc(S["v_one"], 1)
            V.memset(xh[:, :, N:NPAD], 0.0)
            V.memset(xl[:, :, N:NPAD], 0.0)
            V.memset(ones16[:, :], 1.0)
            V.memset(XC[64:CROWS, :], SX)
            V.memset(mkf[:, :], 0.0).then_inc(S["v_jm"], 1)
            V.memset(ssrow[:, N:NPAD], 0.0).then_inc(S["v_pad"], 1)
            dve.wait_ge(d_cst, 16)
            V.tensor_copy(ident16[:, :], ident).then_inc(S["v_cst"], 1)
            for i in range(4):
                K = P if i < 3 else RK
                dve.wait_ge(S["a_xh"], i + 1)
                V.scalar_tensor_tensor(out=xl[0:K, 2 * i:2 * i + 2, 0:N], in0=xsv[0:K, 2 * i:2 * i + 2, :], scalar=SPIX,
                                       in1=xh[0:K, 2 * i:2 * i + 2, 0:N], op0=ALU.mult,
                                       op1=ALU.subtract).then_inc(S["v_xl"], 1)
            dve.wait_ge(d_gb, 16)
            for s in range(SHIFTS):
                dve.wait_ge(d_w[s], 16)
                for j in range(INNER):
                    gamma = gbs[:, 0, s * INNER + j:s * INNER + j + 1]
                    if s == 0:
                        V.tensor_scalar(we[:, j, :], slabv[:, s, j, :], gamma, None, ALU.mult).then_inc(S["v_fold"], 1)
                    else:
                        dve.wait_ge(S["v_fold"], (s - 1) * INNER + j + 1)
                        V.scalar_tensor_tensor(out=we[:, j, :], in0=slabv[:, s, j, :], scalar=gamma, in1=we[:, j, :],
                                               op0=ALU.mult, op1=ALU.add).then_inc(S["v_fold"], 1)
            dve.wait_ge(d_w[SHIFTS], 16)
            for j in range(RING):
                V.tensor_scalar(we[0:RK, INNER + j, :], wring[0:RK, j, :], gbs[0:RK, 0, 30 + j:31 + j], None,
                                ALU.mult).then_inc(S["v_fold"], 1)
            for i in range(4):
                K = P if i < 3 else RK
                dve.wait_ge(S["a_wh"], i + 1)
                V.scalar_tensor_tensor(out=wl[0:K, 2 * i:2 * i + 2, :], in0=we[0:K, 2 * i:2 * i + 2, :], scalar=SPW,
                                       in1=wh[0:K, 2 * i:2 * i + 2, 0:D], op0=ALU.mult,
                                       op1=ALU.subtract).then_inc(S["v_wl"], 1)
            dve.wait_ge(S["v_wl"], 4)
            for C in (CAh, CAl, CB):
                V.memset(C[:, N:NPAD], 0.0)
            V.memset(CC[0:64, N:NPAD], 0.0)
            V.memset(CC[64:CROWS, :], SCTX)
            dve.wait_ge(d_tab, 32)
            V.tensor_reduce(mksum[:, :], tabs[:, :, :], AX.X, ALU.add).then_inc(S["v_jm"], 1)
            V.tensor_scalar(jrep[:, :, :], jrev[:, :].unsqueeze(1).to_broadcast([POSITIONS, HEADS, POSITIONS]),
                            16.0, None, ALU.mult)
            dve.wait_ge(S["v_jm"], 2)
            V.tensor_scalar(mkf[:, 0:POSITIONS], mksum[:, :], 16.0 / HEADS, None, ALU.mult)
            V.tensor_scalar(mkf[:, 64:QROWS], mksum[:, :], 16.0 / HEADS, None, ALU.mult).then_inc(S["v_jm"], 1)
            dve.wait_ge(S["v_jm"], 3)
            V.tensor_copy(mkh[:, :], mkf[:, :]).then_inc(S["v_jm"], 1)
            dve.wait_ge(S["v_jm"], 4)
            V.tensor_tensor(mkl[:, :], mkf[:, :], mkh[:, :], ALU.subtract).then_inc(S["v_mk"], 1)
            for k, (W, rows, a) in enumerate(((WAl, slice(0, P), 0), (WB, slice(64, P), 1), (WC, slice(96, 97), 2))):
                dve.wait_ge(S["a_aw"], k + 1)
                hi = WAh if k == 0 else W
                V.scalar_tensor_tensor(out=W[rows, :], in0=awst[rows, a, :], scalar=SW, in1=hi[rows, :],
                                       op0=ALU.mult, op1=ALU.subtract).then_inc(S["v_awl"], 1)

            stat = [0]

            def step(instruction):
                instruction.then_inc(S["v_stat"], 1)
                stat[0] += 1
                dve.wait_ge(S["v_stat"], stat[0])

            def rsqrt(k, scale=1.0):
                v, sd, r, a, b, rs, o = (small[:, 10 * k + i, :] for i in (0, 1, 2, 3, 4, 5, 9))
                assert stat[0] == VAR_READY[k]
                dve.wait_ge(S["a_sqrt"], k + 1)
                step(V.reciprocal(r, sd))
                V.tensor_scalar(rs, r, scale, None, ALU.mult)
                step(V.tensor_tensor(a, r, r, ALU.mult))
                step(V.scalar_tensor_tensor(out=b, in0=a, scalar=-0.5, in1=v, op0=ALU.mult, op1=ALU.mult))
                step(V.scalar_tensor_tensor(out=o, in0=b, scalar=1.5, in1=rs, op0=ALU.add, op1=ALU.mult))

            dve.wait_ge(S["p_main"], 1)
            dve.wait_ge(S["p_bias"], TILES)
            dve.wait_ge(S["a_cs"], 2)
            nmean, nsq = small[:, 6, :], small[:, 7, :]
            V.tensor_scalar(small[:, 6, 0:4].rearrange("p (a b) -> p a b", a=2),
                            PS[:, 3:5, 0:400].rearrange("p a (b c) -> p a b c", b=2)[:, :, :, D], -1.0 / PATCH_DIM,
                            None, ALU.mult)
            V.tensor_scalar(small[:, 8, :], PS[:, 2, 0:TILES], 1.0 / PATCH_DIM, None, ALU.mult)
            step(V.tensor_scalar(small[:, 6, 4:5], PS[:, 5, D:D + 1], -1.0 / PATCH_DIM, None, ALU.mult))
            step(V.tensor_tensor(nsq, nmean, nmean, ALU.mult))
            step(V.scalar_tensor_tensor(out=small[:, 3, :], in0=nsq, scalar=-1.0 / SPIX ** 2, in1=small[:, 8, :],
                                        op0=ALU.mult, op1=ALU.add))
            step(V.tensor_scalar(small[:, 0, :], small[:, 3, :], 0.0, EPS, ALU.max, ALU.add))
            for t in range(TILES):
                V.scalar_tensor_tensor(out=t1[:, t, :], in0=csum[:, :], scalar=small[:, 6, t:t + 1],
                                       in1=PS[:, 3 + t // 2, 200 * (t % 2):200 * (t % 2) + D], op0=ALU.mult,
                                       op1=ALU.add).then_inc(S["v_h"], 1)
            rsqrt(0, 1.0 / (SPIX * SPW))

            def residual(n, ops):
                for t in range(TILES):
                    ops(t).then_inc(S["v_h"], 1)
                src = h1 if n == 0 else h2
                for t in range(TILES):
                    dve.wait_ge(S["v_h"], (TILES if n == 0 else 2 * TILES) + t + 1)
                    V.bn_stats(bst[:, t, :], src[:, t, :]).then_inc(S["v_bn"], 1)
                for t in range(TILES):
                    dve.wait_ge(S["v_bn"], 2 * TILES * n + t + 1)
                    V.bn_aggr(mv[:, t, :], bst[:, t, :]).then_inc(S["v_bn"], 1)
                dve.wait_ge(S["v_bn"], 2 * TILES * (n + 1))
                k = n + 1
                step(V.tensor_scalar(small[:, 10 * k, :], mv[:, :, 1], EPS, None, ALU.add))
                rsqrt(k)
                if n == 1:
                    dve.wait_ge(S["p_t"], TILES)
                for t in range(TILES):
                    r = small[:, 10 * k + 9, t:t + 1]
                    V.tensor_scalar(hn[:, t, 0:D], src[:, t, :], mv[:, t, 0:1], r, ALU.subtract, ALU.mult)
                    V.tensor_scalar(hn[:, t, D:256], src[:, t, P:D], mv[:, t, 0:1], r, ALU.subtract,
                                    ALU.mult).then_inc(S["v_hn"], 1)

            def low_parts(n, ba, bb, bc):
                for k, (dst, src, hi) in enumerate((
                        (XAl[:, 0:512], PS[:, ba, :], XAh[:, 0:512]), (XC[0:64, 0:512], PS[0:64, bb, :], XB[0:64, 0:512]),
                        (XAl[:, 512:NPAD], PS[:, bc, 0:P], XAh[:, 512:NPAD]),
                        (XC[0:64, 512:NPAD], PS[0:64, bc, P:2 * P], XB[0:64, 512:NPAD]))):
                    dve.wait_ge(S["a_hi"], 4 * n + (k + 1 if k < 2 else 4))
                    V.scalar_tensor_tensor(out=dst, in0=src, scalar=SX, in1=hi, op0=ALU.mult,
                                           op1=ALU.subtract).then_inc(S["v_lo"], 1)

            dve.wait_ge(S["v_h"], TILES)
            residual(0, lambda t: V.scalar_tensor_tensor(
                out=h1[:, t, :], in0=t1[:, t, :], scalar=small[:, 9, t:t + 1],
                in1=PS[:, (6, 6, 7, 7, 0)[t], D * (t % 2):D * (t % 2) + D], op0=ALU.mult, op1=ALU.add))
            low_parts(0, 1, 2, 0)
            for R, X in ((RAh, XAh), (RAl, XAl), (RB, XB), (RC_, XC)):
                if X is XAh:
                    dve.wait_ge(S["v_lo"], 4)
                V.tensor_copy(R[:, :].rearrange("p (b g q) -> p b g q", b=IMAGES, g=GROUPS),
                              X[:, 0:N].rearrange("p (b q) -> p b q", b=IMAGES).unsqueeze(2).to_broadcast(
                                  [X.shape[0], IMAGES, GROUPS, POSITIONS])).then_inc(S["v_xr"], 1)
            for g in range(GROUPS):
                dve.wait_ge(S["a_kf"], 2 * g + 2)
                V.tensor_copy(kh[:, g, :], kf[:, g, :]).then_inc(S["v_kh"], 1)
                dve.wait_ge(S["v_kh"], g + 1)
                V.scalar_tensor_tensor(out=KK[:, g, :], in0=kh[:, g, :], scalar=negm, in1=kf[:, g, :],
                                       op0=ALU.mult, op1=ALU.add).then_inc(S["v_kk"], 1)
            for f in range(6):
                g, half = divmod(f, 2)
                cols = slice(half * HALF, (half + 1) * HALF)
                dve.wait_ge(S["a_q1"], f + 1)
                V.scalar_tensor_tensor(out=Q2[:, g, cols], in0=PS[:, 3 + (f + 6) % 4, 0:HALF], scalar=SQ / XW,
                                       in1=Q1[:, g, cols], op0=ALU.mult, op1=ALU.subtract).then_inc(S["v_q2"], 1)
            for i in range(PAIRS):
                dve.wait_ge(S["p_v"], i + 1)
                V.scalar_tensor_tensor(
                    out=vm[:, 2 * i:2 * i + 2, :],
                    in0=PS[0:BLOCK, (7, 0, 1, 2)[i % 4], 0:2 * D].rearrange("p (b d) -> p b d", b=2), scalar=SV / XW,
                    in1=bmask[0:BLOCK, :].unsqueeze(1).to_broadcast([BLOCK, 2, D]), op0=ALU.mult,
                    op1=ALU.mult).then_inc(S["v_vm"], 1)
            for u in range(2):
                dve.wait_ge(S["p_s"], u + 1)
                banks = ((3, 4, 5, 6), (7, 0, 1, 2))[u]
                for r in range(LANES):
                    s = PS[0:QROWS, banks[r], 0:SCOLS].rearrange("p (h k) -> p h k", k=POSITIONS)
                    V.tensor_reduce(mx[:, u, r, :], s, AX.X, ALU.max).then_inc(S["v_max"], 1)
                for r in range(LANES):
                    s = PS[0:QROWS, banks[r], 0:SCOLS].rearrange("p (h k) -> p h k", k=POSITIONS)
                    dve.wait_ge(S["v_max"], 4 * u + r + 1)
                    V.tensor_tensor(sdif[:, u, r, :].rearrange("p (h k) -> p h k", k=POSITIONS), s,
                                    mx[:, u, r, :].unsqueeze(2).to_broadcast([QROWS, 12, POSITIONS]),
                                    ALU.subtract).then_inc(S["v_sub"], 1)

            def pt_low(p):
                dve.wait_ge(S["a_pth"], p + 1)
                V.scalar_tensor_tensor(out=PTl[:, p].rearrange("p r q -> p (r q)"),
                                       in0=PS[0:BLOCK, 3 + p % 2, 0:LANES * QROWS], scalar=SP_,
                                       in1=PTh[:, p].rearrange("p r q -> p (r q)"), op0=ALU.mult,
                                       op1=ALU.subtract).then_inc(S["v_ptl"], 1)

            def normalise(p):
                dve.wait_ge(S["p_av"], p // 2 * 2 + 2)
                c0 = (p % 2) * LANES * VW
                o = PS[0:QROWS, 5 + (p // 2) % 2, c0:c0 + LANES * VW].rearrange("p (r c) -> p r c", r=LANES)
                V.reciprocal(rden[:, p], o[:, :, GROUPS * HD:VW]).then_inc(S["v_rd"], 1)
                dve.wait_ge(S["v_rd"], p + 1)
                V.tensor_tensor(cn[:, p, 0:D].rearrange("p (r g d) -> p r g d", r=LANES, g=GROUPS),
                                o[:, :, 0:GROUPS * HD].rearrange("p r (g d) -> p r g d", g=GROUPS),
                                rden[:, p].unsqueeze(3).to_broadcast([QROWS, LANES, GROUPS, HD]),
                                ALU.mult).then_inc(S["v_cn"], 1)

            def ctx_low(i):
                dve.wait_ge(S["a_chi"], 2 * i + 2)
                b = (7, 0)[i % 2]
                for k, (C, hi, rows) in enumerate(((CAl, CAh, P), (CC, CB, 64))):
                    for pr in (0, 1):
                        p = 2 * i + pr
                        last = V.tensor_tensor(pair_cols(C, p, rows), pair_queries(b, pr, k, rows),
                                               pair_cols(hi, p, rows), ALU.subtract)
                last.then_inc(S["v_clo"], 2)

            for p in range(PAIRS + 3):
                if p < PAIRS:
                    pt_low(p)
                if p >= 2 and p % 2 == 0:
                    if p <= PAIRS:
                        normalise(p - 2)
                        normalise(p - 1)
                    if p >= 4:
                        ctx_low(p // 2 - 2)

            def ffn_weights(p):
                Ah, Al, Bw, Dh, Dl = split(p)
                for k, (W, hi, st, r0) in enumerate(zip((Al, Bw, Dl), (Ah, Bw, Dh), stages(p), (0, 64, 0))):
                    dve.wait_ge(S["a_fw"], 3 * p + k + 1)
                    V.scalar_tensor_tensor(out=W[r0:P], in0=st[r0:P], scalar=SW, in1=hi[r0:P], op0=ALU.mult,
                                           op1=ALU.subtract).then_inc(S["v_fw"], 1)

            def add_attention(t):
                dve.wait_ge(S["p_wo"], (2, 2, 4, 4, 5)[t])
                return V.scalar_tensor_tensor(
                    out=h2[:, t, :], in0=PS[:, (1, 1, 2, 2, 3)[t], D * (t % 2):D * (t % 2) + D],
                    scalar=1.0 / (SCTX * SW), in1=h1[:, t, :], op0=ALU.mult, op1=ALU.add)

            V.memset(ah[:, :, N:NPAD], 0.0)
            V.memset(al[:, :, N:NPAD], 0.0).then_inc(S["v_pad"], 1)
            residual(1, add_attention)
            low_parts(1, 4, 5, 6)
            ffn_weights(0)

            gate = [0]

            def gstep(instruction):
                instruction.then_inc(S["v_gate"], 1)
                gate[0] += 1
                dve.wait_ge(S["v_gate"], gate[0])

            def over8(v):
                return v.unsqueeze(2).to_broadcast([P, TILES, 8])

            dve.wait_ge(S["p_r"], 1)
            V.tensor_scalar(lg[:, :, :], PS[:, 7, 0:9 * TILES].rearrange("p (t e) -> p t e", t=TILES), 1.0 / XW, None,
                            ALU.mult).then_inc(S["v_lg"], 1)
            dve.wait_ge(S["v_lg"], 1)
            m1, s1, m2, s2, den, rd_ = (small[:, i, :] for i in (32, 33, 34, 35, 36, 37))
            l8 = lg[:, :, 0:8]
            V.tensor_reduce(m1, l8, AX.X, ALU.max).then_inc(S["v_bn"], 1)
            dve.wait_ge(S["v_bn"], 4 * TILES + 1)
            gstep(V.tensor_tensor(g8[:, 0], l8, over8(m1), ALU.subtract))
            rank = cst_rank[:, :].unsqueeze(1).to_broadcast([P, TILES, 8])
            gstep(V.tensor_tensor(g8[:, 2], l8, over8(m1), ALU.is_equal))
            gstep(V.tensor_tensor(g8[:, 3], g8[:, 2], rank, ALU.mult))
            gstep(V.tensor_reduce(s1, g8[:, 3], AX.X, ALU.max))
            gstep(V.tensor_tensor(g8[:, 4], rank, over8(s1), ALU.is_equal))
            gstep(V.scalar_tensor_tensor(out=g8[:, 5], in0=g8[:, 4], scalar=-3e38, in1=l8, op0=ALU.mult, op1=ALU.add))
            gstep(V.tensor_reduce(m2, g8[:, 5], AX.X, ALU.max))
            gstep(V.tensor_tensor(g8[:, 6], g8[:, 5], over8(m2), ALU.is_equal))
            gstep(V.tensor_tensor(g8[:, 7], g8[:, 6], rank, ALU.mult))
            gstep(V.tensor_reduce(s2, g8[:, 7], AX.X, ALU.max))
            gstep(V.tensor_tensor(g8[:, 8], rank, over8(s2), ALU.is_equal))
            gstep(V.tensor_tensor(g8[:, 9], g8[:, 8], g8[:, 4], ALU.add))
            dve.wait_ge(S["a_e"], 1)
            gstep(V.tensor_tensor(g8[:, 10], g8[:, 9], g8[:, 1], ALU.mult))
            gstep(V.tensor_reduce(den, g8[:, 10], AX.X, ALU.add))
            gstep(V.reciprocal(rd_, den))
            dve.wait_ge(S["a_sig"], 2)
            gstep(V.tensor_scalar(small[:, 38, :], small[:, 30, :], 1.0 / (SH * SW), None, ALU.mult))
            gstep(V.scalar_tensor_tensor(out=small[:, 39, :], in0=rd_, scalar=SG, in1=small[:, 31, :], op0=ALU.mult,
                                         op1=ALU.mult))
            gstep(V.tensor_tensor(Gf[:, :, :], g8[:, 10], over8(small[:, 39, :]), ALU.mult))
            gstep(V.tensor_copy(Gh[:, :, :], Gf[:, :, :]))
            V.tensor_tensor(Gl[:, :, :], Gf[:, :, :], Gh[:, :, :], ALU.subtract).then_inc(S["v_gx"], 1)

            def product(i):
                dve.wait_ge(S["a_silu"], i + 1)
                src = silu
                f, half = divmod(i, 2)
                if two_experts(f):
                    if i == 2 * ST + 4:
                        dve.wait_ge(S["a_gb"], EXPERTS + 2)
                    cols = slice(half * HALF, (half + 1) * HALF)
                    for a, e in zip((0, 64), f_expert(f)):
                        last = V.tensor_tensor(sgate[a:a + 64, i % 2, :], silu[a:a + 64, i % 2, :],
                                               Gb[a:a + 64, e, cols], ALU.mult)
                    last.then_inc(S["v_sg"], 1)
                    dve.wait_ge(S["v_sg"], 2 * ((f - ST) // 3) + half + 1)
                elif f >= ST:
                    dve.wait_ge(S["g_sg"], 4 * ((f - ST) // 3) + 2 * ((f - ST) % 3) + half + 1)
                if f >= ST:
                    src = sgate
                if i >= 3:
                    dve.wait_ge(S["g_al"], i - 2)
                V.scalar_tensor_tensor(out=hf[:, i % 3, :], in0=PS[:, 4 + 2 * (i % 2), 0:HALF], scalar=SH / XW,
                                       in1=src[:, i % 2, :], op0=ALU.mult, op1=ALU.mult).then_inc(S["v_hf"], 1)

            for i in range(2 * FT):
                product(i)
                if i == 5:
                    ffn_weights(1)
                if i == 17:
                    ffn_weights(2)
                if i == 2 * ST + 1:
                    dve.wait_ge(S["p_dn"], ST)
                    for t in range(TILES):
                        V.scalar_tensor_tensor(out=acc[:, t, :], in0=PS[:, t // 2, D * (t % 2):D * (t % 2) + D],
                                               scalar=small[:, 38, t:t + 1], in1=h2[:, t, :], op0=ALU.mult,
                                               op1=ALU.add).then_inc(S["v_acc"], 1)
            dve.wait_ge(S["p_dn"], FT)
            for t in range(TILES):
                V.scalar_tensor_tensor(out=fin[:, t, 0:D], in0=PS[:, t // 2, D * (t % 2):D * (t % 2) + D],
                                       scalar=1.0 / (SH * SW), in1=acc[:, t, :], op0=ALU.mult,
                                       op1=ALU.add).then_inc(S["v_fin"], 1)


def _fold_layout(v):
    import numpy as np
    w = v.reshape(16, 16, 5, 3, -1)
    inner = np.zeros((SHIFTS, 3, 16, 16, w.shape[-1]), v.dtype)
    m = np.moveaxis(w, (2, 3), (0, 1))
    inner[0] = m[0]
    inner[1, :, :, :-1] = m[1, :, :, 1:]
    inner[2, :, :, 1:] = m[2, :, :, :-1]
    inner[3, :, :-1] = m[3, :, 1:]
    inner[4, :, 1:] = m[4, :, :-1]
    ring = np.stack([m[3, :, 0], m[4, :, 15], m[1, :, :, 0], m[2, :, :, 15]], 1)
    return inner.reshape(SHIFTS, 768, -1), ring.reshape(192, -1)


def _chunks(a, n):
    return a.reshape(n, -1, a.shape[-1]).swapaxes(0, 1)


def _pad_rows(a, rows=P):
    import numpy as np
    out = np.zeros((rows,) + a.shape[1:], a.dtype)
    out[:a.shape[0]] = a
    return out


def _layouts(x, cls_tok, L0_tok_ln_gamma, L0_tok_ln_beta, L0_tok_W, L0_tok_b, L0_attn_w_q, L0_attn_b_q, L0_attn_w_k,
             L0_attn_b_k, L0_attn_w_v, L0_attn_b_v, L0_attn_w_o, L0_attn_b_o, L0_attn_bias_table, L0_ffn_router_w,
             L0_ffn_w_gate, L0_ffn_w_up, L0_ffn_w_down, L0_ffn_ws_gate, L0_ffn_ws_up, L0_ffn_ws_down, L0_ffn_sg_w,
             L0_ffn_sg_b):
    import numpy as np
    f32 = np.float32
    xp = np.zeros((16, 3, 98, 98), x.dtype)
    xp[:, :, 1:97, 1:97] = x
    inner = np.zeros((3, 16, 16, 16, 37), x.dtype)
    ring = np.zeros((3, 4, 16, 16, 37), x.dtype)
    for py in range(6):
        for px in range(6):
            w = xp[:, :, 16 * py:16 * py + 18, 16 * px:16 * px + 18]
            t = 1 + 6 * py + px
            inner[..., t] = w[:, :, 1:17, 1:17].transpose(1, 2, 3, 0)
            for k, side in enumerate((w[:, :, 0, 1:17], w[:, :, 17, 1:17], w[:, :, 1:17, 0], w[:, :, 1:17, 17])):
                ring[:, k, :, :, t] = side.transpose(1, 2, 0)
    wi, wr = _fold_layout(L0_tok_W)
    gi, gr = _fold_layout(L0_tok_ln_gamma[:, None])
    bi, br = _fold_layout(L0_tok_ln_beta[:, None])
    ci, cr = _fold_layout(np.ones((PATCH_DIM, 1), f32))
    cnt = np.concatenate([_chunks(ci.sum(0), INNER)[..., 0], _pad_rows(_chunks(cr, RING)[..., 0])], 1)
    gb = np.stack([np.concatenate([v.reshape(SHIFTS * INNER, P).T, _pad_rows(_chunks(r, RING)[..., 0])], 1)
                   for v, r in ((gi, gr), (bi, br))], 1)
    rows = np.arange(P)
    own = np.repeat(rows[:, None] // POSITIONS == np.arange(GROUPS)[None, :], HD, 1)
    consts = np.concatenate([
        np.eye(P), cnt, np.where(rows % 32 < HD, 0, -1)[:, None], np.tile(own, (1, LANES)),
        rows[:, None] // POSITIONS == np.arange(GROUPS)[None, :],
        np.broadcast_to(np.arange(EXPERTS, 0, -1), (P, EXPERTS))], 1).astype(f32)
    qk = (4 * np.arange(GROUPS)[:, None, None, None] + np.arange(LANES)[:, None, None]) * HD + np.arange(HD)
    qk = np.broadcast_to(qk, (GROUPS, LANES, 2, HD)).reshape(-1)
    vo = ((4 * np.arange(GROUPS)[:, None] + np.arange(LANES)[:, None, None]) * HD + np.arange(HD)).reshape(-1)
    aw = np.concatenate([L0_attn_w_q.T[:, qk], L0_attn_w_k.T[:, qk], L0_attn_w_v.T[:, vo], L0_attn_w_o.T[vo],
                         L0_ffn_router_w, L0_ffn_sg_w], 1)
    ab = np.concatenate([L0_attn_b_q[qk], L0_attn_b_k[qk], L0_attn_b_v[vo], L0_attn_b_o,
                         np.zeros(EXPERTS, f32), L0_ffn_sg_b])
    aw_c = np.zeros((CROWS, AW), f32)
    aw_c[0:64], aw_c[64], aw_c[96] = aw[P:], ab, ab
    fo = np.concatenate([np.arange(128), HID + np.arange(128), np.arange(128, 192), HID + np.arange(128, 192)])
    fo = (2 * HID * np.arange(EXPERTS // 2)[:, None] + fo).reshape(-1)
    up = [np.concatenate([s, e.transpose(1, 0, 2).reshape(D, -1)[:, fo]], 1)
          for s, e in ((L0_ffn_ws_gate, L0_ffn_w_gate), (L0_ffn_ws_up, L0_ffn_w_up))]
    up = np.stack(up, 1)
    down = np.concatenate([L0_ffn_ws_down, L0_ffn_w_down.reshape(-1, D)[fo]], 0)
    first = (np.arange(NPAD) % POSITIONS == 0) & (np.arange(NPAD) < N)
    j = np.arange(POSITIONS)
    mid = (L0_attn_bias_table.shape[0] - 1) // 2
    return {
        "x_inner": _chunks(inner.reshape(768, N), INNER), "x_ring": _chunks(ring.reshape(192, N), RING),
        "w_inner": np.stack([_chunks(v, INNER) for v in wi]), "w_ring": _chunks(wr, RING),
        "gb": gb, "consts": consts, "j_rev": (j[:, None] + j == POSITIONS - 1).astype(f32),
        "ind": np.stack([~first & (np.arange(NPAD) < N), first]).astype(f32),
        "tok_b": L0_tok_b[None, :], "cls": cls_tok.reshape(1, D),
        "tab": L0_attn_bias_table[mid - (POSITIONS - 1) + j[:, None] + j],
        "aw_a": aw[0:P], "aw_b": np.concatenate([aw[P:], aw[P:]], 0), "aw_c": aw_c,
        "f_a": up[0:P], "f_b": np.concatenate([up[P:], up[P:]], 0), "f_d": _chunks(down, FT),
    }


def kernel(**inputs):
    import numpy as _np
    import concourse.bacc as _bacc
    from concourse.bass_utils import run_bass_kernel_spmd as _run

    nc = _bacc.Bacc("TRN2", target_bir_lowering=False, num_devices=1)
    arrays, aps = {}, {}
    for name, a in _layouts(**{k: _np.asarray(v) for k, v in inputs.items()}).items():
        a = _np.ascontiguousarray(a)
        arrays[f"in_{name}_dram"] = a
        aps[name] = nc.dram_tensor(f"in_{name}_dram", a.shape, mybir.dt.from_np(a.dtype), kind="ExternalInput").ap()
    out = nc.dram_tensor("out_0_dram", (N, D), F32, kind="ExternalOutput").ap()
    vit_kernel(nc, out=out, **aps)
    r = _run(nc, [arrays], core_ids=[0])
    return r.results[0]["out_0_dram"].reshape(IMAGES, POSITIONS, D)
```

```python
from contextlib import ExitStack

import concourse.bass as bass
from concourse import mybir

F32 = mybir.dt.float32
F16 = mybir.dt.float16
ALU = mybir.AluOpType
ACT = mybir.ActivationFunctionType
AX = mybir.AxisListType

P = 128
IMAGES, POSITIONS, D = 16, 37, 192
N = IMAGES * POSITIONS
HALF = N // 2
TILES = 5
NPAD = TILES * P
REST = N - 4 * P
PATCH_DIM = 16 * 16 * 15
EPS = 1e-5

INNER, RING, RK = 6, 2, 96
CHUNKS = INNER + RING
SHIFTS = 5

HEADS, HD = 12, 16
GROUPS, LANES = 3, 4
BLOCK = GROUPS * POSITIONS
QROWS = 64 + POSITIONS
PAIRS = IMAGES // 2
VW = GROUPS * HD + GROUPS

QC, KC, VC, OC, RC = 0, 384, 768, 960, 1152
AW = RC + 9
CROWS = 97

EXPERTS, HID, SHARED = 8, 192, 768
FT = (SHARED + EXPERTS * HID) // P
ST = SHARED // P
FCOLS = FT * P
PIECES = 3
PT_ = FT // PIECES

SX, SW, SPIX, SPW, SK, SQ, SP_, SV, SCTX, SH, SG = 64.0, 64.0, 16.0, 256.0, 16.0, 4.0, 256.0, 16.0, 16.0, 16.0, 256.0
XW = SX * SW

GATE_STEP = 6
CONSTS = 128 + 2 * CHUNKS + 1 + D + GROUPS + EXPERTS
VAR_READY = (4, 9, 14)


def f_expert(f):
    pair, k = divmod(f - ST, 3)
    return (2 * pair, 2 * pair + 1) if k == 2 else (2 * pair + k, 2 * pair + k)


def two_experts(f):
    return f >= ST and (f - ST) % 3 == 2


def vit_kernel(nc, x_inner, x_ring, w_inner, w_ring, gb, consts, j_rev, ind, tok_b, cls, tab,
               aw_a, aw_b, aw_c, f_a, f_b, f_d, gate_rows, out):
    with ExitStack() as ctx:
        def sb(name, shape, dt=F32):
            return ctx.enter_context(nc.sbuf_tensor(name, shape, dt))

        def sem(name):
            return ctx.enter_context(nc.semaphore(name))

        PS = ctx.enter_context(nc.psum_tensor("PS", [P, 8, 512], F32))

        xs = sb("xs", [P, CHUNKS * N])
        xsv = xs[:, :].rearrange("p (c n) -> p c n", c=CHUNKS)
        slab = sb("slab", [P, SHIFTS * INNER * D])
        slabv = slab[:, :].rearrange("p (s c d) -> p s c d", s=SHIFTS, c=INNER)
        wring = sb("wring", [P, RING, D])
        xsq = sb("xsq", [P, 9 * N])
        xsqv = xsq[:, 0:CHUNKS * NPAD].rearrange("p (c n) -> p c n", c=CHUNKS)
        gbs = sb("gbs", [P, 2, SHIFTS * INNER + RING])
        cst = sb("cst", [P, CONSTS])
        ident = cst[:, 0:128]
        cnt = cst[:, 128:136]
        negm = cst[:, 136:137]
        bmask = cst[:, 137:329]
        bones = cst[:, 329:332]
        cst_rank = cst[:, 332:340]
        cntroot = cst[:, 340:348]
        jrev = sb("jrev", [QROWS, POSITIONS])
        inds = sb("inds", [2, NPAD])
        tokb = sb("tokb", [1, D])
        biasrow = sb("biasrow", [2, D])
        tabs = sb("tabs", [QROWS, POSITIONS, HEADS])
        one = sb("one", [P, 1])
        xhl = sb("xhl", [P, CHUNKS * NPAD])
        xhlv = xhl[:, :].bitcast(F16).rearrange("p (k c n) -> p k c n", k=2, c=CHUNKS)
        xh, xl = xhlv[:, 0], xhlv[:, 1]
        wef = sb("we", [P, CHUNKS * D])
        we = wef[:, :].rearrange("p (c d) -> p c d", c=CHUNKS)
        whl = sb("whl", [P, CHUNKS * (2 * D + 1) // 2])
        WHC = CHUNKS * (D + 1) // 2
        wh = whl[:, 0:WHC].bitcast(F16).rearrange("p (c d) -> p c d", c=CHUNKS)
        wl = whl[:, WHC:].bitcast(F16).rearrange("p (c d) -> p c d", c=CHUNKS)
        ones16 = sb("ones16", [P, P], F16)
        ident16 = sb("ident16", [P, P], F16)
        jrep = sb("jrep", [QROWS, 6, POSITIONS], F16)
        mkf = sb("mkf", [QROWS, QROWS])
        mksum = sb("mksum", [QROWS, POSITIONS])
        mk = sb("mk", [QROWS, QROWS], F16)
        csum = sb("csum", [P, D])
        small = sb("small", [P, 48, TILES])
        t1 = sb("t1", [P, TILES, D])
        h1 = sb("h1", [P, TILES, D])
        h2 = sb("h2", [P, TILES, D])
        hn = sb("hn", [P, TILES, 256])
        bst = sb("bst", [P, TILES, 6])
        mv = sb("mv", [P, TILES, 2])
        XAh, XAl, XB = (sb(n, [P, NPAD], F16) for n in ("XAh", "XAl", "XB"))
        XC = sb("XC", [CROWS, NPAD], F16)
        ctxv = wef[:, 0:2 * NPAD].bitcast(F16).rearrange("p (k n) -> p k n", k=4)
        CAh, CAl, CB, CC = ctxv[:, 0], ctxv[:, 1], ctxv[:, 2], ctxv[0:CROWS, 3]
        awst = sb("awst", [P, 3, AW])
        WAh, WAl, WB = (sb(n, [P, AW], F16) for n in ("WAh", "WAl", "WB"))
        WC = sb("WC", [CROWS, AW], F16)
        KFC = 2 * LANES * 4 * BLOCK
        kh = xsq[:, KFC:KFC + GROUPS * N // 2].bitcast(F16).rearrange("p (g n) -> p g n", g=GROUPS)
        kq = sb("kq", [P, 3 * GROUPS * N // 2 + 192])
        kqv = kq[:, 0:3 * GROUPS * N // 2].bitcast(F16).rearrange("p (k g n) -> p k g n", k=3, g=GROUPS)
        KK, Q1, Q2 = kqv[:, 0], kqv[:, 1], kqv[:, 2]
        vm = xs[0:BLOCK, 0:IMAGES * D].rearrange("p (b d) -> p b d", b=IMAGES)
        vhl = sb("vhl", [P, IMAGES * LANES * VW])
        vhlv = vhl[0:BLOCK, :].bitcast(F16).rearrange("p (k b r c) -> p k b r c", k=2, b=IMAGES, r=LANES)
        vh, vl = vhlv[:, 0], vhlv[:, 1]
        SCOLS = 2 * BLOCK
        dp = xsq[0:QROWS, 0:4 * LANES * SCOLS].rearrange("p (k u r c) -> p k u r c", k=2, u=2, r=LANES)
        sdif, prob = dp[:, 0], dp[:, 1]
        repv = slab[:, 0:KFC].bitcast(F16).rearrange("p (k n) -> p k n", k=4)
        RAh, RAl, RB, RC_ = repv[:, 0], repv[:, 1], repv[:, 2], repv[0:CROWS, 3]
        mx = sb("mx", [QROWS, 2, LANES, 6])
        ptv = xhl[0:BLOCK, 0:PAIRS * LANES * QROWS].bitcast(F16).rearrange(
            "p (k b r q) -> p k b r q", k=2, b=PAIRS, r=LANES)
        PTh, PTl = ptv[:, 0], ptv[:, 1]
        rden = sb("rden", [QROWS, PAIRS, LANES, GROUPS])
        cn = awst[0:QROWS, :, :].rearrange("p a b -> p (a b)")[:, 0:PAIRS * 256].rearrange(
            "p (b d) -> p b d", b=PAIRS)
        PC = PT_ * P
        stage = sb("stage", [P, 4 * PC + PT_ * D])
        piece0 = sb("piece0", [P, 3 * PC + PT_ * D])

        def stages(p):
            r = (stage, stage, xhl)[p]
            ab = r[:, 0:4 * PC].rearrange("p (k g c) -> p k g c", k=2, g=2)
            return ab[:, 0], ab[:, 1], r[:, 4 * PC:4 * PC + PT_ * D].rearrange("p (f d) -> p f d", f=PT_)

        def split(p):
            r = (piece0, slab, xsq)[p]
            up = r[:, 0:3 * PC].bitcast(F16).rearrange("p (k g c) -> p k g c", k=3, g=2)
            dn = r[:, 3 * PC:3 * PC + PT_ * D].bitcast(F16).rearrange("p (k f d) -> p k f d", k=2, f=PT_)
            return up[:, 0], up[:, 1], up[:, 2], dn[:, 0], dn[:, 1]

        Gb = xs[:, 0:EXPERTS * N].rearrange("p (e n) -> p e n", e=EXPERTS)
        g8 = whl[:, 0:480].rearrange("p (k t e) -> p k t e", k=12, t=TILES)
        lg = whl[:, 480:525].rearrange("p (t e) -> p t e", t=TILES)
        Gf = whl[:, 525:565].rearrange("p (t e) -> p t e", t=TILES)
        GT = sb("GT", [EXPERTS, NPAD])
        work = vhl[:, 0:7 * HALF].rearrange("p (k n) -> p k n", k=7)
        silu, sgate, hf = work[:, 0:2], work[:, 2:4], work[:, 4:7]
        ABUF = 3
        ahlv = kq[:, 0:ABUF * NPAD].bitcast(F16).rearrange("p (k b n) -> p k b n", k=2, b=ABUF)
        ah, al = ahlv[:, 0], ahlv[:, 1]
        acc = t1
        fin = hn

        d_x = [sem(f"d_x{i}") for i in range(4)]
        d_w = [sem(f"d_w{i}") for i in range(SHIFTS + 1)]
        d_gb, d_cst, d_rows, d_tab, d_aw = sem("d_gb"), sem("d_cst"), sem("d_rows"), sem("d_tab"), sem("d_aw")
        d_f = [sem(f"d_f{i}") for i in range(PIECES)]
        d_g = [sem(f"d_g{e}") for e in range(EXPERTS)]
        d_gt, d_out = sem("d_gt"), sem("d_out")
        names = """p_st p_bw p_main p_bias p_t p_k p_q p_v p_s p_pt p_av p_ct p_wo p_r p_gt p_gu p_dn p_end
                   a_first a_xh a_xsq a_ring a_bw a_cs a_aw a_wh a_sqrt a_hi a_kh a_q1 a_vh a_exp a_pth a_chi a_e a_dup a_sig a_gt
                   a_fw a_silu a_ah
                   v_one v_cst v_pad v_jm v_jr v_xl v_fold v_wl v_awl v_mk v_stat v_h v_hn v_lo  v_kk v_q2 v_vm v_xr v_sg v_max v_sub
                   v_ptl v_cn v_rd v_clo v_lg v_gate v_gx v_fw v_hf v_acc v_fin v_al v_bn
                   g_sum g_pad g_vl g_sg g_al g_dup""".split()
        S = {n: sem(n) for n in names}

        def bank(b, rows=P):
            return PS[0:rows, b, :]

        def xparts(cols, kc=CROWS):
            return [XAh[:, cols], XAh[:, cols], XB[:, cols], XAl[:, cols], XC[0:kc, cols]]

        def cparts(cols):
            return [CAh[:, cols], CAh[:, cols], CB[:, cols], CAl[:, cols], CC[:, cols]]

        def wparts(c0, c1):
            return [WAh[:, c0:c1], WAl[:, c0:c1], WB[:, c0:c1], WAh[:, c0:c1], WC[:, c0:c1]]

        def pair_cols(C, p, rows):
            c0 = 2 * p * POSITIONS
            return C[0:rows, c0:c0 + 2 * POSITIONS].rearrange("p (b q) -> p b q", b=2)

        def pair_queries(b, pr, k, rows):
            c0 = (2 * pr + k) * QROWS
            return PS[0:rows, b, c0:c0 + 2 * 64].rearrange("p (b q) -> p b q", b=2)[:, :, 0:POSITIONS]

        block = ctx.enter_context(nc.Block())

        @block.sync
        def _(sp):
            sp.dma_start(cst[:, :], consts).then_inc(d_cst, 16)
            def load_pixels(i):
                rows, src = (P, x_inner[:, 2 * i:2 * i + 2, :]) if i < 3 else (RK, x_ring)
                sp.dma_start(xsv[0:rows, 2 * i:2 * i + 2, :], src).then_inc(d_x[i], 16)

            sp.dma_start(gbs[:, :, :], gb).then_inc(d_gb, 16)
            for s in range(SHIFTS):
                sp.dma_start(slabv[:, s], w_inner[s]).then_inc(d_w[s], 16)
                if s == 0:
                    load_pixels(0)
                if s == 1:
                    sp.dma_start(wring[0:RK, :, :], w_ring).then_inc(d_w[SHIFTS], 16)
                    load_pixels(1)
            load_pixels(2)
            load_pixels(3)
            sp.dma_start(tokb[:, :], tok_b).then_inc(d_rows, 16)
            sp.dma_start(biasrow[1:2, :], cls).then_inc(d_rows, 16)
            sp.dma_start(inds[:, :], ind).then_inc(d_rows, 16)
            for r0 in (0, 64):
                sp.dma_start(tabs[r0:r0 + POSITIONS, :, :], tab).then_inc(d_tab, 16)
                sp.dma_start(jrev[r0:r0 + POSITIONS, :], j_rev).then_inc(d_tab, 16)
            sp.dma_start(awst[:, 0, :], aw_a).then_inc(d_aw, 16)
            sp.dma_start(awst[:, 1, :], aw_b).then_inc(d_aw, 16)
            sp.dma_start(awst[0:CROWS, 2, :], aw_c).then_inc(d_aw, 16)
            for p in range(PIECES):
                if p == 1:
                    sp.wait_ge(S["a_fw"], 6)
                    sp.wait_ge(S["v_fw"], 6)
                if p == 2:
                    sp.wait_ge(S["p_av"], PAIRS)
                cols = slice(p * PC, (p + 1) * PC)
                sa, sbb, sd = stages(p)
                sp.dma_start(sa, f_a[:, :, cols]).then_inc(d_f[p], 16)
                sp.dma_start(sbb, f_b[:, :, cols]).then_inc(d_f[p], 16)
                sp.dma_start(sd, f_d[:, p * PT_:(p + 1) * PT_, :]).then_inc(d_f[p], 16)
            sp.wait_ge(S["a_gt"], 2)
            sp.dma_start(gate_rows[:, :], GT[:, 0:N]).then_inc(d_gt, 16)
            sp.wait_ge(d_gt, 16)
            for e in range(EXPERTS):
                sp.dma_start(Gb[:, e, :], gate_rows[e:e + 1, :].to_broadcast([P, N])).then_inc(d_g[e], 16)
            for t0, t1_ in ((0, 2), (2, 4)):
                sp.wait_ge(S["v_fin"], t1_)
                sp.dma_start(out[t0 * P:t1_ * P, :].rearrange("(t p) d -> p t d", p=P),
                             fin[:, t0:t1_, 0:D]).then_inc(d_out, 16)
            sp.wait_ge(S["v_fin"], TILES)
            sp.dma_start(out[4 * P:N, :], fin[0:REST, 4, 0:D]).then_inc(d_out, 16)
            sp.wait_ge(d_out, 48)

        @block.tensor
        def _(pe):
            mm = nc.tensor.matmul

            def beta_rows(first, chunks, weights):
                for j, (K, w) in enumerate(zip(chunks, weights)):
                    mm(PS[0:1, 2, 0:D], gbs[0:K, 1, first + j:first + j + 1], w, start=(first + j == 0), stop=False)

            pe.wait_ge(d_gb, 16)
            for s in range(SHIFTS):
                pe.wait_ge(d_w[s], 16)
                beta_rows(s * INNER, [P] * INNER, [slabv[:, s, j, :] for j in range(INNER)])
                if s == 1:
                    pe.wait_ge(d_w[SHIFTS], 16)
                    beta_rows(SHIFTS * INNER, [RK] * RING, [wring[0:RK, j, :] for j in range(RING)])
            def square_sums():
                pe.wait_ge(S["g_sum"], 4)
                pe.wait_ge(S["v_pad"], 1)
                for t in range(TILES):
                    last = mm(PS[:, 1, t:t + 1], xsqv[:, 0, t * P:(t + 1) * P], one[:, :], start=(t == 0), stop=True,
                              skip_group_check=True)
                last.then_inc(S["p_st"], 1)

            pe.wait_ge(S["a_cs"], 1)
            for j in range(CHUNKS):
                if j == 2:
                    pe.wait_ge(d_rows, 48)
                    pe.wait_ge(S["v_one"], 1)
                    mm(PS[0:1, 2, 0:D], one[0:1, :], tokb[:, :], start=False, stop=True).then_inc(S["p_bw"], 1)
                if j == INNER + 1:
                    square_sums()
                K = P if j < INNER else RK
                pe.wait_ge(S["a_xh"], j // 2 + 1)
                pe.wait_ge(S["v_xl"], j // 2 + 1)
                pe.wait_ge(S["a_wh"], j // 2 + 1)
                pe.wait_ge(S["v_wl"], j // 2 + 1)
                for t in range(TILES):
                    tok = slice(t * P, (t + 1) * P)
                    o = PS[:, 3 + t // 2, 200 * (t % 2):200 * (t % 2) + D + 1]
                    mm(o, xh[0:K, j, tok], wh[0:K, j, :], start=(j == 0 and t % 2 == 0), stop=False,
                       skip_group_check=True)
                    mm(o, xl[0:K, j, tok], wh[0:K, j, :], start=False, stop=False, skip_group_check=True)
                    mm(o[:, 0:D], xh[0:K, j, tok], wl[0:K, j, :], start=False, stop=(j == CHUNKS - 1),
                       skip_group_check=True)
                for w in (wh, wl):
                    last = mm(PS[:, 5, 200:200 + D], ones16[0:K, :], w[0:K, j, 0:D], start=False,
                              stop=(j == CHUNKS - 1), skip_group_check=True)
            last.then_inc(S["p_main"], 1)
            pe.wait_ge(S["a_bw"], 1)
            for t in range(TILES):
                tok = slice(t * P, (t + 1) * P)
                mm(PS[:, (6, 6, 7, 7, 0)[t], D * (t % 2):D * (t % 2) + D], inds[:, tok], biasrow[:, :],
                   start=(t % 2 == 0), stop=True, skip_group_check=True).then_inc(S["p_bias"], 1)

            def transposes(n0, ba, bb, bc):
                for t in range(TILES):
                    pe.wait_ge(S["v_hn"], n0 + t + 1)
                    oa = PS[:, ba, t * P:(t + 1) * P] if t < 4 else PS[:, bc, 0:P]
                    ob = PS[:, bb, t * P:(t + 1) * P] if t < 4 else PS[:, bc, P:2 * P]
                    nc.tensor.transpose(oa, hn[:, t, 0:P], ident)
                    pe.wait_ge(S["a_dup"], n0 + t + 1)
                    nc.tensor.transpose(ob, hn[:, t, P:2 * P], ident).then_inc(S["p_t"], 1)

            transposes(0, 1, 2, 0)

            def tokens_ready(n, half, k):
                if k in (0, 2):
                    pe.wait_ge(S["a_hi"], 4 * n + 2 * half + (1 if k == 0 else 2))
                if k in (3, 4):
                    pe.wait_ge(S["v_lo"], 4 * n + 2 * half + (1 if k == 3 else 2))

            pe.wait_ge(S["a_aw"], 3)
            pe.wait_ge(S["v_awl"], 3)
            for f in range(12):
                g, half = divmod(f % 6, 2)
                c0 = (KC if f < 6 else QC) + g * P
                if 4 <= f:
                    if f - 4 < 6:
                        pe.wait_ge(S["v_kk"], f - 3)
                    else:
                        pe.wait_ge(S["v_q2"], f - 9)
                cols = slice(half * HALF, (half + 1) * HALF)
                for i, (w, x) in enumerate(zip(wparts(c0, c0 + P), xparts(cols))):
                    if f < 2:
                        tokens_ready(0, half, i)
                    last = mm(PS[:, 3 + f % 4, 0:HALF], w, x, start=(i == 0), stop=(i == 4))
                last.then_inc(S["p_k" if f < 6 else "p_q"], 1)

            def values(i):
                if i >= 4:
                    pe.wait_ge(S["v_vm"], i - 3)
                for b in (0, 1):
                    xr = [x[:, (2 * i + b) * BLOCK:(2 * i + b + 1) * BLOCK] for x in (RAh, RAh, RB, RAl, RC_)]
                    for k, (w, x) in enumerate(zip(wparts(VC, VC + D), xr)):
                        last = mm(PS[0:BLOCK, (7, 0, 1, 2)[i % 4], b * D:(b + 1) * D], x, w,
                                  start=(k == 0 and b == 0), stop=(k == 4), skip_group_check=True)
                last.then_inc(S["p_v"], 1)

            def scores(u):
                if u >= 1:
                    pe.wait_ge(S["v_sub"], u)
                for r in range(LANES):
                    mm(PS[0:QROWS, 3 + r, 0:SCOLS], mk[:, :], jrep[:, :, :].rearrange("p h k -> p (h k)"),
                       start=True, stop=False, skip_group_check=True)
                for pair in range(2):
                    for bi in (0, 1):
                        b = 2 * (2 * u + pair) + bi
                        tok = slice(b * POSITIONS, (b + 1) * POSITIONS)
                        for g in range(GROUPS):
                            for Q in (Q1, Q2):
                                for r in range(LANES):
                                    rows = slice(32 * r, 32 * r + 32)
                                    col = pair * BLOCK + g * POSITIONS
                                    last = mm(PS[64 * bi:64 * bi + POSITIONS, 3 + r, col:col + POSITIONS],
                                              Q[rows, g, tok], KK[rows, g, tok], start=False, stop=(Q is Q2),
                                              skip_group_check=True)
                last.then_inc(S["p_s"], 1)

            def pt(p):
                u, pair = divmod(p, 2)
                pe.wait_ge(S["a_exp"], u + 1)
                if p >= 2:
                    pe.wait_ge(S["v_ptl"], p - 1)
                for r in range(LANES):
                    last = nc.tensor.transpose(PS[0:BLOCK, (7, 0)[p % 2], r * QROWS:(r + 1) * QROWS],
                                               prob[:, u % 2, r, pair * BLOCK:(pair + 1) * BLOCK],
                                               ident[0:QROWS, 0:QROWS])
                last.then_inc(S["p_pt"], 1)

            def av(p):
                pe.wait_ge(S["a_pth"], p + 1)
                pe.wait_ge(S["v_ptl"], p + 1)
                pe.wait_ge(S["g_vl"], p + 1)
                if p in (2, 4):
                    pe.wait_ge(S["v_cn"], p)
                if p == 6:
                    pe.wait_ge(S["v_sub"], 4)
                for bi in (0, 1):
                    q0, q1 = (0, 64) if bi == 0 else (64, QROWS)
                    for r in range(LANES):
                        c0 = (p % 2) * LANES * VW + r * VW
                        for k, (a, v) in enumerate(((PTh, vh), (PTl, vh), (PTh, vl))):
                            last = mm(PS[q0:q1, 1 if p < 6 else 6, c0:c0 + VW], a[:, p, r, q0:q1], v[:, 2 * p + bi, r, :],
                                      start=(p % 2 == 0 and r == 0 and k == 0), stop=(k == 2),
                                      skip_group_check=True)
                last.then_inc(S["p_av"], 1)

            def ct(p):
                pe.wait_ge(S["v_cn"], p + 1)
                pe.wait_ge(S["g_dup"], p + 1)
                if p in (2, 4):
                    pe.wait_ge(S["v_clo"], p)
                if p == 6:
                    pe.wait_ge(S["v_ptl"], PAIRS)
                b = 2 if p < 6 else 7
                c0 = (p % 2) * 2 * QROWS
                nc.tensor.transpose(PS[:, b, c0:c0 + QROWS], cn[:, p, 0:P], ident[0:QROWS, 0:QROWS])
                nc.tensor.transpose(PS[:, b, c0 + QROWS:c0 + 2 * QROWS], cn[:, p, P:2 * P],
                                    ident[0:QROWS, 0:QROWS]).then_inc(S["p_ct"], 1)

            def wo(t):
                need = min(2 * (t + 1), PAIRS)
                pe.wait_ge(S["v_clo"], need)
                tok = slice(t * P, (t + 1) * P)
                for k, (x, w) in enumerate(zip(cparts(tok), wparts(OC, OC + D))):
                    last = mm(PS[:, (3, 3, 4, 4, 5)[t], D * (t % 2):D * (t % 2) + D], x, w,
                              start=(k == 0 and t % 2 == 0), stop=(k == 4), skip_group_check=True)
                last.then_inc(S["p_wo"], 1)

            pe.wait_ge(S["v_xr"], 4)
            for i in range(4):
                values(i)
            pe.wait_ge(S["v_mk"], 1)
            pe.wait_ge(S["v_jr"], 2)
            pe.wait_ge(S["v_kk"], 6)
            pe.wait_ge(S["v_q2"], 6)
            scores(0)
            for i in range(4, 7):
                values(i)
            for u in range(4):
                if u < 3:
                    scores(u + 1)
                if u == 0:
                    pe.wait_ge(S["v_vm"], 6)
                pt(2 * u)
                pt(2 * u + 1)
                if u == 0:
                    values(7)
                if u == 1:
                    pe.wait_ge(S["v_vm"], PAIRS)
                if u >= 1:
                    av(2 * u - 2)
                    av(2 * u - 1)
                if u >= 2:
                    ct(2 * u - 4)
                    ct(2 * u - 3)
            av(6)
            av(7)
            ct(4)
            ct(5)
            wo(0)
            wo(1)
            ct(6)
            ct(7)
            wo(2)
            wo(3)
            wo(4)

            transposes(TILES, 0, 1, 2)

            def router():
                pe.wait_ge(S["a_hi"], 8)
                pe.wait_ge(S["v_lo"], 8)
                for t in range(TILES):
                    tok = slice(t * P, (t + 1) * P)
                    for k, (x, w) in enumerate(zip(xparts(tok), wparts(RC, RC + 9))):
                        last = mm(PS[:, 7, 9 * t:9 * t + 9], x, w, start=(t == 0 and k == 0), stop=(k == 4),
                                  skip_group_check=True)
                last.then_inc(S["p_r"], 1)

            def gu(i):
                f, half = divmod(i, 2)
                if i % (2 * PT_) == 0:
                    pe.wait_ge(S["a_fw"], 6 * (f // PT_) + 6)
                    pe.wait_ge(S["v_fw"], 6 * (f // PT_) + 6)
                if i >= 2:
                    pe.wait_ge(S["v_hf"], i - 1)
                cols = slice(half * HALF, (half + 1) * HALF)
                Ah, Al, Bw, _, _ = split(f // PT_)
                fc = slice(f % PT_ * P, (f % PT_ + 1) * P)
                for m in range(2):
                    if i == 0 and m == 1:
                        router()
                    w5 = (Ah[:, m, fc], Al[:, m, fc], Bw[:, m, fc], Ah[:, m, fc], Bw[0:64, m, fc])
                    for k, (w, x) in enumerate(zip(w5, xparts(cols, 64))):
                        if i < 2 and m == 0:
                            tokens_ready(1, i, k)
                        last = mm(PS[:, 3 + 2 * (i % 2) + m, 0:HALF], w, x, start=(k == 0), stop=(k == 4))
                last.then_inc(S["p_gu"], 1)

            def gates(k):
                if k == 0:
                    pe.wait_ge(S["v_gx"], 1)
                else:
                    pe.wait_ge(S["a_gt"], 1)
                for t in (range(4) if k == 0 else (4,)):
                    last = nc.tensor.transpose(PS[0:EXPERTS, 7, t % 4 * P:(t % 4 + 1) * P], Gf[:, t, :], ident)
                last.then_inc(S["p_gt"], 1)

            def down(f):
                pe.wait_ge(S["a_ah"], 2 * f + 2)
                pe.wait_ge(S["g_al"], min(2 * f + 2, 2 * FT - 1))
                if f == FT - 1:
                    pe.wait_ge(S["v_al"], 1)
                if f == 0:
                    pe.wait_ge(S["v_pad"], 2)
                if f == ST:
                    pe.wait_ge(S["v_acc"], TILES)
                Dh, Dl = split(f // PT_)[3:]
                for t in range(TILES):
                    tok = slice(t * P, (t + 1) * P)
                    o = PS[:, t // 2, D * (t % 2):D * (t % 2) + D]
                    for k, (a, w) in enumerate(((ah, Dh), (al, Dh), (ah, Dl))):
                        last = mm(o, a[:, f % ABUF, tok], w[:, f % PT_, :], start=(f in (0, ST) and t % 2 == 0 and k == 0),
                                  stop=(f in (ST - 1, FT - 1) and k == 2), skip_group_check=True)
                    if f == FT - 1 and t in (1, 3):
                        last.then_inc(S["p_end"], 1)
                last.then_inc(S["p_dn"] if f < FT - 1 else S["p_end"], 1)

            for f in range(FT + 2):
                for half in range(2):
                    if f < FT:
                        gu(2 * f + half)
                    if 0 <= 2 * f + half - GATE_STEP < 2:
                        gates(2 * f + half - GATE_STEP)
                if f >= 2:
                    down(f - 2)

        @block.scalar
        def _(act):
            A = nc.scalar.activation
            def squares(i):
                act.wait_ge(d_x[i], 16)
                K = P if i < 3 else RK
                for j in (2 * i, 2 * i + 1):
                    A(xsqv[0:K, j, 0:N], xsv[0:K, j, :], ACT.Square,
                      scale=cntroot[0:K, j:j + 1]).then_inc(S["a_xsq"], 1)

            def pixels(i):
                act.wait_ge(d_x[i], 16)
                K = P if i < 3 else RK
                A(xh[0:K, 2 * i:2 * i + 2, 0:N], xsv[0:K, 2 * i:2 * i + 2, :], ACT.Copy,
                  scale=SPIX).then_inc(S["a_xh"], 1)

            act.wait_ge(S["v_one"], 1)
            A(small[:, 47, 0:1], one[:, :], ACT.Square).then_inc(S["a_first"], 1)
            act.wait_ge(d_cst, 16)
            pixels(0)
            squares(0)
            pixels(1)
            squares(1)
            A(wh[:, :, D:D + 1].rearrange("p c o -> p (c o)"), cnt, ACT.Copy).then_inc(S["a_cs"], 1)
            act.wait_ge(d_w[SHIFTS], 16)
            act.wait_ge(d_gb, 16)
            for j in range(RING):
                A(we[0:RK, INNER + j, :], wring[0:RK, j, :], ACT.Identity,
                  scale=gbs[0:RK, 0, 30 + j:31 + j]).then_inc(S["a_ring"], 1)
            def weights_high(i):
                K = P if i < 3 else RK
                if i < 3:
                    act.wait_ge(S["v_fold"], (SHIFTS - 1) * INNER + 2 * i + 2)
                else:
                    act.wait_ge(S["a_ring"], RING)
                A(wh[0:K, 2 * i:2 * i + 2, 0:D], we[0:K, 2 * i:2 * i + 2, :], ACT.Copy, scale=SPW).then_inc(S["a_wh"], 1)

            weights_high(0)
            pixels(2)
            weights_high(1)
            squares(2)
            weights_high(2)
            pixels(3)
            squares(3)
            weights_high(3)
            act.wait_ge(S["p_bw"], 1)
            A(biasrow[0:1, :], PS[0:1, 2, 0:D], ACT.Copy).then_inc(S["a_bw"], 1)
            act.wait_ge(d_aw, 48)
            A(WAh[:, :], awst[:, 0, :], ACT.Copy, scale=SW).then_inc(S["a_aw"], 1)
            A(WB[:, :], awst[:, 1, :], ACT.Copy, scale=SW).then_inc(S["a_aw"], 1)
            A(WC[:, :], awst[0:CROWS, 2, :], ACT.Copy, scale=SW).then_inc(S["a_aw"], 1)

            def ffn_high(p, q):
                if q == 0:
                    act.wait_ge(d_f[p], 48)
                Ah, _, Bw, Dh, _ = split(p)
                k, m = divmod(q, 2)
                W, st = (Ah, Bw, Dh)[k], stages(p)[k]
                part = slice(3 * m, 3 * m + 3) if k == 2 else slice(m, m + 1)
                A(W[:, part], st[:, part], ACT.Copy, scale=SW).then_inc(S["a_fw"], 1)

            for q in range(3):
                ffn_high(0, q)
            act.wait_ge(S["p_main"], 1)
            A(csum[:, :], PS[:, 5, 200:200 + D], ACT.Copy).then_inc(S["a_cs"], 1)

            def root(k):
                act.wait_ge(S["v_stat"], VAR_READY[k])
                A(small[:, 10 * k + 1, :], small[:, 10 * k, :], ACT.Sqrt).then_inc(S["a_sqrt"], 1)

            def high_parts(n, ba, bb, bc):
                for k, (dst, src, need) in enumerate((
                        (XAh[:, 0:512], PS[:, ba, :], 4), (XB[:, 0:512], PS[:, bb, :], 4),
                        (XAh[:, 512:NPAD], PS[:, bc, 0:P], 5), (XB[:, 512:NPAD], PS[:, bc, P:2 * P], 5))):
                    act.wait_ge(S["p_t"], TILES * n + need)
                    if n == 1 and k == 0:
                        act.wait_ge(S["p_v"], PAIRS)
                    A(dst, src, ACT.Copy, scale=SX).then_inc(S["a_hi"], 1)

            def copies(n):
                for t in range(TILES):
                    act.wait_ge(S["v_hn"], TILES * n + t + 1)
                    A(hn[:, t, D:256], hn[:, t, P:D], ACT.Copy).then_inc(S["a_dup"], 1)

            root(0)
            root(1)
            copies(0)
            high_parts(0, 1, 2, 0)
            ffn_high(0, 3)
            ffn_high(0, 4)
            ffn_high(0, 5)
            for f in range(6):
                g, half = divmod(f, 2)
                act.wait_ge(S["p_k"], f + 1)
                A(kh[:, g, half * HALF:(half + 1) * HALF], PS[:, 3 + f % 4, 0:HALF], ACT.Copy,
                  scale=negm).then_inc(S["a_kh"], 1)
            for f in range(6):
                g, half = divmod(f, 2)
                act.wait_ge(S["p_q"], f + 1)
                A(Q1[:, g, half * HALF:(half + 1) * HALF], PS[:, 3 + (f + 6) % 4, 0:HALF], ACT.Copy,
                  scale=SQ / XW).then_inc(S["a_q1"], 1)

            def exps(u):
                act.wait_ge(S["v_sub"], u + 1)
                if u >= 2:
                    act.wait_ge(S["p_pt"], 2 * u - 2)
                A(prob[:, u % 2], sdif[:, u % 2], ACT.Exp, scale=1.0 / (SK * SQ * 4)).then_inc(S["a_exp"], 1)

            act.wait_ge(S["g_pad"], 1)
            A(vh[:, :, :, GROUPS * HD:VW].rearrange("p b r o -> p (b r) o"),
              bones[0:BLOCK, :].unsqueeze(1).to_broadcast([BLOCK, IMAGES * LANES, GROUPS]),
              ACT.Copy).then_inc(S["a_vh"], 1)
            def values_high(i):
                act.wait_ge(S["v_vm"], i + 1)
                A(vh[:, 2 * i:2 * i + 2, :, 0:GROUPS * HD],
                  vm[:, 2 * i:2 * i + 2, :].rearrange("p b (r c) -> p b r c", r=LANES),
                  ACT.Copy).then_inc(S["a_vh"], 1)

            for i in range(4):
                values_high(i)
            exps(0)
            for i in range(4, 7):
                values_high(i)

            def ctx_high(i):
                act.wait_ge(S["p_ct"], 2 * i + 2)
                for k, C in enumerate((CAh, CB)):
                    for pr in (0, 1):
                        last = A(pair_cols(C, 2 * i + pr, P), pair_queries(2 if i < 3 else 7, pr, k, P), ACT.Copy)
                last.then_inc(S["a_chi"], 2)

            for u in range(4):
                for p in (2 * u, 2 * u + 1):
                    act.wait_ge(S["p_pt"], p + 1)
                    A(PTh[:, p].rearrange("p r q -> p (r q)"), PS[0:BLOCK, (7, 0)[p % 2], 0:LANES * QROWS], ACT.Copy,
                      scale=SP_).then_inc(S["a_pth"], 1)
                if u < 3:
                    exps(u + 1)
                if u == 0:
                    values_high(7)
                if u >= 2:
                    ctx_high(u - 2)
                if u == 3:
                    ffn_high(1, 0)
                    ffn_high(1, 1)
            ctx_high(2)
            ctx_high(3)
            ffn_high(1, 2)
            ffn_high(1, 3)
            root(2)
            copies(1)
            high_parts(1, 0, 1, 2)
            act.wait_ge(S["v_lg"], 1)
            A(small[:, 30, :], lg[:, :, 8], ACT.Exp, scale=-1.0).then_inc(S["a_sig"], 1)
            A(small[:, 31, :], lg[:, :, 8], ACT.Exp).then_inc(S["a_sig"], 1)
            act.wait_ge(S["v_gate"], 1)
            A(g8[:, 1], g8[:, 0], ACT.Exp).then_inc(S["a_e"], 1)

            def silu_step(i):
                act.wait_ge(S["p_gu"], i + 1)
                if i >= 2:
                    act.wait_ge(S["v_hf"], i - 1)
                A(silu[:, i % 2, :], PS[:, 3 + 2 * (i % 2), 0:HALF], ACT.Silu, scale=1.0 / XW).then_inc(S["a_silu"], 1)

            def act_high(i):
                f, half = divmod(i, 2)
                act.wait_ge(S["v_hf"], i + 1)
                if half == 0 and f >= ABUF:
                    act.wait_ge(S["p_dn"], f - ABUF + 1)
                A(ah[:, f % ABUF, half * HALF:(half + 1) * HALF], hf[:, i % 3, :], ACT.Copy).then_inc(S["a_ah"], 1)

            def gate_copy(k):
                act.wait_ge(S["p_gt"], k + 1)
                c0, c1 = ((0, 512), (512, NPAD))[k]
                A(GT[:, c0:c1], PS[0:EXPERTS, 7, 0:c1 - c0], ACT.Copy).then_inc(S["a_gt"], 1)

            for i in range(2 * FT + 1):
                if 0 <= i - 1 - GATE_STEP < 2:
                    gate_copy(i - 1 - GATE_STEP)
                if i < 2 * FT:
                    silu_step(i)
                if i >= 1:
                    act_high(i - 1)
                if i in (2, 3):
                    ffn_high(1, 2 + i)
                if i in range(8, 20, 2):
                    ffn_high(2, (i - 8) // 2)

        @block.gpsimd
        def _(pool):
            G = nc.gpsimd
            for i in (1, 2, 3):
                K = P if i < 3 else RK
                pool.wait_ge(S["a_xsq"], 2 * i + 2)
                if i > 1:
                    pool.wait_ge(S["g_sum"], i - 1)
                G.tensor_tensor(xsqv[0:K, 0:2, 0:N], xsqv[0:K, 0:2, 0:N], xsqv[0:K, 2 * i:2 * i + 2, 0:N],
                                ALU.add).then_inc(S["g_sum"], 1)
            pool.wait_ge(S["g_sum"], 3)
            G.tensor_tensor(xsqv[:, 0, 0:N], xsqv[:, 0, 0:N], xsqv[:, 1, 0:N], ALU.add).then_inc(S["g_sum"], 1)
            G.memset(vl[:, :, :, :].rearrange("p b r c -> p (b r c)"), 0.0).then_inc(S["g_pad"], 1)
            pool.wait_ge(S["g_pad"], 1)
            for i in range(PAIRS):
                pool.wait_ge(S["a_vh"], i + 2)
                G.tensor_tensor(vl[:, 2 * i:2 * i + 2, :, 0:GROUPS * HD],
                                vm[:, 2 * i:2 * i + 2, :].rearrange("p b (r c) -> p b r c", r=LANES),
                                vh[:, 2 * i:2 * i + 2, :, 0:GROUPS * HD], ALU.subtract).then_inc(S["g_vl"], 1)
            for p in range(PAIRS):
                pool.wait_ge(S["v_cn"], p + 1)
                G.tensor_copy(cn[:, p, D:256], cn[:, p, P:D]).then_inc(S["g_dup"], 1)

            def gated(i):
                f, half = divmod(i, 2)
                n = i - 2 * ST
                pool.wait_ge(d_g[f_expert(f)[0]], 16)
                pool.wait_ge(S["a_silu"], i + 1)
                if n >= 2:
                    pool.wait_ge(S["v_hf"], i - 1)
                cols = slice(half * HALF, (half + 1) * HALF)
                G.tensor_tensor(sgate[:, i % 2, :], silu[:, i % 2, :], Gb[:, f_expert(f)[0], cols],
                                ALU.mult).then_inc(S["g_sg"], 1)

            def act_low(i):
                f, half = divmod(i, 2)
                cols = slice(half * HALF, (half + 1) * HALF)
                pool.wait_ge(S["a_ah"], i + 1)
                if half == 0 and f >= ABUF:
                    pool.wait_ge(S["p_dn"], f - ABUF + 1)
                G.tensor_tensor(al[:, f % ABUF, cols], hf[:, i % 3, :], ah[:, f % ABUF, cols],
                                ALU.subtract).then_inc(S["g_al"], 1)

            for i in range(2 * FT):
                if 2 * ST <= i < 2 * FT and not two_experts(i // 2):
                    gated(i)
                if i >= 1:
                    act_low(i - 1)

        @block.vector
        def _(dve):
            V = nc.vector
            V.memset(one[:, :], 1.0).then_inc(S["v_one"], 1)
            V.memset(xh[:, :, N:NPAD], 0.0)
            V.memset(xl[:, :, N:NPAD], 0.0)
            V.memset(ones16[:, :], 1.0)
            V.memset(XC[64:CROWS, :], SX)
            V.memset(mk[:, :], 0.0)
            V.memset(jrep[:, :, :], 0.0)
            V.memset(mkf[:, :], 0.0).then_inc(S["v_jm"], 1)
            V.memset(xsqv[:, 0:2, N:NPAD], 0.0).then_inc(S["v_pad"], 1)
            dve.wait_ge(d_cst, 16)
            V.tensor_copy(ident16[:, :], ident).then_inc(S["v_cst"], 1)
            def pixels_low(i):
                K = P if i < 3 else RK
                dve.wait_ge(S["a_xh"], i + 1)
                V.scalar_tensor_tensor(out=xl[0:K, 2 * i:2 * i + 2, 0:N], in0=xsv[0:K, 2 * i:2 * i + 2, :], scalar=SPIX,
                                       in1=xh[0:K, 2 * i:2 * i + 2, 0:N], op0=ALU.mult,
                                       op1=ALU.subtract).then_inc(S["v_xl"], 1)

            dve.wait_ge(d_gb, 16)
            def weights_low(i):
                K = P if i < 3 else RK
                dve.wait_ge(S["a_wh"], i + 1)
                V.scalar_tensor_tensor(out=wl[0:K, 2 * i:2 * i + 2, :], in0=we[0:K, 2 * i:2 * i + 2, :], scalar=SPW,
                                       in1=wh[0:K, 2 * i:2 * i + 2, 0:D], op0=ALU.mult,
                                       op1=ALU.subtract).then_inc(S["v_wl"], 1)

            for s in range(SHIFTS):
                dve.wait_ge(d_w[s], 16)
                for j in range(INNER):
                    gamma = gbs[:, 0, s * INNER + j:s * INNER + j + 1]
                    if s == 0:
                        V.tensor_scalar(we[:, j, :], slabv[:, s, j, :], gamma, None, ALU.mult).then_inc(S["v_fold"], 1)
                    else:
                        dve.wait_ge(S["v_fold"], (s - 1) * INNER + j + 1)
                        V.scalar_tensor_tensor(out=we[:, j, :], in0=slabv[:, s, j, :], scalar=gamma, in1=we[:, j, :],
                                               op0=ALU.mult, op1=ALU.add).then_inc(S["v_fold"], 1)
                    if s == SHIFTS - 1 and j in (3, 5):
                        weights_low(j // 2 - 1)
                if s in (0, 1):
                    pixels_low(s)
            pixels_low(2)
            weights_low(2)
            pixels_low(3)
            weights_low(3)
            dve.wait_ge(S["v_wl"], 4)
            for C in (CAh, CAl, CB):
                V.memset(C[:, N:NPAD], 0.0)
            V.memset(CC[0:64, N:NPAD], 0.0)
            V.memset(CC[64:CROWS, :], SCTX)
            dve.wait_ge(d_tab, 64)
            dve.wait_ge(S["v_jm"], 1)
            two = (slice(0, POSITIONS), slice(64, QROWS))
            for r in two:
                V.tensor_reduce(mksum[r, :], tabs[r, :, :], AX.X, ALU.add).then_inc(S["v_jm"], 1)
                V.tensor_scalar(jrep[r, :, :], jrev[r, :].unsqueeze(1).to_broadcast([POSITIONS, 6, POSITIONS]),
                                16.0, None, ALU.mult).then_inc(S["v_jr"], 1)
            dve.wait_ge(S["v_jm"], 3)
            for r in two:
                for c0 in (0, 64):
                    V.tensor_scalar(mkf[r, c0:c0 + POSITIONS], mksum[r, :], 16.0 / HEADS, None,
                                    ALU.mult).then_inc(S["v_jm"], 1)
            dve.wait_ge(S["v_jm"], 7)
            for r in two:
                V.tensor_copy(mk[r, :], mkf[r, :]).then_inc(S["v_jm"], 1)
            dve.wait_ge(S["v_jm"], 9)
            V.tensor_tensor(mk[two[1], :], mkf[two[1], :], mk[two[1], :], ALU.subtract).then_inc(S["v_mk"], 1)
            def attention_low(k):
                W, rows, a = ((WAl, slice(0, P), 0), (WB, slice(64, P), 1), (WC, slice(96, 97), 2))[k]
                dve.wait_ge(S["a_aw"], k + 1)
                hi = WAh if k == 0 else W
                V.scalar_tensor_tensor(out=W[rows, :], in0=awst[rows, a, :], scalar=SW, in1=hi[rows, :],
                                       op0=ALU.mult, op1=ALU.subtract).then_inc(S["v_awl"], 1)

            attention_low(0)
            attention_low(1)

            def ffn_low(p, q):
                Ah, Al, Bw, Dh, Dl = split(p)
                k, m = divmod(q, 2)
                W, hi, st, r0 = (Al, Bw, Dl)[k], (Ah, Bw, Dh)[k], stages(p)[k], (0, 64, 0)[k]
                part = slice(3 * m, 3 * m + 3) if k == 2 else slice(m, m + 1)
                dve.wait_ge(S["a_fw"], 6 * p + q + 1)
                V.scalar_tensor_tensor(out=W[r0:P, part], in0=st[r0:P, part], scalar=SW, in1=hi[r0:P, part],
                                       op0=ALU.mult, op1=ALU.subtract).then_inc(S["v_fw"], 1)

            stat = [0]

            def step(instruction):
                instruction.then_inc(S["v_stat"], 1)
                stat[0] += 1
                dve.wait_ge(S["v_stat"], stat[0])

            def rsqrt(k, scale=1.0):
                v, sd, r, a, b, rs, o = (small[:, 10 * k + i, :] for i in (0, 1, 2, 3, 4, 5, 9))
                assert stat[0] == VAR_READY[k]
                dve.wait_ge(S["a_sqrt"], k + 1)
                step(V.reciprocal(r, sd))
                V.tensor_scalar(rs, r, scale, None, ALU.mult)
                step(V.tensor_tensor(a, r, r, ALU.mult))
                step(V.scalar_tensor_tensor(out=b, in0=a, scalar=-0.5, in1=v, op0=ALU.mult, op1=ALU.mult))
                step(V.scalar_tensor_tensor(out=o, in0=b, scalar=1.5, in1=rs, op0=ALU.add, op1=ALU.mult))

            nmean, nsq = small[:, 6, :], small[:, 7, :]

            def centred(t):
                V.scalar_tensor_tensor(out=t1[:, t, :], in0=csum[:, :], scalar=small[:, 6, t:t + 1],
                                       in1=PS[:, 3 + t // 2, 200 * (t % 2):200 * (t % 2) + D], op0=ALU.mult,
                                       op1=ALU.add).then_inc(S["v_h"], 1)

            dve.wait_ge(S["p_st"], 1)
            V.tensor_scalar(small[:, 8, :], PS[:, 1, 0:TILES], 1.0 / PATCH_DIM, None, ALU.mult)
            dve.wait_ge(S["p_main"], 1)
            V.tensor_scalar(small[:, 6, 0:4].rearrange("p (a b) -> p a b", a=2),
                            PS[:, 3:5, 0:400].rearrange("p a (b c) -> p a b c", b=2)[:, :, :, D], -1.0 / PATCH_DIM,
                            None, ALU.mult)
            dve.wait_ge(S["a_cs"], 2)
            step(V.tensor_scalar(small[:, 6, 4:5], PS[:, 5, D:D + 1], -1.0 / PATCH_DIM, None, ALU.mult))
            step(V.tensor_tensor(nsq, nmean, nmean, ALU.mult))
            step(V.scalar_tensor_tensor(out=small[:, 3, :], in0=nsq, scalar=-1.0 / SPIX ** 2, in1=small[:, 8, :],
                                        op0=ALU.mult, op1=ALU.add))
            step(V.tensor_scalar(small[:, 0, :], small[:, 3, :], 0.0, EPS, ALU.max, ALU.add))
            for t in range(TILES):
                centred(t)
            rsqrt(0, 1.0 / (SPIX * SPW))

            def residual(n, op, tiles):
                src = (h1, h2)[n]
                for t in tiles:
                    op(t).then_inc(S["v_h"], 1)
                for t in tiles:
                    dve.wait_ge(S["v_h"], TILES * (n + 1) + t + 1)
                    V.bn_stats(bst[:, t, :], src[:, t, :]).then_inc(S["v_bn"], 1)

            def normed(n):
                src, k = (h1, h2)[n], n + 1
                for t in range(TILES):
                    dve.wait_ge(S["v_bn"], 2 * TILES * n + t + 1)
                    V.bn_aggr(mv[:, t, :], bst[:, t, :]).then_inc(S["v_bn"], 1)
                dve.wait_ge(S["v_bn"], 2 * TILES * (n + 1))
                step(V.tensor_scalar(small[:, 10 * k, :], mv[:, :, 1], EPS, None, ALU.add))
                rsqrt(k)
                if n == 1:
                    dve.wait_ge(S["p_t"], TILES)
                for t in range(TILES):
                    V.tensor_scalar(hn[:, t, 0:D], src[:, t, :], mv[:, t, 0:1], small[:, 10 * k + 9, t:t + 1],
                                    ALU.subtract, ALU.mult).then_inc(S["v_hn"], 1)

            def low_parts(n, ba, bb, bc):
                for k, (dst, src, hi) in enumerate((
                        (XAl[:, 0:512], PS[:, ba, :], XAh[:, 0:512]), (XC[0:64, 0:512], PS[0:64, bb, :], XB[0:64, 0:512]),
                        (XAl[:, 512:NPAD], PS[:, bc, 0:P], XAh[:, 512:NPAD]),
                        (XC[0:64, 512:NPAD], PS[0:64, bc, P:2 * P], XB[0:64, 512:NPAD]))):
                    dve.wait_ge(S["a_hi"], 4 * n + (k + 1 if k < 2 else 4))
                    V.scalar_tensor_tensor(out=dst, in0=src, scalar=SX, in1=hi, op0=ALU.mult,
                                           op1=ALU.subtract).then_inc(S["v_lo"], 1)

            dve.wait_ge(S["v_h"], TILES)
            dve.wait_ge(S["p_bias"], TILES)
            residual(0, lambda t: V.scalar_tensor_tensor(
                out=h1[:, t, :], in0=t1[:, t, :], scalar=small[:, 9, t:t + 1],
                in1=PS[:, (6, 6, 7, 7, 0)[t], D * (t % 2):D * (t % 2) + D], op0=ALU.mult, op1=ALU.add), range(TILES))
            normed(0)
            attention_low(2)
            low_parts(0, 1, 2, 0)
            copies_made = [0]

            def thrice():
                R, X = ((RAh, XAh), (RAl, XAl), (RB, XB), (RC_, XC))[copies_made[0]]
                if X is XAh:
                    dve.wait_ge(S["v_lo"], 4)
                copies_made[0] += 1
                V.tensor_copy(R[:, :].rearrange("p (b g q) -> p b g q", b=IMAGES, g=GROUPS),
                              X[:, 0:N].rearrange("p (b q) -> p b q", b=IMAGES).unsqueeze(2).to_broadcast(
                                  [X.shape[0], IMAGES, GROUPS, POSITIONS])).then_inc(S["v_xr"], 1)

            for f in range(6):
                g, half = divmod(f, 2)
                cols = slice(half * HALF, (half + 1) * HALF)
                dve.wait_ge(S["a_kh"], f + 1)
                V.scalar_tensor_tensor(out=KK[:, g, cols], in0=PS[:, 3 + f % 4, 0:HALF], scalar=SK / XW,
                                       in1=kh[:, g, cols], op0=ALU.mult, op1=ALU.add).then_inc(S["v_kk"], 1)
                if f in (1, 3, 5):
                    thrice()
            for f in range(6):
                g, half = divmod(f, 2)
                cols = slice(half * HALF, (half + 1) * HALF)
                dve.wait_ge(S["a_q1"], f + 1)
                V.scalar_tensor_tensor(out=Q2[:, g, cols], in0=PS[:, 3 + (f + 6) % 4, 0:HALF], scalar=SQ / XW,
                                       in1=Q1[:, g, cols], op0=ALU.mult, op1=ALU.subtract).then_inc(S["v_q2"], 1)
                if f == 1:
                    thrice()
            def differences(u):
                dve.wait_ge(S["p_s"], u + 1)
                s = PS[0:QROWS, 3:7, 0:SCOLS].rearrange("p r (h k) -> p r h k", k=POSITIONS)
                V.tensor_reduce(mx[:, u % 2], s, AX.X, ALU.max).then_inc(S["v_max"], 1)
                dve.wait_ge(S["v_max"], u + 1)
                if u >= 2:
                    dve.wait_ge(S["a_exp"], u - 1)
                V.tensor_tensor(sdif[:, u % 2].rearrange("p r (h k) -> p r h k", k=POSITIONS), s,
                                mx[:, u % 2].unsqueeze(3).to_broadcast([QROWS, LANES, 6, POSITIONS]),
                                ALU.subtract).then_inc(S["v_sub"], 1)

            def own_values(i):
                dve.wait_ge(S["p_v"], i + 1)
                V.scalar_tensor_tensor(
                    out=vm[:, 2 * i:2 * i + 2, :],
                    in0=PS[0:BLOCK, (7, 0, 1, 2)[i % 4], 0:2 * D].rearrange("p (b d) -> p b d", b=2), scalar=SV / XW,
                    in1=bmask[0:BLOCK, :].unsqueeze(1).to_broadcast([BLOCK, 2, D]), op0=ALU.mult,
                    op1=ALU.mult).then_inc(S["v_vm"], 1)

            def pt_low(p):
                dve.wait_ge(S["a_pth"], p + 1)
                V.scalar_tensor_tensor(out=PTl[:, p].rearrange("p r q -> p (r q)"),
                                       in0=PS[0:BLOCK, (7, 0)[p % 2], 0:LANES * QROWS], scalar=SP_,
                                       in1=PTh[:, p].rearrange("p r q -> p (r q)"), op0=ALU.mult,
                                       op1=ALU.subtract).then_inc(S["v_ptl"], 1)

            def normalise(p):
                dve.wait_ge(S["p_av"], p // 2 * 2 + 2)
                c0 = (p % 2) * LANES * VW
                o = PS[0:QROWS, 1 if p < 6 else 6, c0:c0 + LANES * VW].rearrange("p (r c) -> p r c", r=LANES)
                V.reciprocal(rden[:, p], o[:, :, GROUPS * HD:VW]).then_inc(S["v_rd"], 1)
                dve.wait_ge(S["v_rd"], p + 1)
                V.tensor_tensor(cn[:, p, 0:D].rearrange("p (r g d) -> p r g d", r=LANES, g=GROUPS),
                                o[:, :, 0:GROUPS * HD].rearrange("p r (g d) -> p r g d", g=GROUPS),
                                rden[:, p].unsqueeze(3).to_broadcast([QROWS, LANES, GROUPS, HD]),
                                ALU.mult).then_inc(S["v_cn"], 1)

            def ctx_low(i):
                dve.wait_ge(S["a_chi"], 2 * i + 2)
                for k, (C, hi, rows) in enumerate(((CAl, CAh, P), (CC, CB, 64))):
                    for pr in (0, 1):
                        p = 2 * i + pr
                        last = V.tensor_tensor(pair_cols(C, p, rows), pair_queries(2 if i < 3 else 7, pr, k, rows),
                                               pair_cols(hi, p, rows), ALU.subtract)
                last.then_inc(S["v_clo"], 2)

            for i in range(4):
                own_values(i)
            differences(0)
            for i in range(4, 7):
                own_values(i)
            for u in range(4):
                if u < 3:
                    differences(u + 1)
                pt_low(2 * u)
                pt_low(2 * u + 1)
                if u == 0:
                    own_values(7)
                if u >= 1:
                    normalise(2 * u - 2)
                    normalise(2 * u - 1)
                if u >= 2:
                    ctx_low(u - 2)
                for q in ((0, 1, 2), (3, 4, 5), (), ())[u]:
                    ffn_low(0, q)
            def add_attention(t):
                dve.wait_ge(S["p_wo"], (2, 2, 4, 4, 5)[t])
                return V.scalar_tensor_tensor(
                    out=h2[:, t, :], in0=PS[:, (3, 3, 4, 4, 5)[t], D * (t % 2):D * (t % 2) + D],
                    scalar=1.0 / (SCTX * SW), in1=h1[:, t, :], op0=ALU.mult, op1=ALU.add)

            normalise(6)
            normalise(7)
            ctx_low(2)
            residual(1, add_attention, (0, 1))
            ctx_low(3)

            V.memset(ah[:, :, N:NPAD], 0.0)
            V.memset(al[:, :, N:NPAD], 0.0).then_inc(S["v_pad"], 1)
            residual(1, add_attention, (2, 3))
            residual(1, add_attention, (4,))
            normed(1)
            low_parts(1, 0, 1, 2)

            gate = [0]

            def gstep(instruction):
                instruction.then_inc(S["v_gate"], 1)
                gate[0] += 1
                dve.wait_ge(S["v_gate"], gate[0])

            def over8(v):
                return v.unsqueeze(2).to_broadcast([P, TILES, 8])

            m1, s1, m2, s2, den, rd_ = (small[:, i, :] for i in (32, 33, 34, 35, 36, 37))
            l8 = lg[:, :, 0:8]
            rank = cst_rank[:, :].unsqueeze(1).to_broadcast([P, TILES, 8])

            dve.wait_ge(S["p_r"], 1)
            V.tensor_scalar(lg[:, :, :], PS[:, 7, 0:9 * TILES].rearrange("p (t e) -> p t e", t=TILES), 1.0 / XW, None,
                            ALU.mult).then_inc(S["v_lg"], 1)
            dve.wait_ge(S["v_lg"], 1)
            V.tensor_reduce(m1, l8, AX.X, ALU.max).then_inc(S["v_bn"], 1)
            dve.wait_ge(S["v_bn"], 4 * TILES + 1)
            gstep(V.tensor_tensor(g8[:, 0], l8, over8(m1), ALU.subtract))

            def choose_first():
                gstep(V.tensor_tensor(g8[:, 2], l8, over8(m1), ALU.is_equal))
                gstep(V.tensor_tensor(g8[:, 3], g8[:, 2], rank, ALU.mult))
                gstep(V.tensor_reduce(s1, g8[:, 3], AX.X, ALU.max))
                gstep(V.tensor_tensor(g8[:, 4], rank, over8(s1), ALU.is_equal))

            def second_largest():
                gstep(V.scalar_tensor_tensor(out=g8[:, 5], in0=g8[:, 4], scalar=-3e38, in1=l8, op0=ALU.mult,
                                             op1=ALU.add))
                gstep(V.tensor_reduce(m2, g8[:, 5], AX.X, ALU.max))
                gstep(V.tensor_tensor(g8[:, 6], g8[:, 5], over8(m2), ALU.is_equal))

            def choose_second():
                gstep(V.tensor_tensor(g8[:, 7], g8[:, 6], rank, ALU.mult))
                gstep(V.tensor_reduce(s2, g8[:, 7], AX.X, ALU.max))
                gstep(V.tensor_tensor(g8[:, 8], rank, over8(s2), ALU.is_equal))
                gstep(V.tensor_tensor(g8[:, 9], g8[:, 8], g8[:, 4], ALU.add))

            def gate_sum():
                dve.wait_ge(S["a_e"], 1)
                gstep(V.tensor_tensor(g8[:, 10], g8[:, 9], g8[:, 1], ALU.mult))
                gstep(V.tensor_reduce(den, g8[:, 10], AX.X, ALU.add))
                gstep(V.reciprocal(rd_, den))

            def gate_split():
                dve.wait_ge(S["a_sig"], 2)
                gstep(V.tensor_scalar(small[:, 40:42, :], small[:, 30:32, :], 1.0, None, ALU.add))
                gstep(V.reciprocal(small[:, 42:44, :], small[:, 40:42, :]))
                gstep(V.tensor_scalar(small[:, 38, :], small[:, 42, :], 1.0 / (SH * SW), None, ALU.mult))
                gstep(V.scalar_tensor_tensor(out=small[:, 39, :], in0=rd_, scalar=1.0, in1=small[:, 43, :],
                                             op0=ALU.mult, op1=ALU.mult))
                V.tensor_tensor(Gf[:, :, :], g8[:, 10], over8(small[:, 39, :]), ALU.mult).then_inc(S["v_gx"], 1)

            def product(i):
                dve.wait_ge(S["a_silu"], i + 1)
                src = silu
                f, half = divmod(i, 2)
                if two_experts(f):
                    dve.wait_ge(d_g[f_expert(f)[0]], 16)
                    dve.wait_ge(d_g[f_expert(f)[1]], 16)
                    cols = slice(half * HALF, (half + 1) * HALF)
                    for a, e in zip((0, 64), f_expert(f)):
                        last = V.tensor_tensor(sgate[a:a + 64, i % 2, :], silu[a:a + 64, i % 2, :],
                                               Gb[a:a + 64, e, cols], ALU.mult)
                    last.then_inc(S["v_sg"], 1)
                    dve.wait_ge(S["v_sg"], 2 * ((f - ST) // 3) + half + 1)
                elif f >= ST:
                    dve.wait_ge(S["g_sg"], 4 * ((f - ST) // 3) + 2 * ((f - ST) % 3) + half + 1)
                if f >= ST:
                    src = sgate
                if i >= 3:
                    dve.wait_ge(S["g_al"], i - 2)
                V.scalar_tensor_tensor(out=hf[:, i % 3, :], in0=PS[:, 4 + 2 * (i % 2), 0:HALF], scalar=SH / XW,
                                       in1=src[:, i % 2, :], op0=ALU.mult, op1=ALU.mult).then_inc(S["v_hf"], 1)

            for i in range(2 * FT):
                product(i)
                if i == 0:
                    choose_first()
                if i == 1:
                    second_largest()
                if i == 2:
                    choose_second()
                if i == 3:
                    gate_sum()
                if i == 4:
                    gate_split()
                if 5 <= i < 11:
                    ffn_low(1, i - 5)
                if i in (11, 12, 13, 14, 18, 19):
                    ffn_low(2, (11, 12, 13, 14, 18, 19).index(i))
                if i == 2 * ST + 3:
                    dve.wait_ge(S["p_dn"], ST)
                    for t in range(TILES):
                        V.scalar_tensor_tensor(out=acc[:, t, :], in0=PS[:, t // 2, D * (t % 2):D * (t % 2) + D],
                                               scalar=small[:, 38, t:t + 1], in1=h2[:, t, :], op0=ALU.mult,
                                               op1=ALU.add).then_inc(S["v_acc"], 1)
            dve.wait_ge(S["a_ah"], 2 * FT)
            V.tensor_tensor(al[:, (FT - 1) % ABUF, HALF:N], hf[:, (2 * FT - 1) % 3, :],
                            ah[:, (FT - 1) % ABUF, HALF:N], ALU.subtract).then_inc(S["v_al"], 1)
            for t in range(TILES):
                dve.wait_ge(S["p_end"], t // 2 + 1)
                V.scalar_tensor_tensor(out=fin[:, t, 0:D], in0=PS[:, t // 2, D * (t % 2):D * (t % 2) + D],
                                       scalar=1.0 / (SH * SW), in1=acc[:, t, :], op0=ALU.mult,
                                       op1=ALU.add).then_inc(S["v_fin"], 1)


def _fold_layout(v):
    import numpy as np
    w = v.reshape(16, 16, 5, 3, -1)
    inner = np.zeros((SHIFTS, 3, 16, 16, w.shape[-1]), v.dtype)
    m = np.moveaxis(w, (2, 3), (0, 1))
    inner[0] = m[0]
    inner[1, :, :, :-1] = m[1, :, :, 1:]
    inner[2, :, :, 1:] = m[2, :, :, :-1]
    inner[3, :, :-1] = m[3, :, 1:]
    inner[4, :, 1:] = m[4, :, :-1]
    ring = np.stack([m[3, :, 0], m[4, :, 15], m[1, :, :, 0], m[2, :, :, 15]], 1)
    return inner.reshape(SHIFTS, 768, -1), ring.reshape(192, -1)


def _chunks(a, n):
    return a.reshape(n, -1, a.shape[-1]).swapaxes(0, 1)


def _pad_rows(a, rows=P):
    import numpy as np
    out = np.zeros((rows,) + a.shape[1:], a.dtype)
    out[:a.shape[0]] = a
    return out


def _layouts(x, cls_tok, L0_tok_ln_gamma, L0_tok_ln_beta, L0_tok_W, L0_tok_b, L0_attn_w_q, L0_attn_b_q, L0_attn_w_k,
             L0_attn_b_k, L0_attn_w_v, L0_attn_b_v, L0_attn_w_o, L0_attn_b_o, L0_attn_bias_table, L0_ffn_router_w,
             L0_ffn_w_gate, L0_ffn_w_up, L0_ffn_w_down, L0_ffn_ws_gate, L0_ffn_ws_up, L0_ffn_ws_down, L0_ffn_sg_w,
             L0_ffn_sg_b):
    import numpy as np
    f32 = np.float32
    xp = np.zeros((16, 3, 98, 98), x.dtype)
    xp[:, :, 1:97, 1:97] = x
    inner = np.zeros((3, 16, 16, 16, 37), x.dtype)
    ring = np.zeros((3, 4, 16, 16, 37), x.dtype)
    for py in range(6):
        for px in range(6):
            w = xp[:, :, 16 * py:16 * py + 18, 16 * px:16 * px + 18]
            t = 1 + 6 * py + px
            inner[..., t] = w[:, :, 1:17, 1:17].transpose(1, 2, 3, 0)
            for k, side in enumerate((w[:, :, 0, 1:17], w[:, :, 17, 1:17], w[:, :, 1:17, 0], w[:, :, 1:17, 17])):
                ring[:, k, :, :, t] = side.transpose(1, 2, 0)
    wi, wr = _fold_layout(L0_tok_W)
    gi, gr = _fold_layout(L0_tok_ln_gamma[:, None])
    bi, br = _fold_layout(L0_tok_ln_beta[:, None])
    ci, cr = _fold_layout(np.ones((PATCH_DIM, 1), f32))
    cnt = np.concatenate([_chunks(ci.sum(0), INNER)[..., 0], _pad_rows(_chunks(cr, RING)[..., 0])], 1)
    gb = np.stack([np.concatenate([v.reshape(SHIFTS * INNER, P).T, _pad_rows(_chunks(r, RING)[..., 0])], 1)
                   for v, r in ((gi, gr), (bi, br))], 1)
    rows = np.arange(P)
    own = np.repeat(rows[:, None] // POSITIONS == np.arange(GROUPS)[None, :], HD, 1)
    consts = np.concatenate([
        np.eye(P), cnt, np.where(rows % 32 < HD, 0, -SK / XW)[:, None], np.tile(own, (1, LANES)),
        rows[:, None] // POSITIONS == np.arange(GROUPS)[None, :],
        np.broadcast_to(np.arange(EXPERTS, 0, -1), (P, EXPERTS)), np.sqrt(cnt)], 1).astype(f32)
    qk = (4 * np.arange(GROUPS)[:, None, None, None] + np.arange(LANES)[:, None, None]) * HD + np.arange(HD)
    qk = np.broadcast_to(qk, (GROUPS, LANES, 2, HD)).reshape(-1)
    vo = ((4 * np.arange(GROUPS)[:, None] + np.arange(LANES)[:, None, None]) * HD + np.arange(HD)).reshape(-1)
    aw = np.concatenate([L0_attn_w_q.T[:, qk], L0_attn_w_k.T[:, qk], L0_attn_w_v.T[:, vo], L0_attn_w_o.T[vo],
                         L0_ffn_router_w, L0_ffn_sg_w], 1)
    ab = np.concatenate([L0_attn_b_q[qk], L0_attn_b_k[qk], L0_attn_b_v[vo], L0_attn_b_o,
                         np.zeros(EXPERTS, f32), L0_ffn_sg_b])
    aw_c = np.zeros((CROWS, AW), f32)
    aw_c[0:64], aw_c[64], aw_c[96] = aw[P:], ab, ab
    fo = np.concatenate([np.arange(128), HID + np.arange(128), np.arange(128, 192), HID + np.arange(128, 192)])
    fo = (2 * HID * np.arange(EXPERTS // 2)[:, None] + fo).reshape(-1)
    up = [np.concatenate([s, e.transpose(1, 0, 2).reshape(D, -1)[:, fo]], 1)
          for s, e in ((L0_ffn_ws_gate, L0_ffn_w_gate), (L0_ffn_ws_up, L0_ffn_w_up))]
    up = np.stack(up, 1)
    down = np.concatenate([L0_ffn_ws_down, L0_ffn_w_down.reshape(-1, D)[fo]], 0)
    first = (np.arange(NPAD) % POSITIONS == 0) & (np.arange(NPAD) < N)
    j = np.arange(POSITIONS)
    mid = (L0_attn_bias_table.shape[0] - 1) // 2
    return {
        "x_inner": _chunks(inner.reshape(768, N), INNER), "x_ring": _chunks(ring.reshape(192, N), RING),
        "w_inner": np.stack([_chunks(v, INNER) for v in wi]), "w_ring": _chunks(wr, RING),
        "gb": gb, "consts": consts, "j_rev": (j[:, None] + j == POSITIONS - 1).astype(f32),
        "ind": np.stack([~first & (np.arange(NPAD) < N), first]).astype(f32),
        "tok_b": L0_tok_b[None, :], "cls": cls_tok.reshape(1, D),
        "tab": L0_attn_bias_table[mid - (POSITIONS - 1) + j[:, None] + j],
        "aw_a": aw[0:P], "aw_b": np.concatenate([aw[P:], aw[P:]], 0), "aw_c": aw_c,
        "f_a": up[0:P], "f_b": np.concatenate([up[P:], up[P:]], 0), "f_d": _chunks(down, FT),
    }


def kernel(**inputs):
    import numpy as _np
    import concourse.bacc as _bacc
    from concourse.bass_utils import run_bass_kernel_spmd as _run

    nc = _bacc.Bacc("TRN2", target_bir_lowering=False, num_devices=1)
    arrays, aps = {}, {}
    for name, a in _layouts(**{k: _np.asarray(v) for k, v in inputs.items()}).items():
        a = _np.ascontiguousarray(a)
        arrays[f"in_{name}_dram"] = a
        aps[name] = nc.dram_tensor(f"in_{name}_dram", a.shape, mybir.dt.from_np(a.dtype), kind="ExternalInput").ap()
    out = nc.dram_tensor("out_0_dram", (N, D), F32, kind="ExternalOutput").ap()
    gate_rows = nc.dram_tensor("gate_rows_dram", (EXPERTS, N), F32).ap()
    vit_kernel(nc, gate_rows=gate_rows, out=out, **aps)
    r = _run(nc, [arrays], core_ids=[0])
    return r.results[0]["out_0_dram"].reshape(IMAGES, POSITIONS, D)
```

```python
from contextlib import ExitStack

import concourse.bass as bass
from concourse import mybir

F32 = mybir.dt.float32
F16 = mybir.dt.float16
ALU = mybir.AluOpType
ACT = mybir.ActivationFunctionType
AX = mybir.AxisListType

P = 128
IMAGES, POSITIONS, D = 16, 37, 192
N = IMAGES * POSITIONS
HALF = N // 2
TILES = 5
NPAD = TILES * P
REST = N - 4 * P
PATCH_DIM = 16 * 16 * 15
EPS = 1e-5

INNER, RING, RK = 6, 2, 96
CHUNKS = INNER + RING
SHIFTS = 5

HEADS, HD = 12, 16
GROUPS, LANES = 3, 4
BLOCK = GROUPS * POSITIONS
QROWS = 64 + POSITIONS
PAIRS = IMAGES // 2
VW = GROUPS * HD + GROUPS

QC, KC, VC, OC, RC = 0, 384, 768, 960, 1152
AW = RC + 9
CROWS = 97

EXPERTS, HID, SHARED = 8, 192, 768
FT = (SHARED + EXPERTS * HID) // P
ST = SHARED // P
PIECES = 3
PT_ = FT // PIECES

SX, SW, SPIX, SPW, SK, SQ, SP_, SV, SCTX, SH = 64.0, 64.0, 16.0, 256.0, 16.0, 4.0, 256.0, 16.0, 16.0, 16.0
XW = SX * SW

GATE_STEP = 6
CONSTS = 128 + 2 * CHUNKS + 1 + D + GROUPS + EXPERTS
FRONT = 3 * P
NORMS = ((0, range(0, 5), 5), (10, range(0, 3), 10), (10, range(3, 5), 15), (20, range(0, 5), 20))


def f_expert(f):
    pair, k = divmod(f - ST, 3)
    return (2 * pair, 2 * pair + 1) if k == 1 else (2 * pair + k // 2, 2 * pair + k // 2)


def kq_product(f):
    half, r = divmod(f, 6)
    return r // GROUPS, r % GROUPS, half


def two_experts(f):
    return f >= ST and (f - ST) % 3 == 1


def vit_kernel(nc, x_inner, x_ring, w_inner, w_ring, gb, consts, j_rev, ind, tok_b, cls, tab,
               aw_a, aw_b, aw_c, f_a, f_b, f_d, gate_rows, out):
    with ExitStack() as ctx:
        def sb(name, shape, dt=F32):
            return ctx.enter_context(nc.sbuf_tensor(name, shape, dt))

        def sem(name):
            return ctx.enter_context(nc.semaphore(name))

        PS = ctx.enter_context(nc.psum_tensor("PS", [P, 8, 512], F32))

        xs = sb("xs", [P, CHUNKS * N])
        xsv = xs[:, :].rearrange("p (c n) -> p c n", c=CHUNKS)
        slab = sb("slab", [P, SHIFTS * INNER * D])
        slabv = slab[:, :].rearrange("p (s c d) -> p s c d", s=SHIFTS, c=INNER)
        wring = sb("wring", [P, RING, D])
        xsq = sb("xsq", [P, 9 * N])
        xsqv = xsq[:, 0:CHUNKS * NPAD].rearrange("p (c n) -> p c n", c=CHUNKS)
        gbs = sb("gbs", [P, 2, SHIFTS * INNER + RING])
        cst = sb("cst", [P, CONSTS])
        ident = cst[:, 0:128]
        cnt = cst[:, 128:136]
        kscale = cst[:, 136:137]
        bmask = cst[:, 137:329]
        bones = cst[:, 329:332]
        cst_rank = cst[:, 332:340]
        cntroot = cst[:, 340:348]
        jrev = sb("jrev", [QROWS, POSITIONS])
        inds = sb("inds", [2, NPAD])
        tokb = sb("tokb", [1, D])
        biasrow = sb("biasrow", [2, D])
        tabs = sb("tabs", [QROWS, POSITIONS, HEADS])
        one = sb("one", [P, 1])
        xhl = sb("xhl", [P, CHUNKS * NPAD])
        xhlv = xhl[:, :].bitcast(F16).rearrange("p (k c n) -> p k c n", k=2, c=CHUNKS)
        xh, xl = xhlv[:, 0], xhlv[:, 1]
        wef = sb("we", [P, CHUNKS * D])
        we = wef[:, :].rearrange("p (c d) -> p c d", c=CHUNKS)
        whl = sb("whl", [P, CHUNKS * (2 * D + 1) // 2])
        WHC = CHUNKS * (D + 1) // 2
        wh = whl[:, 0:WHC].bitcast(F16).rearrange("p (c d) -> p c d", c=CHUNKS)
        wl = whl[:, WHC:].bitcast(F16).rearrange("p (c d) -> p c d", c=CHUNKS)
        jrep = sb("jrep", [QROWS, 6, POSITIONS], F16)
        mkf = sb("mkf", [QROWS, QROWS])
        mksum = sb("mksum", [QROWS, POSITIONS])
        mk = sb("mk", [QROWS, QROWS], F16)
        csum = sb("csum", [P, D])
        small = sb("small", [P, 48, TILES])
        t1 = sb("t1", [P, TILES, D])
        h1 = sb("h1", [P, TILES, D])
        h2 = sb("h2", [P, TILES, D])
        hn = sb("hn", [P, TILES, 256])
        bst = sb("bst", [P, TILES, 6])
        mv = sb("mv", [P, TILES, 2])
        XAh, XAl, XB = (sb(n, [P, NPAD], F16) for n in ("XAh", "XAl", "XB"))
        XC = sb("XC", [CROWS, NPAD], F16)
        ctxv = wef[:, 0:2 * NPAD].bitcast(F16).rearrange("p (k n) -> p k n", k=4)
        CAh, CAl, CB, CC = ctxv[:, 0], ctxv[:, 1], ctxv[:, 2], ctxv[0:CROWS, 3]
        awst = sb("awst", [P, 3, AW])
        WAh, WAl, WB = (sb(n, [P, AW], F16) for n in ("WAh", "WAl", "WB"))
        WC = sb("WC", [CROWS, AW], F16)
        KFC = 2 * LANES * 4 * BLOCK
        kh = xsq[:, KFC:KFC + GROUPS * N // 2].bitcast(F16).rearrange("p (g n) -> p g n", g=GROUPS)
        kq = sb("kq", [P, 3 * GROUPS * N // 2 + 192])
        kqv = kq[:, 0:3 * GROUPS * N // 2].bitcast(F16).rearrange("p (k g n) -> p k g n", k=3, g=GROUPS)
        KK, Q1, Q2 = kqv[:, 0], kqv[:, 1], kqv[:, 2]
        vm = xs[0:BLOCK, 0:IMAGES * D].rearrange("p (b d) -> p b d", b=IMAGES)
        vhl = sb("vhl", [P, IMAGES * LANES * VW])
        vhlv = vhl[0:BLOCK, :].bitcast(F16).rearrange("p (k b r c) -> p k b r c", k=2, b=IMAGES, r=LANES)
        vh, vl = vhlv[:, 0], vhlv[:, 1]
        SCOLS = 2 * BLOCK
        dp = xsq[0:QROWS, 0:4 * LANES * SCOLS].rearrange("p (k u r c) -> p k u r c", k=2, u=2, r=LANES)
        sdif, prob = dp[:, 0], dp[:, 1]
        repv = slab[:, 0:KFC].bitcast(F16).rearrange("p (k n) -> p k n", k=4)
        RAh, RAl, RB, RC_ = repv[:, 0], repv[:, 1], repv[:, 2], repv[0:CROWS, 3]
        mx = sb("mx", [QROWS, 2, LANES, 6])
        ptv = xhl[0:BLOCK, 0:PAIRS * LANES * QROWS].bitcast(F16).rearrange(
            "p (k b r q) -> p k b r q", k=2, b=PAIRS, r=LANES)
        PTh, PTl = ptv[:, 0], ptv[:, 1]
        rden = sb("rden", [QROWS, PAIRS, LANES, GROUPS])
        cn = awst[0:QROWS, :, :].rearrange("p a b -> p (a b)")[:, 0:PAIRS * 256].rearrange(
            "p (b d) -> p b d", b=PAIRS)
        PC = PT_ * P
        stage = sb("stage", [P, 4 * PC + PT_ * D])
        piece0 = sb("piece0", [P, 3 * PC + PT_ * D])

        def stages(p):
            r = (stage, stage, xhl)[p]
            ab = r[:, 0:4 * PC].rearrange("p (k g c) -> p k g c", k=2, g=2)
            return ab[:, 0], ab[:, 1], r[:, 4 * PC:4 * PC + PT_ * D].rearrange("p (f d) -> p f d", f=PT_)

        def split(p):
            r = (piece0, slab, xsq)[p]
            up = r[:, 0:3 * PC].bitcast(F16).rearrange("p (k g c) -> p k g c", k=3, g=2)
            dn = r[:, 3 * PC:3 * PC + PT_ * D].bitcast(F16).rearrange("p (k f d) -> p k f d", k=2, f=PT_)
            return up[:, 0], up[:, 1], up[:, 2], dn[:, 0], dn[:, 1]

        Gb = xs[:, 0:EXPERTS * N].rearrange("p (e n) -> p e n", e=EXPERTS)
        g8 = whl[:, 0:480].rearrange("p (k t e) -> p k t e", k=12, t=TILES)
        lg = whl[:, 480:525].rearrange("p (t e) -> p t e", t=TILES)
        Gf = whl[:, 525:565].rearrange("p (t e) -> p t e", t=TILES)
        GT = sb("GT", [EXPERTS, NPAD])
        work = vhl[:, 0:7 * HALF].rearrange("p (k n) -> p k n", k=7)
        silu, sgate, hf = work[:, 0:2], work[:, 2:4], work[:, 4:7]
        ABUF = 3
        ahlv = kq[:, 0:ABUF * NPAD].bitcast(F16).rearrange("p (k b n) -> p k b n", k=2, b=ABUF)
        ah, al = ahlv[:, 0], ahlv[:, 1]
        acc = t1
        wsum = hn[:, 0:3, :].rearrange("p t d -> p (t d)")[:, 0:3 * D]
        fin = hn

        d_x = [sem(f"d_x{i}") for i in range(4)]
        d_w = [sem(f"d_w{i}") for i in range(SHIFTS + 1)]
        d_gb, d_cst, d_rows, d_tab, d_aw = sem("d_gb"), sem("d_cst"), sem("d_rows"), sem("d_tab"), sem("d_aw")
        d_f = [sem(f"d_f{i}") for i in range(PIECES)]
        d_g = [sem(f"d_g{e}") for e in range(EXPERTS)]
        d_gt, d_out = sem("d_gt"), sem("d_out")
        names = """p_st p_cs p_bw p_main p_bias p_t p_k p_q p_v p_s p_pt p_av p_ct p_wo p_r p_gt p_gu p_dn p_end
                   a_first a_xh a_xsq a_ring a_bw a_cs a_aw a_wh a_sqrt a_hi a_kh a_q1 a_vh a_exp a_pth a_chi a_e a_dup a_sig a_gt
                   a_fw a_silu a_ah
                   v_one v_pad v_jm v_jr v_xl v_fold v_wl v_awl v_mk v_stat v_h v_hn v_lo  v_kk v_q2 v_vm v_xr v_sg v_max v_sub
                   v_ptl v_cn v_rd v_clo v_lg v_gate v_gx v_fw v_hf v_acc v_fin v_al v_bn
                   g_sum g_cs g_awl g_pad g_vl g_sg g_al g_dup""".split()
        S = {n: sem(n) for n in names}

        def bank(b, rows=P):
            return PS[0:rows, b, :]

        def xparts(cols, kc=CROWS):
            return [XAh[:, cols], XAh[:, cols], XB[:, cols], XAl[:, cols], XC[0:kc, cols]]

        def cparts(cols):
            return [CAh[:, cols], CAh[:, cols], CB[:, cols], CAl[:, cols], CC[:, cols]]

        def wparts(c0, c1):
            return [WAh[:, c0:c1], WAl[:, c0:c1], WB[:, c0:c1], WAh[:, c0:c1], WC[:, c0:c1]]

        def pair_cols(C, p, rows):
            c0 = 2 * p * POSITIONS
            return C[0:rows, c0:c0 + 2 * POSITIONS].rearrange("p (b q) -> p b q", b=2)

        def pair_queries(b, pr, k, rows):
            c0 = (2 * pr + k) * QROWS
            return PS[0:rows, b, c0:c0 + 2 * 64].rearrange("p (b q) -> p b q", b=2)[:, :, 0:POSITIONS]

        block = ctx.enter_context(nc.Block())

        @block.sync
        def _(sp):
            def load_pixels(i):
                rows, src = (P, x_inner[:, 2 * i:2 * i + 2, :]) if i < 3 else (RK, x_ring)
                sp.dma_start(xsv[0:rows, 2 * i:2 * i + 2, :], src).then_inc(d_x[i], 16)

            sp.dma_start(gbs[:, :, :], gb).then_inc(d_gb, 16)
            for s in range(SHIFTS):
                sp.dma_start(slabv[:, s], w_inner[s]).then_inc(d_w[s], 16)
                if s == 0:
                    sp.dma_start(cst[:, :], consts).then_inc(d_cst, 16)
                    load_pixels(0)
                if s == 1:
                    sp.dma_start(wring[0:RK, :, :], w_ring).then_inc(d_w[SHIFTS], 16)
                    load_pixels(1)
            load_pixels(2)
            load_pixels(3)
            sp.dma_start(tokb[:, :], tok_b).then_inc(d_rows, 16)
            sp.dma_start(biasrow[1:2, :], cls).then_inc(d_rows, 16)
            sp.dma_start(inds[:, :], ind).then_inc(d_rows, 16)
            for r0 in (0, 64):
                sp.dma_start(tabs[r0:r0 + POSITIONS, :, :], tab).then_inc(d_tab, 16)
                sp.dma_start(jrev[r0:r0 + POSITIONS, :], j_rev).then_inc(d_tab, 16)
            sp.dma_start(awst[:, 0, :], aw_a).then_inc(d_aw, 16)
            sp.dma_start(awst[:, 1, :], aw_b).then_inc(d_aw, 16)
            sp.dma_start(awst[0:CROWS, 2, :], aw_c).then_inc(d_aw, 16)
            for p in range(PIECES):
                if p == 1:
                    sp.wait_ge(S["a_fw"], 6)
                    sp.wait_ge(S["v_fw"], 6)
                if p == 2:
                    sp.wait_ge(S["p_av"], PAIRS)
                cols = slice(p * PC, (p + 1) * PC)
                sa, sbb, sd = stages(p)
                sp.dma_start(sa, f_a[:, :, cols]).then_inc(d_f[p], 16)
                sp.dma_start(sbb, f_b[:, :, cols]).then_inc(d_f[p], 16)
                sp.dma_start(sd, f_d[:, p * PT_:(p + 1) * PT_, :]).then_inc(d_f[p], 16)
            sp.wait_ge(S["a_gt"], 2)
            sp.dma_start(gate_rows[:, :], GT[:, 0:N]).then_inc(d_gt, 16)
            sp.wait_ge(d_gt, 16)
            for e in range(EXPERTS):
                sp.dma_start(Gb[:, e, :], gate_rows[e:e + 1, :].to_broadcast([P, N])).then_inc(d_g[e], 16)
            for t0, t1_ in ((0, 2), (2, 4)):
                sp.wait_ge(S["v_fin"], t1_)
                sp.dma_start(out[t0 * P:t1_ * P, :].rearrange("(t p) d -> p t d", p=P),
                             fin[:, t0:t1_, 0:D]).then_inc(d_out, 16)
            sp.wait_ge(S["v_fin"], TILES)
            sp.dma_start(out[4 * P:N, :], fin[0:REST, 4, 0:D]).then_inc(d_out, 16)
            sp.wait_ge(d_out, 48)

        @block.tensor
        def _(pe):
            mm = nc.tensor.matmul

            def beta_rows(first, chunks, weights):
                for j, (K, w) in enumerate(zip(chunks, weights)):
                    mm(PS[0:1, 2, 0:D], gbs[0:K, 1, first + j:first + j + 1], w, start=(first + j == 0), stop=False)

            pe.wait_ge(d_gb, 16)
            for s in range(SHIFTS):
                pe.wait_ge(d_w[s], 16)
                beta_rows(s * INNER, [P] * INNER, [slabv[:, s, j, :] for j in range(INNER)])
                if s == 1:
                    pe.wait_ge(d_w[SHIFTS], 16)
                    beta_rows(SHIFTS * INNER, [RK] * RING, [wring[0:RK, j, :] for j in range(RING)])
            def square_sums():
                pe.wait_ge(S["g_sum"], 3)
                pe.wait_ge(S["v_pad"], 1)
                for t in range(TILES):
                    for k in (0, 1):
                        last = mm(PS[:, 1, t:t + 1], xsqv[:, k, t * P:(t + 1) * P], one[:, :],
                                  start=(t == 0 and k == 0), stop=(k == 1), skip_group_check=True)
                last.then_inc(S["p_st"], 1)
            def weight_sums():
                pe.wait_ge(S["g_cs"], 4)
                pe.wait_ge(S["a_bw"], 1)
                mm(PS[:, 2, 0:D], one[:, :].to_broadcast([P, P]), wsum[:, 0:D], start=True,
                   stop=True).then_inc(S["p_cs"], 1)

            pe.wait_ge(S["a_cs"], 1)
            for j in range(CHUNKS):
                if j == 2:
                    pe.wait_ge(d_rows, 48)
                    pe.wait_ge(S["v_one"], 1)
                    mm(PS[0:1, 2, 0:D], one[0:1, :], tokb[:, :], start=False, stop=True).then_inc(S["p_bw"], 1)
                if j == INNER + 1:
                    weight_sums()
                K = P if j < INNER else RK
                pe.wait_ge(S["a_xh"], j // 2 + 1)
                pe.wait_ge(S["v_xl"], j // 2 + 1)
                pe.wait_ge(S["a_wh"], j // 2 + 1)
                pe.wait_ge(S["v_wl"], j // 2 + 1)
                for t in range(TILES):
                    tok = slice(t * P, (t + 1) * P)
                    o = PS[:, 3 + t // 2, 200 * (t % 2):200 * (t % 2) + D + 1]
                    mm(o, xh[0:K, j, tok], wh[0:K, j, :], start=(j == 0 and t % 2 == 0), stop=False,
                       skip_group_check=True)
                    mm(o, xl[0:K, j, tok], wh[0:K, j, :], start=False, stop=False, skip_group_check=True)
                    last = mm(o[:, 0:D], xh[0:K, j, tok], wl[0:K, j, :], start=False, stop=(j == CHUNKS - 1),
                              skip_group_check=True)
            last.then_inc(S["p_main"], 1)
            square_sums()
            pe.wait_ge(S["a_bw"], 1)
            for t in range(TILES):
                tok = slice(t * P, (t + 1) * P)
                mm(PS[:, (6, 6, 7, 7, 0)[t], D * (t % 2):D * (t % 2) + D], inds[:, tok], biasrow[:, :],
                   start=(t % 2 == 0), stop=True, skip_group_check=True).then_inc(S["p_bias"], 1)

            def transposes(n, banks, tiles):
                for t in tiles:
                    pe.wait_ge(S["v_hn"], TILES * n + t + 1)
                    oa = PS[:, banks[0], t * P:(t + 1) * P] if t < 3 else PS[:, banks[2], (t - 3) * P:(t - 2) * P]
                    ob = PS[:, banks[1], t * P:(t + 1) * P] if t < 3 else PS[:, banks[2], (t - 1) * P:t * P]
                    nc.tensor.transpose(oa, hn[:, t, 0:P], ident)
                    pe.wait_ge(S["a_dup"], TILES * n + t + 1)
                    nc.tensor.transpose(ob, hn[:, t, P:2 * P], ident).then_inc(S["p_t"], 1)

            transposes(0, (1, 2, 0), range(3))

            def tokens_ready(n, half, k):
                if k in (0, 2):
                    pe.wait_ge(S["a_hi"], 4 * n + 2 * half + (1 if k == 0 else 2))
                if k in (3, 4):
                    pe.wait_ge(S["v_lo"], 4 * n + 2 * half + (1 if k == 3 else 2))

            pe.wait_ge(S["a_aw"], 3)
            pe.wait_ge(S["v_awl"], 2)
            pe.wait_ge(S["g_awl"], 2)
            for f in range(12):
                q, g, half = kq_product(f)
                if f == 3:
                    transposes(0, (1, 2, 0), (3, 4))
                c0 = (QC if q else KC) + g * P
                if f >= 4:
                    q4, g4, half4 = kq_product(f - 4)
                    pe.wait_ge(S["v_q2" if q4 else "v_kk"], GROUPS * half4 + g4 + 1)
                cols = slice(half * HALF, (half + 1) * HALF)
                for i, (w, x) in enumerate(zip(wparts(c0, c0 + P), xparts(cols))):
                    if f in (0, 6):
                        tokens_ready(0, half, i)
                    last = mm(PS[:, 3 + f % 4, 0:HALF], w, x, start=(i == 0), stop=(i == 4))
                last.then_inc(S["p_q" if q else "p_k"], 1)

            def values(i):
                pe.wait_ge(S["v_awl"], 4)
                pe.wait_ge(S["v_xr"], 4 if i < 4 else 8)
                if i >= 4:
                    pe.wait_ge(S["v_vm"], i - 3)
                for b in (0, 1):
                    xr = [x[:, (2 * i + b) * BLOCK:(2 * i + b + 1) * BLOCK] for x in (RAh, RAh, RB, RAl, RC_)]
                    for k, (w, x) in enumerate(zip(wparts(VC, VC + D), xr)):
                        last = mm(PS[0:BLOCK, (7, 0, 1, 2)[i % 4], b * D:(b + 1) * D], x, w,
                                  start=(k == 0 and b == 0), stop=(k == 4), skip_group_check=True)
                last.then_inc(S["p_v"], 1)

            def scores(u):
                if u >= 1:
                    pe.wait_ge(S["v_sub"], u)
                for r in range(LANES):
                    mm(PS[0:QROWS, 3 + r, 0:SCOLS], mk[:, :], jrep[:, :, :].rearrange("p h k -> p (h k)"),
                       start=True, stop=False, skip_group_check=True)
                for pair in range(2):
                    for bi in (0, 1):
                        b = 2 * (2 * u + pair) + bi
                        tok = slice(b * POSITIONS, (b + 1) * POSITIONS)
                        for g in range(GROUPS):
                            for Q in (Q1, Q2):
                                for r in range(LANES):
                                    rows = slice(32 * r, 32 * r + 32)
                                    col = pair * BLOCK + g * POSITIONS
                                    last = mm(PS[64 * bi:64 * bi + POSITIONS, 3 + r, col:col + POSITIONS],
                                              Q[rows, g, tok], KK[rows, g, tok], start=False, stop=(Q is Q2),
                                              skip_group_check=True)
                last.then_inc(S["p_s"], 1)

            def pt(p):
                u, pair = divmod(p, 2)
                pe.wait_ge(S["a_exp"], u + 1)
                if p >= 2:
                    pe.wait_ge(S["v_ptl"], p - 1)
                for r in range(LANES):
                    last = nc.tensor.transpose(PS[0:BLOCK, (7, 0)[p % 2], r * QROWS:(r + 1) * QROWS],
                                               prob[:, u % 2, r, pair * BLOCK:(pair + 1) * BLOCK],
                                               ident[0:QROWS, 0:QROWS])
                last.then_inc(S["p_pt"], 1)

            def av(p):
                pe.wait_ge(S["a_pth"], p + 1)
                pe.wait_ge(S["v_ptl"], p + 1)
                pe.wait_ge(S["g_vl"], p + 1)
                if p in (2, 4):
                    pe.wait_ge(S["v_cn"], p)
                if p == 6:
                    pe.wait_ge(S["v_sub"], 4)
                for bi in (0, 1):
                    q0, q1 = (0, 64) if bi == 0 else (64, QROWS)
                    for r in range(LANES):
                        c0 = (p % 2) * LANES * VW + r * VW
                        for k, (a, v) in enumerate(((PTh, vh), (PTl, vh), (PTh, vl))):
                            last = mm(PS[q0:q1, 1 if p < 6 else 6, c0:c0 + VW], a[:, p, r, q0:q1], v[:, 2 * p + bi, r, :],
                                      start=(p % 2 == 0 and r == 0 and k == 0), stop=(k == 2),
                                      skip_group_check=True)
                last.then_inc(S["p_av"], 1)

            def ct(p):
                pe.wait_ge(S["v_cn"], p + 1)
                pe.wait_ge(S["g_dup"], p + 1)
                if p in (2, 4):
                    pe.wait_ge(S["v_clo"], p)
                if p == 6:
                    pe.wait_ge(S["v_ptl"], PAIRS)
                b = 2 if p < 6 else 7
                c0 = (p % 2) * 2 * QROWS
                nc.tensor.transpose(PS[:, b, c0:c0 + QROWS], cn[:, p, 0:P], ident[0:QROWS, 0:QROWS])
                nc.tensor.transpose(PS[:, b, c0 + QROWS:c0 + 2 * QROWS], cn[:, p, P:2 * P],
                                    ident[0:QROWS, 0:QROWS]).then_inc(S["p_ct"], 1)

            def wo(t):
                need = min(2 * (t + 1), PAIRS)
                pe.wait_ge(S["v_clo"], need)
                tok = slice(t * P, (t + 1) * P)
                for k, (x, w) in enumerate(zip(cparts(tok), wparts(OC, OC + D))):
                    last = mm(PS[:, (3, 3, 4, 4, 5)[t], D * (t % 2):D * (t % 2) + D], x, w,
                              start=(k == 0 and t % 2 == 0), stop=(k == 4), skip_group_check=True)
                last.then_inc(S["p_wo"], 1)

            for i in range(4):
                values(i)
            pe.wait_ge(S["v_mk"], 1)
            pe.wait_ge(S["v_jr"], 2)
            pe.wait_ge(S["v_kk"], 6)
            pe.wait_ge(S["v_q2"], 6)
            scores(0)
            for i in range(4, 7):
                values(i)
            for u in range(4):
                if u < 3:
                    scores(u + 1)
                if u == 0:
                    pe.wait_ge(S["v_vm"], 6)
                pt(2 * u)
                pt(2 * u + 1)
                if u == 0:
                    values(7)
                if u == 1:
                    pe.wait_ge(S["v_vm"], PAIRS)
                if u >= 1:
                    av(2 * u - 2)
                    av(2 * u - 1)
                if u >= 2:
                    ct(2 * u - 4)
                    ct(2 * u - 3)
            av(6)
            av(7)
            ct(4)
            ct(5)
            wo(0)
            wo(1)
            ct(6)
            ct(7)
            wo(2)
            wo(3)
            wo(4)

            transposes(1, (0, 1, 2), range(TILES))

            def router():
                pe.wait_ge(S["a_hi"], 8)
                pe.wait_ge(S["v_lo"], 8)
                for t in range(TILES):
                    tok = slice(t * P, (t + 1) * P)
                    for k, (x, w) in enumerate(zip(xparts(tok), wparts(RC, RC + 9))):
                        last = mm(PS[:, 7, 9 * t:9 * t + 9], x, w, start=(t == 0 and k == 0), stop=(k == 4),
                                  skip_group_check=True)
                last.then_inc(S["p_r"], 1)

            def gu(i):
                f, half = divmod(i, 2)
                if i % (2 * PT_) == 0:
                    pe.wait_ge(S["a_fw"], 6 * (f // PT_) + 6)
                    pe.wait_ge(S["v_fw"], 6 * (f // PT_) + 6)
                if i >= 2:
                    pe.wait_ge(S["v_hf"], i - 1)
                cols = slice(half * HALF, (half + 1) * HALF)
                Ah, Al, Bw, _, _ = split(f // PT_)
                fc = slice(f % PT_ * P, (f % PT_ + 1) * P)
                for m in range(2):
                    if i == 0 and m == 1:
                        router()
                    w5 = (Ah[:, m, fc], Al[:, m, fc], Bw[:, m, fc], Ah[:, m, fc], Bw[0:64, m, fc])
                    for k, (w, x) in enumerate(zip(w5, xparts(cols, 64))):
                        if i < 2 and m == 0:
                            tokens_ready(1, i, k)
                        last = mm(PS[:, 3 + 2 * (i % 2) + m, 0:HALF], w, x, start=(k == 0), stop=(k == 4))
                last.then_inc(S["p_gu"], 1)

            def gates(k):
                if k == 0:
                    pe.wait_ge(S["v_gx"], 1)
                else:
                    pe.wait_ge(S["a_gt"], 1)
                for t in (range(4) if k == 0 else (4,)):
                    last = nc.tensor.transpose(PS[0:EXPERTS, 7, t % 4 * P:(t % 4 + 1) * P], Gf[:, t, :], ident)
                last.then_inc(S["p_gt"], 1)

            def down(f):
                pe.wait_ge(S["a_ah"], 2 * f + 2)
                pe.wait_ge(S["g_al"], min(2 * f + 2, 2 * FT - 1))
                if f == FT - 1:
                    pe.wait_ge(S["v_al"], 1)
                if f == 0:
                    pe.wait_ge(S["v_pad"], 2)
                if f == ST:
                    pe.wait_ge(S["v_acc"], TILES)
                Dh, Dl = split(f // PT_)[3:]
                for t in range(TILES):
                    tok = slice(t * P, (t + 1) * P)
                    o = PS[:, t // 2, D * (t % 2):D * (t % 2) + D]
                    for k, (a, w) in enumerate(((ah, Dh), (al, Dh), (ah, Dl))):
                        last = mm(o, a[:, f % ABUF, tok], w[:, f % PT_, :], start=(f in (0, ST) and t % 2 == 0 and k == 0),
                                  stop=(f in (ST - 1, FT - 1) and k == 2), skip_group_check=True)
                    if f == FT - 1 and t in (1, 3):
                        last.then_inc(S["p_end"], 1)
                last.then_inc(S["p_dn"] if f < FT - 1 else S["p_end"], 1)

            for f in range(FT + 2):
                for half in range(2):
                    if f < FT:
                        gu(2 * f + half)
                    if 0 <= 2 * f + half - GATE_STEP < 2:
                        gates(2 * f + half - GATE_STEP)
                if f >= 2:
                    down(f - 2)

        @block.scalar
        def _(act):
            A = nc.scalar.activation
            def squares(i):
                act.wait_ge(d_x[i], 16)
                K = P if i < 3 else RK
                for j in (2 * i, 2 * i + 1):
                    A(xsqv[0:K, j, 0:N], xsv[0:K, j, :], ACT.Square,
                      scale=cntroot[0:K, j:j + 1]).then_inc(S["a_xsq"], 1)

            def pixels(i):
                act.wait_ge(d_x[i], 16)
                K = P if i < 3 else RK
                A(xh[0:K, 2 * i:2 * i + 2, 0:N], xsv[0:K, 2 * i:2 * i + 2, :], ACT.Copy,
                  scale=SPIX).then_inc(S["a_xh"], 1)

            act.wait_ge(S["v_one"], 1)
            A(small[:, 47, 0:1], one[:, :], ACT.Square).then_inc(S["a_first"], 1)
            act.wait_ge(d_cst, 16)
            pixels(0)
            squares(0)
            pixels(1)
            squares(1)
            A(wh[:, :, D:D + 1].rearrange("p c o -> p (c o)"), cnt, ACT.Copy).then_inc(S["a_cs"], 1)
            act.wait_ge(d_w[SHIFTS], 16)
            act.wait_ge(d_gb, 16)
            for j in range(RING):
                A(we[0:RK, INNER + j, :], wring[0:RK, j, :], ACT.Identity,
                  scale=gbs[0:RK, 0, 30 + j:31 + j]).then_inc(S["a_ring"], 1)
            def weights_high(i):
                K = P if i < 3 else RK
                if i < 3:
                    act.wait_ge(S["v_fold"], (SHIFTS - 1) * INNER + 2 * i + 2)
                else:
                    act.wait_ge(S["a_ring"], RING)
                A(wh[0:K, 2 * i:2 * i + 2, 0:D], we[0:K, 2 * i:2 * i + 2, :], ACT.Copy, scale=SPW).then_inc(S["a_wh"], 1)

            weights_high(0)
            pixels(2)
            weights_high(1)
            squares(2)
            weights_high(2)
            pixels(3)
            squares(3)
            weights_high(3)
            act.wait_ge(S["p_bw"], 1)
            A(biasrow[0:1, :], PS[0:1, 2, 0:D], ACT.Copy).then_inc(S["a_bw"], 1)
            act.wait_ge(d_aw, 48)
            A(WAh[:, :], awst[:, 0, :], ACT.Copy, scale=SW).then_inc(S["a_aw"], 1)
            A(WB[:, :], awst[:, 1, :], ACT.Copy, scale=SW).then_inc(S["a_aw"], 1)
            A(WC[:, :], awst[0:CROWS, 2, :], ACT.Copy, scale=SW).then_inc(S["a_aw"], 1)

            def ffn_high(p, q):
                if q == 0:
                    act.wait_ge(d_f[p], 48)
                Ah, _, Bw, Dh, _ = split(p)
                k, m = divmod(q, 2)
                W, st = (Ah, Bw, Dh)[k], stages(p)[k]
                part = slice(3 * m, 3 * m + 3) if k == 2 else slice(m, m + 1)
                A(W[:, part], st[:, part], ACT.Copy, scale=SW).then_inc(S["a_fw"], 1)

            act.wait_ge(S["p_cs"], 1)
            A(csum[:, :], PS[:, 2, 0:D], ACT.Copy, scale=SPW).then_inc(S["a_cs"], 1)

            def root(k):
                row, tiles, ready = NORMS[k]
                act.wait_ge(S["v_stat"], ready)
                A(small[:, row + 1, tiles[0]:tiles[-1] + 1], small[:, row, tiles[0]:tiles[-1] + 1],
                  ACT.Sqrt).then_inc(S["a_sqrt"], 1)

            def high_parts(n, banks, part):
                a, b = ((PS[:, banks[0], 0:FRONT], PS[:, banks[1], 0:FRONT]) if part == 0 else
                        (PS[:, banks[2], 0:2 * P], PS[:, banks[2], 2 * P:4 * P]))
                cols = slice(0, FRONT) if part == 0 else slice(FRONT, NPAD)
                act.wait_ge(S["p_t"], TILES * n + (3, 5)[part])
                if n == 1 and part == 0:
                    act.wait_ge(S["p_v"], PAIRS)
                A(XAh[:, cols], a, ACT.Copy, scale=SX).then_inc(S["a_hi"], 1)
                A(XB[:, cols], b, ACT.Copy, scale=SX).then_inc(S["a_hi"], 1)

            def copies(n, tiles):
                for t in tiles:
                    act.wait_ge(S["v_hn"], TILES * n + t + 1)
                    A(hn[:, t, D:256], hn[:, t, P:D], ACT.Copy).then_inc(S["a_dup"], 1)

            def kq_high(f):
                q, g, half = kq_product(f)
                cols = slice(half * HALF, (half + 1) * HALF)
                act.wait_ge(S["p_q" if q else "p_k"], GROUPS * half + g + 1)
                if q:
                    A(Q1[:, g, cols], PS[:, 3 + f % 4, 0:HALF], ACT.Copy, scale=SQ / XW).then_inc(S["a_q1"], 1)
                else:
                    A(kh[:, g, cols], PS[:, 3 + f % 4, 0:HALF], ACT.Copy, scale=kscale).then_inc(S["a_kh"], 1)

            root(0)
            ffn_high(0, 0)
            ffn_high(0, 1)
            root(1)
            copies(0, range(3))
            root(2)
            high_parts(0, (1, 2, 0), 0)
            copies(0, (3, 4))
            kq_high(0)
            kq_high(1)
            kq_high(2)
            high_parts(0, (1, 2, 0), 1)
            for f in range(3, 12):
                kq_high(f)

            def exps(u):
                act.wait_ge(S["v_sub"], u + 1)
                if u >= 2:
                    act.wait_ge(S["p_pt"], 2 * u - 2)
                A(prob[:, u % 2], sdif[:, u % 2], ACT.Exp, scale=1.0 / (SK * SQ * 4)).then_inc(S["a_exp"], 1)

            act.wait_ge(S["g_pad"], 1)
            A(vh[:, :, :, GROUPS * HD:VW].rearrange("p b r o -> p (b r) o"),
              bones[0:BLOCK, :].unsqueeze(1).to_broadcast([BLOCK, IMAGES * LANES, GROUPS]),
              ACT.Copy).then_inc(S["a_vh"], 1)
            def values_high(i):
                act.wait_ge(S["v_vm"], i + 1)
                A(vh[:, 2 * i:2 * i + 2, :, 0:GROUPS * HD],
                  vm[:, 2 * i:2 * i + 2, :].rearrange("p b (r c) -> p b r c", r=LANES),
                  ACT.Copy).then_inc(S["a_vh"], 1)

            for i in range(4):
                values_high(i)
            for q in range(2, 6):
                ffn_high(0, q)
            exps(0)
            for i in range(4, 7):
                values_high(i)

            def ctx_high(i):
                act.wait_ge(S["p_ct"], 2 * i + 2)
                for k, C in enumerate((CAh, CB)):
                    for pr in (0, 1):
                        last = A(pair_cols(C, 2 * i + pr, P), pair_queries(2 if i < 3 else 7, pr, k, P), ACT.Copy)
                last.then_inc(S["a_chi"], 2)

            for u in range(4):
                for p in (2 * u, 2 * u + 1):
                    act.wait_ge(S["p_pt"], p + 1)
                    A(PTh[:, p].rearrange("p r q -> p (r q)"), PS[0:BLOCK, (7, 0)[p % 2], 0:LANES * QROWS], ACT.Copy,
                      scale=SP_).then_inc(S["a_pth"], 1)
                if u < 3:
                    exps(u + 1)
                if u == 0:
                    values_high(7)
                if u >= 2:
                    ctx_high(u - 2)
            ctx_high(2)
            ctx_high(3)
            ffn_high(1, 0)
            ffn_high(1, 1)
            root(3)
            copies(1, range(TILES))
            high_parts(1, (0, 1, 2), 0)
            high_parts(1, (0, 1, 2), 1)
            act.wait_ge(S["v_lg"], 1)
            A(small[:, 30, :], lg[:, :, 8], ACT.Exp, scale=-1.0).then_inc(S["a_sig"], 1)
            A(small[:, 31, :], lg[:, :, 8], ACT.Exp).then_inc(S["a_sig"], 1)
            act.wait_ge(S["v_gate"], 1)
            A(g8[:, 1], g8[:, 0], ACT.Exp).then_inc(S["a_e"], 1)

            def silu_step(i):
                act.wait_ge(S["p_gu"], i + 1)
                if i >= 2:
                    act.wait_ge(S["v_hf"], i - 1)
                A(silu[:, i % 2, :], PS[:, 3 + 2 * (i % 2), 0:HALF], ACT.Silu, scale=1.0 / XW).then_inc(S["a_silu"], 1)

            def act_high(i):
                f, half = divmod(i, 2)
                act.wait_ge(S["v_hf"], i + 1)
                if half == 0 and f >= ABUF:
                    act.wait_ge(S["p_dn"], f - ABUF + 1)
                A(ah[:, f % ABUF, half * HALF:(half + 1) * HALF], hf[:, i % 3, :], ACT.Copy).then_inc(S["a_ah"], 1)

            def gate_copy(k):
                act.wait_ge(S["p_gt"], k + 1)
                c0, c1 = ((0, 512), (512, NPAD))[k]
                A(GT[:, c0:c1], PS[0:EXPERTS, 7, 0:c1 - c0], ACT.Copy).then_inc(S["a_gt"], 1)

            for i in range(2 * FT + 1):
                if 0 <= i - 1 - GATE_STEP < 2:
                    gate_copy(i - 1 - GATE_STEP)
                if i < 2 * FT:
                    silu_step(i)
                if i >= 1:
                    act_high(i - 1)
                if 2 <= i < 6:
                    ffn_high(1, i)
                if i in range(8, 20, 2):
                    ffn_high(2, (i - 8) // 2)

        @block.gpsimd
        def _(pool):
            G = nc.gpsimd
            def square_sum(i):
                K = P if i < 3 else RK
                pool.wait_ge(S["a_xsq"], 2 * i + 2)
                if i > 1:
                    pool.wait_ge(S["g_sum"], i - 1)
                G.tensor_tensor(xsqv[0:K, 0:2, 0:N], xsqv[0:K, 0:2, 0:N], xsqv[0:K, 2 * i:2 * i + 2, 0:N],
                                ALU.add).then_inc(S["g_sum"], 1)

            square_sum(1)
            pool.wait_ge(S["v_fold"], SHIFTS * INNER)
            G.tensor_tensor(wsum[:, :], wef[:, 0:3 * D], wef[:, 3 * D:6 * D], ALU.add).then_inc(S["g_cs"], 1)
            pool.wait_ge(S["a_ring"], RING)
            pool.wait_ge(S["g_cs"], 1)
            G.tensor_tensor(wsum[0:RK, 0:2 * D], wsum[0:RK, 0:2 * D], wef[0:RK, 6 * D:8 * D],
                            ALU.add).then_inc(S["g_cs"], 1)
            for k in (1, 2):
                pool.wait_ge(S["g_cs"], k + 1)
                G.tensor_tensor(wsum[:, 0:D], wsum[:, 0:D], wsum[:, k * D:(k + 1) * D], ALU.add).then_inc(S["g_cs"], 1)
            pool.wait_ge(S["g_cs"], 4)
            square_sum(2)
            square_sum(3)
            pool.wait_ge(S["a_aw"], 3)
            pool.wait_ge(S["g_sum"], 3)
            G.tensor_scalar(awst[96:97, 2, :], awst[96:97, 2, :], SW, None, ALU.mult).then_inc(S["g_awl"], 1)
            pool.wait_ge(S["g_awl"], 1)
            G.tensor_tensor(WC[96:97, :], awst[96:97, 2, :], WC[96:97, :], ALU.subtract).then_inc(S["g_awl"], 1)
            pool.wait_ge(S["g_awl"], 2)
            G.memset(vl[:, :, :, :].rearrange("p b r c -> p (b r c)"), 0.0).then_inc(S["g_pad"], 1)
            pool.wait_ge(S["g_pad"], 1)
            for i in range(PAIRS):
                pool.wait_ge(S["a_vh"], i + 2)
                G.tensor_tensor(vl[:, 2 * i:2 * i + 2, :, 0:GROUPS * HD],
                                vm[:, 2 * i:2 * i + 2, :].rearrange("p b (r c) -> p b r c", r=LANES),
                                vh[:, 2 * i:2 * i + 2, :, 0:GROUPS * HD], ALU.subtract).then_inc(S["g_vl"], 1)
            for p in range(PAIRS):
                pool.wait_ge(S["v_cn"], p + 1)
                G.tensor_copy(cn[:, p, D:256], cn[:, p, P:D]).then_inc(S["g_dup"], 1)

            def gated(i):
                f, half = divmod(i, 2)
                n = i - 2 * ST
                pool.wait_ge(d_g[f_expert(f)[0]], 16)
                pool.wait_ge(S["a_silu"], i + 1)
                if n >= 2:
                    pool.wait_ge(S["v_hf"], i - 1)
                cols = slice(half * HALF, (half + 1) * HALF)
                G.tensor_tensor(sgate[:, i % 2, :], silu[:, i % 2, :], Gb[:, f_expert(f)[0], cols],
                                ALU.mult).then_inc(S["g_sg"], 1)

            def act_low(i):
                f, half = divmod(i, 2)
                cols = slice(half * HALF, (half + 1) * HALF)
                pool.wait_ge(S["a_ah"], i + 1)
                if half == 0 and f >= ABUF:
                    pool.wait_ge(S["p_dn"], f - ABUF + 1)
                G.tensor_tensor(al[:, f % ABUF, cols], hf[:, i % 3, :], ah[:, f % ABUF, cols],
                                ALU.subtract).then_inc(S["g_al"], 1)

            for i in range(2 * FT):
                if 2 * ST <= i < 2 * FT - 2 and not two_experts(i // 2):
                    gated(i)
                if i >= 1:
                    act_low(i - 1)

        @block.vector
        def _(dve):
            V = nc.vector
            V.memset(one[:, :], 1.0).then_inc(S["v_one"], 1)
            V.memset(xh[:, :, N:NPAD], 0.0)
            V.memset(xl[:, :, N:NPAD], 0.0)
            V.memset(XC[64:CROWS, :], SX)
            V.memset(mk[:, :], 0.0)
            V.memset(jrep[:, :, :], 0.0)
            V.memset(mkf[:, :], 0.0).then_inc(S["v_jm"], 1)
            V.memset(xsqv[:, 0:2, N:NPAD], 0.0).then_inc(S["v_pad"], 1)
            def pixels_low(i):
                K = P if i < 3 else RK
                dve.wait_ge(S["a_xh"], i + 1)
                V.scalar_tensor_tensor(out=xl[0:K, 2 * i:2 * i + 2, 0:N], in0=xsv[0:K, 2 * i:2 * i + 2, :], scalar=SPIX,
                                       in1=xh[0:K, 2 * i:2 * i + 2, 0:N], op0=ALU.mult,
                                       op1=ALU.subtract).then_inc(S["v_xl"], 1)

            dve.wait_ge(d_gb, 16)
            def weights_low(i):
                K = P if i < 3 else RK
                dve.wait_ge(S["a_wh"], i + 1)
                V.scalar_tensor_tensor(out=wl[0:K, 2 * i:2 * i + 2, :], in0=we[0:K, 2 * i:2 * i + 2, :], scalar=SPW,
                                       in1=wh[0:K, 2 * i:2 * i + 2, 0:D], op0=ALU.mult,
                                       op1=ALU.subtract).then_inc(S["v_wl"], 1)

            for s in range(SHIFTS):
                dve.wait_ge(d_w[s], 16)
                for j in range(INNER):
                    gamma = gbs[:, 0, s * INNER + j:s * INNER + j + 1]
                    if s == 0:
                        V.tensor_scalar(we[:, j, :], slabv[:, s, j, :], gamma, None, ALU.mult).then_inc(S["v_fold"], 1)
                    else:
                        dve.wait_ge(S["v_fold"], (s - 1) * INNER + j + 1)
                        V.scalar_tensor_tensor(out=we[:, j, :], in0=slabv[:, s, j, :], scalar=gamma, in1=we[:, j, :],
                                               op0=ALU.mult, op1=ALU.add).then_inc(S["v_fold"], 1)
                    if s == SHIFTS - 1 and j == 3:
                        weights_low(0)
                if s == 0:
                    pixels_low(0)
            pixels_low(1)
            weights_low(1)
            pixels_low(2)
            weights_low(2)
            pixels_low(3)
            weights_low(3)
            dve.wait_ge(S["v_wl"], 4)
            dve.wait_ge(S["g_cs"], 2)
            for C in (CAh, CAl, CB):
                V.memset(C[:, N:NPAD], 0.0)
            V.memset(CC[0:64, N:NPAD], 0.0)
            V.memset(CC[64:CROWS, :], SCTX)
            dve.wait_ge(d_tab, 64)
            dve.wait_ge(S["v_jm"], 1)
            two = (slice(0, POSITIONS), slice(64, QROWS))
            for r in two:
                V.tensor_reduce(mksum[r, :], tabs[r, :, :], AX.X, ALU.add).then_inc(S["v_jm"], 1)
                V.tensor_scalar(jrep[r, :, :], jrev[r, :].unsqueeze(1).to_broadcast([POSITIONS, 6, POSITIONS]),
                                16.0, None, ALU.mult).then_inc(S["v_jr"], 1)
            dve.wait_ge(S["v_jm"], 3)
            for r in two:
                for c0 in (0, 64):
                    V.tensor_scalar(mkf[r, c0:c0 + POSITIONS], mksum[r, :], 16.0 / HEADS, None,
                                    ALU.mult).then_inc(S["v_jm"], 1)
            dve.wait_ge(S["v_jm"], 7)
            for r in two:
                V.tensor_copy(mk[r, :], mkf[r, :]).then_inc(S["v_jm"], 1)
            dve.wait_ge(S["v_jm"], 9)
            V.tensor_tensor(mk[two[1], :], mkf[two[1], :], mk[two[1], :], ALU.subtract).then_inc(S["v_mk"], 1)
            def attention_low(k, c0, c1):
                W, hi, rows = ((WAl, WAh, slice(0, P)), (WB, WB, slice(64, P)))[k]
                dve.wait_ge(S["a_aw"], k + 1)
                V.scalar_tensor_tensor(out=W[rows, c0:c1], in0=awst[rows, k, c0:c1], scalar=SW, in1=hi[rows, c0:c1],
                                       op0=ALU.mult, op1=ALU.subtract).then_inc(S["v_awl"], 1)

            attention_low(0, 0, VC)
            attention_low(1, 0, VC)

            def ffn_low(p, q):
                Ah, Al, Bw, Dh, Dl = split(p)
                k, m = divmod(q, 2)
                W, hi, st, r0 = (Al, Bw, Dl)[k], (Ah, Bw, Dh)[k], stages(p)[k], (0, 64, 0)[k]
                part = slice(3 * m, 3 * m + 3) if k == 2 else slice(m, m + 1)
                dve.wait_ge(S["a_fw"], 6 * p + q + 1)
                V.scalar_tensor_tensor(out=W[r0:P, part], in0=st[r0:P, part], scalar=SW, in1=hi[r0:P, part],
                                       op0=ALU.mult, op1=ALU.subtract).then_inc(S["v_fw"], 1)

            stat = [0]

            def step(instruction):
                instruction.then_inc(S["v_stat"], 1)
                stat[0] += 1
                dve.wait_ge(S["v_stat"], stat[0])

            def rsqrt(k, scale=1.0):
                row, tiles, ready = NORMS[k]
                v, sd, r, a, b, rs, o = (small[:, row + i, tiles[0]:tiles[-1] + 1] for i in (0, 1, 2, 3, 4, 5, 9))
                assert stat[0] == ready
                dve.wait_ge(S["a_sqrt"], k + 1)
                step(V.reciprocal(r, sd))
                V.tensor_scalar(rs, r, scale, None, ALU.mult)
                step(V.tensor_tensor(a, r, r, ALU.mult))
                step(V.scalar_tensor_tensor(out=b, in0=a, scalar=-0.5, in1=v, op0=ALU.mult, op1=ALU.mult))
                step(V.scalar_tensor_tensor(out=o, in0=b, scalar=1.5, in1=rs, op0=ALU.add, op1=ALU.mult))

            nmean, nsq = small[:, 6, :], small[:, 7, :]

            def centred(t):
                V.scalar_tensor_tensor(out=t1[:, t, :], in0=csum[:, :], scalar=small[:, 6, t:t + 1],
                                       in1=PS[:, 3 + t // 2, 200 * (t % 2):200 * (t % 2) + D], op0=ALU.mult,
                                       op1=ALU.add).then_inc(S["v_h"], 1)

            dve.wait_ge(S["p_main"], 1)
            V.tensor_scalar(small[:, 6, 0:4].rearrange("p (a b) -> p a b", a=2),
                            PS[:, 3:5, 0:400].rearrange("p a (b c) -> p a b c", b=2)[:, :, :, D], -1.0 / PATCH_DIM,
                            None, ALU.mult)
            step(V.tensor_scalar(small[:, 6, 4:5], PS[:, 5, D:D + 1], -1.0 / PATCH_DIM, None, ALU.mult))
            V.tensor_tensor(nsq, nmean, nmean, ALU.mult).then_inc(S["v_stat"], 1)
            stat[0] += 1
            dve.wait_ge(S["a_cs"], 2)
            for t in range(4):
                centred(t)
            dve.wait_ge(S["v_stat"], stat[0])
            dve.wait_ge(S["p_st"], 1)
            step(V.tensor_scalar(small[:, 8, :], PS[:, 1, 0:TILES], 1.0 / PATCH_DIM, None, ALU.mult))
            step(V.scalar_tensor_tensor(out=small[:, 3, :], in0=nsq, scalar=-1.0 / SPIX ** 2, in1=small[:, 8, :],
                                        op0=ALU.mult, op1=ALU.add))
            step(V.tensor_scalar(small[:, 0, :], small[:, 3, :], 0.0, EPS, ALU.max, ALU.add))
            centred(4)
            rsqrt(0, 1.0 / (SPIX * SPW))

            bn = [0]

            def residual(n, op, tiles):
                src = (h1, h2)[n]
                for t in tiles:
                    op(t).then_inc(S["v_h"], 1)
                for t in tiles:
                    dve.wait_ge(S["v_h"], TILES * (n + 1) + t + 1)
                    V.bn_stats(bst[:, t, :], src[:, t, :]).then_inc(S["v_bn"], 1)
                    bn[0] += 1

            def variances(k):
                row, tiles, _ = NORMS[k]
                dve.wait_ge(S["v_bn"], bn[0])
                for t in tiles:
                    V.bn_aggr(mv[:, t, :], bst[:, t, :]).then_inc(S["v_bn"], 1)
                bn[0] += len(tiles)
                dve.wait_ge(S["v_bn"], bn[0])
                step(V.tensor_scalar(small[:, row, tiles[0]:tiles[-1] + 1], mv[:, tiles[0]:tiles[-1] + 1, 1], EPS, None,
                                     ALU.add))

            def normed(n, tiles):
                src, row = (h1, h2)[n], 10 * (n + 1)
                for t in tiles:
                    V.tensor_scalar(hn[:, t, 0:D], src[:, t, :], mv[:, t, 0:1], small[:, row + 9, t:t + 1],
                                    ALU.subtract, ALU.mult).then_inc(S["v_hn"], 1)

            def low_parts(n, banks, part):
                a, b = ((PS[:, banks[0], 0:FRONT], PS[0:64, banks[1], 0:FRONT]) if part == 0 else
                        (PS[:, banks[2], 0:2 * P], PS[0:64, banks[2], 2 * P:4 * P]))
                cols = slice(0, FRONT) if part == 0 else slice(FRONT, NPAD)
                for k, (dst, src, hi) in enumerate(((XAl[:, cols], a, XAh[:, cols]), (XC[0:64, cols], b, XB[0:64, cols]))):
                    dve.wait_ge(S["a_hi"], 4 * n + (k + 1 if part == 0 else 4))
                    V.scalar_tensor_tensor(out=dst, in0=src, scalar=SX, in1=hi, op0=ALU.mult,
                                           op1=ALU.subtract).then_inc(S["v_lo"], 1)

            dve.wait_ge(S["v_h"], TILES)

            def add_patches(t):
                dve.wait_ge(S["p_bias"], (2, 2, 4, 4, 5)[t])
                return V.scalar_tensor_tensor(
                    out=h1[:, t, :], in0=t1[:, t, :], scalar=small[:, 9, t:t + 1],
                    in1=PS[:, (6, 6, 7, 7, 0)[t], D * (t % 2):D * (t % 2) + D], op0=ALU.mult, op1=ALU.add)

            residual(0, add_patches, (0, 1, 2))
            variances(1)
            residual(0, add_patches, (3, 4))
            rsqrt(1)
            normed(0, range(3))
            variances(2)

            def kq_low(f):
                q, g, half = kq_product(f)
                cols = slice(half * HALF, (half + 1) * HALF)
                if q:
                    dve.wait_ge(S["a_q1"], GROUPS * half + g + 1)
                    V.scalar_tensor_tensor(out=Q2[:, g, cols], in0=PS[:, 3 + f % 4, 0:HALF], scalar=SQ / XW,
                                           in1=Q1[:, g, cols], op0=ALU.mult, op1=ALU.subtract).then_inc(S["v_q2"], 1)
                else:
                    dve.wait_ge(S["a_kh"], GROUPS * half + g + 1)
                    V.scalar_tensor_tensor(out=KK[:, g, cols], in0=PS[:, 3 + f % 4, 0:HALF], scalar=SK / XW,
                                           in1=kh[:, g, cols], op0=ALU.mult, op1=ALU.add).then_inc(S["v_kk"], 1)

            def thrice(i, half):
                R, X = ((RAh, XAh), (RAl, XAl), (RB, XB), (RC_, XC))[i]
                if i == 0:
                    dve.wait_ge(S["v_lo"], 2 + 2 * half)
                c0 = half * GROUPS * HALF
                V.tensor_copy(R[:, c0:c0 + GROUPS * HALF].rearrange("p (b g q) -> p b g q", b=PAIRS, g=GROUPS),
                              X[:, half * HALF:(half + 1) * HALF].rearrange("p (b q) -> p b q", b=PAIRS).unsqueeze(
                                  2).to_broadcast([X.shape[0], PAIRS, GROUPS, POSITIONS])).then_inc(S["v_xr"], 1)

            rsqrt(2)
            low_parts(0, (1, 2, 0), 0)
            normed(0, (3, 4))
            attention_low(0, VC, AW)
            kq_low(0)
            attention_low(1, VC, AW)
            kq_low(1)
            kq_low(2)
            low_parts(0, (1, 2, 0), 1)
            for f in range(3, 12):
                kq_low(f)
                if 3 <= f < 7:
                    thrice(f - 3, 0)
                if 7 <= f < 11:
                    thrice(f - 7, 1)

            def differences(u):
                dve.wait_ge(S["p_s"], u + 1)
                s = PS[0:QROWS, 3:7, 0:SCOLS].rearrange("p r (h k) -> p r h k", k=POSITIONS)
                V.tensor_reduce(mx[:, u % 2], s, AX.X, ALU.max).then_inc(S["v_max"], 1)
                dve.wait_ge(S["v_max"], u + 1)
                if u >= 2:
                    dve.wait_ge(S["a_exp"], u - 1)
                V.tensor_tensor(sdif[:, u % 2].rearrange("p r (h k) -> p r h k", k=POSITIONS), s,
                                mx[:, u % 2].unsqueeze(3).to_broadcast([QROWS, LANES, 6, POSITIONS]),
                                ALU.subtract).then_inc(S["v_sub"], 1)

            def own_values(i):
                dve.wait_ge(S["p_v"], i + 1)
                V.scalar_tensor_tensor(
                    out=vm[:, 2 * i:2 * i + 2, :],
                    in0=PS[0:BLOCK, (7, 0, 1, 2)[i % 4], 0:2 * D].rearrange("p (b d) -> p b d", b=2), scalar=SV / XW,
                    in1=bmask[0:BLOCK, :].unsqueeze(1).to_broadcast([BLOCK, 2, D]), op0=ALU.mult,
                    op1=ALU.mult).then_inc(S["v_vm"], 1)

            def pt_low(p):
                dve.wait_ge(S["a_pth"], p + 1)
                V.scalar_tensor_tensor(out=PTl[:, p].rearrange("p r q -> p (r q)"),
                                       in0=PS[0:BLOCK, (7, 0)[p % 2], 0:LANES * QROWS], scalar=SP_,
                                       in1=PTh[:, p].rearrange("p r q -> p (r q)"), op0=ALU.mult,
                                       op1=ALU.subtract).then_inc(S["v_ptl"], 1)

            def normalise(p):
                dve.wait_ge(S["p_av"], p // 2 * 2 + 2)
                c0 = (p % 2) * LANES * VW
                o = PS[0:QROWS, 1 if p < 6 else 6, c0:c0 + LANES * VW].rearrange("p (r c) -> p r c", r=LANES)
                V.reciprocal(rden[:, p], o[:, :, GROUPS * HD:VW]).then_inc(S["v_rd"], 1)
                dve.wait_ge(S["v_rd"], p + 1)
                V.tensor_tensor(cn[:, p, 0:D].rearrange("p (r g d) -> p r g d", r=LANES, g=GROUPS),
                                o[:, :, 0:GROUPS * HD].rearrange("p r (g d) -> p r g d", g=GROUPS),
                                rden[:, p].unsqueeze(3).to_broadcast([QROWS, LANES, GROUPS, HD]),
                                ALU.mult).then_inc(S["v_cn"], 1)

            def ctx_low(i):
                dve.wait_ge(S["a_chi"], 2 * i + 2)
                for k, (C, hi, rows) in enumerate(((CAl, CAh, P), (CC, CB, 64))):
                    for pr in (0, 1):
                        p = 2 * i + pr
                        last = V.tensor_tensor(pair_cols(C, p, rows), pair_queries(2 if i < 3 else 7, pr, k, rows),
                                               pair_cols(hi, p, rows), ALU.subtract)
                last.then_inc(S["v_clo"], 2)

            for i in range(4):
                own_values(i)
            ffn_low(0, 0)
            ffn_low(0, 1)
            differences(0)
            for i in range(4, 7):
                own_values(i)
            for u in range(4):
                if u < 3:
                    differences(u + 1)
                pt_low(2 * u)
                pt_low(2 * u + 1)
                if u == 0:
                    own_values(7)
                if u >= 1:
                    normalise(2 * u - 2)
                    normalise(2 * u - 1)
                if u >= 2:
                    ctx_low(u - 2)
                for q in ((), (2, 3, 4), (5,), ())[u]:
                    ffn_low(0, q)
            def add_attention(t):
                dve.wait_ge(S["p_wo"], (2, 2, 4, 4, 5)[t])
                return V.scalar_tensor_tensor(
                    out=h2[:, t, :], in0=PS[:, (3, 3, 4, 4, 5)[t], D * (t % 2):D * (t % 2) + D],
                    scalar=1.0 / (SCTX * SW), in1=h1[:, t, :], op0=ALU.mult, op1=ALU.add)

            normalise(6)
            normalise(7)
            ctx_low(2)
            residual(1, add_attention, (0, 1))
            ctx_low(3)

            V.memset(ah[:, :, N:NPAD], 0.0)
            V.memset(al[:, :, N:NPAD], 0.0).then_inc(S["v_pad"], 1)
            residual(1, add_attention, (2, 3))
            residual(1, add_attention, (4,))
            variances(3)
            rsqrt(3)
            dve.wait_ge(S["p_t"], TILES)
            normed(1, range(TILES))
            low_parts(1, (0, 1, 2), 0)
            low_parts(1, (0, 1, 2), 1)

            gate = [0]

            def gstep(instruction):
                instruction.then_inc(S["v_gate"], 1)
                gate[0] += 1
                dve.wait_ge(S["v_gate"], gate[0])

            def over8(v):
                return v.unsqueeze(2).to_broadcast([P, TILES, 8])

            m1, s1, m2, s2, den, rd_ = (small[:, i, :] for i in (32, 33, 34, 35, 36, 37))
            l8 = lg[:, :, 0:8]
            rank = cst_rank[:, :].unsqueeze(1).to_broadcast([P, TILES, 8])

            dve.wait_ge(S["p_r"], 1)
            V.tensor_scalar(lg[:, :, :], PS[:, 7, 0:9 * TILES].rearrange("p (t e) -> p t e", t=TILES), 1.0 / XW, None,
                            ALU.mult).then_inc(S["v_lg"], 1)
            dve.wait_ge(S["v_lg"], 1)
            V.tensor_reduce(m1, l8, AX.X, ALU.max).then_inc(S["v_bn"], 1)
            dve.wait_ge(S["v_bn"], bn[0] + 1)
            gstep(V.tensor_tensor(g8[:, 0], l8, over8(m1), ALU.subtract))

            def choose_first():
                gstep(V.tensor_tensor(g8[:, 2], l8, over8(m1), ALU.is_equal))
                gstep(V.tensor_tensor(g8[:, 3], g8[:, 2], rank, ALU.mult))
                gstep(V.tensor_reduce(s1, g8[:, 3], AX.X, ALU.max))
                gstep(V.tensor_tensor(g8[:, 4], rank, over8(s1), ALU.is_equal))

            def second_largest():
                gstep(V.scalar_tensor_tensor(out=g8[:, 5], in0=g8[:, 4], scalar=-3e38, in1=l8, op0=ALU.mult,
                                             op1=ALU.add))
                gstep(V.tensor_reduce(m2, g8[:, 5], AX.X, ALU.max))
                gstep(V.tensor_tensor(g8[:, 6], g8[:, 5], over8(m2), ALU.is_equal))

            def choose_second():
                gstep(V.tensor_tensor(g8[:, 7], g8[:, 6], rank, ALU.mult))
                gstep(V.tensor_reduce(s2, g8[:, 7], AX.X, ALU.max))
                gstep(V.tensor_tensor(g8[:, 8], rank, over8(s2), ALU.is_equal))
                gstep(V.tensor_tensor(g8[:, 9], g8[:, 8], g8[:, 4], ALU.add))

            def gate_sum():
                dve.wait_ge(S["a_e"], 1)
                gstep(V.tensor_tensor(g8[:, 10], g8[:, 9], g8[:, 1], ALU.mult))
                gstep(V.tensor_reduce(den, g8[:, 10], AX.X, ALU.add))
                gstep(V.reciprocal(rd_, den))

            def gate_split():
                dve.wait_ge(S["a_sig"], 2)
                gstep(V.tensor_scalar(small[:, 40:42, :], small[:, 30:32, :], 1.0, None, ALU.add))
                gstep(V.reciprocal(small[:, 42:44, :], small[:, 40:42, :]))
                gstep(V.tensor_scalar(small[:, 38, :], small[:, 42, :], 1.0 / (SH * SW), None, ALU.mult))
                gstep(V.scalar_tensor_tensor(out=small[:, 39, :], in0=rd_, scalar=1.0, in1=small[:, 43, :],
                                             op0=ALU.mult, op1=ALU.mult))
                V.tensor_tensor(Gf[:, :, :], g8[:, 10], over8(small[:, 39, :]), ALU.mult).then_inc(S["v_gx"], 1)

            def product(i):
                dve.wait_ge(S["a_silu"], i + 1)
                src = silu
                f, half = divmod(i, 2)
                if two_experts(f) or f == FT - 1:
                    dve.wait_ge(d_g[f_expert(f)[0]], 16)
                    dve.wait_ge(d_g[f_expert(f)[1]], 16)
                    cols = slice(half * HALF, (half + 1) * HALF)
                    e0, e1 = f_expert(f)
                    for r0, r1, e in ((0, 64, e0), (64, P, e1)) if e0 != e1 else ((0, P, e0),):
                        last = V.tensor_tensor(sgate[r0:r1, i % 2, :], silu[r0:r1, i % 2, :],
                                               Gb[r0:r1, e, cols], ALU.mult)
                    last.then_inc(S["v_sg"], 1)
                    dve.wait_ge(S["v_sg"], 2 * ((f - ST) // 3 + (f == FT - 1)) + half + 1)
                elif f >= ST:
                    dve.wait_ge(S["g_sg"], 4 * ((f - ST) // 3) + (f - ST) % 3 + half + 1)
                if f >= ST:
                    src = sgate
                if i >= 3:
                    dve.wait_ge(S["g_al"], i - 2)
                V.scalar_tensor_tensor(out=hf[:, i % 3, :], in0=PS[:, 4 + 2 * (i % 2), 0:HALF], scalar=SH / XW,
                                       in1=src[:, i % 2, :], op0=ALU.mult, op1=ALU.mult).then_inc(S["v_hf"], 1)

            for i in range(2 * FT):
                product(i)
                if i == 0:
                    choose_first()
                if i == 1:
                    second_largest()
                if i == 2:
                    choose_second()
                if i == 3:
                    gate_sum()
                if i == 4:
                    gate_split()
                if 5 <= i < 11:
                    ffn_low(1, i - 5)
                if i in (10, 12, 13, 17, 18, 19):
                    ffn_low(2, (10, 12, 13, 17, 18, 19).index(i))
                if i == 2 * ST + 3:
                    dve.wait_ge(S["p_dn"], ST)
                    for t in range(TILES):
                        V.scalar_tensor_tensor(out=acc[:, t, :], in0=PS[:, t // 2, D * (t % 2):D * (t % 2) + D],
                                               scalar=small[:, 38, t:t + 1], in1=h2[:, t, :], op0=ALU.mult,
                                               op1=ALU.add).then_inc(S["v_acc"], 1)
            dve.wait_ge(S["a_ah"], 2 * FT)
            V.tensor_tensor(al[:, (FT - 1) % ABUF, HALF:N], hf[:, (2 * FT - 1) % 3, :],
                            ah[:, (FT - 1) % ABUF, HALF:N], ALU.subtract).then_inc(S["v_al"], 1)
            for t in range(TILES):
                dve.wait_ge(S["p_end"], t // 2 + 1)
                V.scalar_tensor_tensor(out=fin[:, t, 0:D], in0=PS[:, t // 2, D * (t % 2):D * (t % 2) + D],
                                       scalar=1.0 / (SH * SW), in1=acc[:, t, :], op0=ALU.mult,
                                       op1=ALU.add).then_inc(S["v_fin"], 1)


def _fold_layout(v):
    import numpy as np
    w = v.reshape(16, 16, 5, 3, -1)
    inner = np.zeros((SHIFTS, 3, 16, 16, w.shape[-1]), v.dtype)
    m = np.moveaxis(w, (2, 3), (0, 1))
    inner[0] = m[0]
    inner[1, :, :, :-1] = m[1, :, :, 1:]
    inner[2, :, :, 1:] = m[2, :, :, :-1]
    inner[3, :, :-1] = m[3, :, 1:]
    inner[4, :, 1:] = m[4, :, :-1]
    ring = np.stack([m[3, :, 0], m[4, :, 15], m[1, :, :, 0], m[2, :, :, 15]], 1)
    return inner.reshape(SHIFTS, 768, -1), ring.reshape(192, -1)


def _chunks(a, n):
    return a.reshape(n, -1, a.shape[-1]).swapaxes(0, 1)


def _pad_rows(a, rows=P):
    import numpy as np
    out = np.zeros((rows,) + a.shape[1:], a.dtype)
    out[:a.shape[0]] = a
    return out


def _layouts(x, cls_tok, L0_tok_ln_gamma, L0_tok_ln_beta, L0_tok_W, L0_tok_b, L0_attn_w_q, L0_attn_b_q, L0_attn_w_k,
             L0_attn_b_k, L0_attn_w_v, L0_attn_b_v, L0_attn_w_o, L0_attn_b_o, L0_attn_bias_table, L0_ffn_router_w,
             L0_ffn_w_gate, L0_ffn_w_up, L0_ffn_w_down, L0_ffn_ws_gate, L0_ffn_ws_up, L0_ffn_ws_down, L0_ffn_sg_w,
             L0_ffn_sg_b):
    import numpy as np
    f32 = np.float32
    xp = np.zeros((16, 3, 98, 98), x.dtype)
    xp[:, :, 1:97, 1:97] = x
    inner = np.zeros((3, 16, 16, 16, 37), x.dtype)
    ring = np.zeros((3, 4, 16, 16, 37), x.dtype)
    for py in range(6):
        for px in range(6):
            w = xp[:, :, 16 * py:16 * py + 18, 16 * px:16 * px + 18]
            t = 1 + 6 * py + px
            inner[..., t] = w[:, :, 1:17, 1:17].transpose(1, 2, 3, 0)
            for k, side in enumerate((w[:, :, 0, 1:17], w[:, :, 17, 1:17], w[:, :, 1:17, 0], w[:, :, 1:17, 17])):
                ring[:, k, :, :, t] = side.transpose(1, 2, 0)
    wi, wr = _fold_layout(L0_tok_W)
    gi, gr = _fold_layout(L0_tok_ln_gamma[:, None])
    bi, br = _fold_layout(L0_tok_ln_beta[:, None])
    ci, cr = _fold_layout(np.ones((PATCH_DIM, 1), f32))
    cnt = np.concatenate([_chunks(ci.sum(0), INNER)[..., 0], _pad_rows(_chunks(cr, RING)[..., 0])], 1)
    gb = np.stack([np.concatenate([v.reshape(SHIFTS * INNER, P).T, _pad_rows(_chunks(r, RING)[..., 0])], 1)
                   for v, r in ((gi, gr), (bi, br))], 1)
    rows = np.arange(P)
    own = np.repeat(rows[:, None] // POSITIONS == np.arange(GROUPS)[None, :], HD, 1)
    consts = np.concatenate([
        np.eye(P), cnt, np.where(rows % 32 < HD, 0, -SK / XW)[:, None], np.tile(own, (1, LANES)),
        rows[:, None] // POSITIONS == np.arange(GROUPS)[None, :],
        np.broadcast_to(np.arange(EXPERTS, 0, -1), (P, EXPERTS)), np.sqrt(cnt)], 1).astype(f32)
    qk = (4 * np.arange(GROUPS)[:, None, None, None] + np.arange(LANES)[:, None, None]) * HD + np.arange(HD)
    qk = np.broadcast_to(qk, (GROUPS, LANES, 2, HD)).reshape(-1)
    vo = ((4 * np.arange(GROUPS)[:, None] + np.arange(LANES)[:, None, None]) * HD + np.arange(HD)).reshape(-1)
    aw = np.concatenate([L0_attn_w_q.T[:, qk], L0_attn_w_k.T[:, qk], L0_attn_w_v.T[:, vo], L0_attn_w_o.T[vo],
                         L0_ffn_router_w, L0_ffn_sg_w], 1)
    ab = np.concatenate([L0_attn_b_q[qk], L0_attn_b_k[qk], L0_attn_b_v[vo], L0_attn_b_o,
                         np.zeros(EXPERTS, f32), L0_ffn_sg_b])
    aw_c = np.zeros((CROWS, AW), f32)
    aw_c[0:64], aw_c[64], aw_c[96] = aw[P:], ab, ab
    fo = np.concatenate([np.arange(128), np.arange(128, 192), HID + np.arange(128, 192), HID + np.arange(128)])
    fo = (2 * HID * np.arange(EXPERTS // 2)[:, None] + fo).reshape(-1)
    up = [np.concatenate([s, e.transpose(1, 0, 2).reshape(D, -1)[:, fo]], 1)
          for s, e in ((L0_ffn_ws_gate, L0_ffn_w_gate), (L0_ffn_ws_up, L0_ffn_w_up))]
    up = np.stack(up, 1)
    down = np.concatenate([L0_ffn_ws_down, L0_ffn_w_down.reshape(-1, D)[fo]], 0)
    first = (np.arange(NPAD) % POSITIONS == 0) & (np.arange(NPAD) < N)
    j = np.arange(POSITIONS)
    mid = (L0_attn_bias_table.shape[0] - 1) // 2
    return {
        "x_inner": _chunks(inner.reshape(768, N), INNER), "x_ring": _chunks(ring.reshape(192, N), RING),
        "w_inner": np.stack([_chunks(v, INNER) for v in wi]), "w_ring": _chunks(wr, RING),
        "gb": gb, "consts": consts, "j_rev": (j[:, None] + j == POSITIONS - 1).astype(f32),
        "ind": np.stack([~first & (np.arange(NPAD) < N), first]).astype(f32),
        "tok_b": L0_tok_b[None, :], "cls": cls_tok.reshape(1, D),
        "tab": L0_attn_bias_table[mid - (POSITIONS - 1) + j[:, None] + j],
        "aw_a": aw[0:P], "aw_b": np.concatenate([aw[P:], aw[P:]], 0), "aw_c": aw_c,
        "f_a": up[0:P], "f_b": np.concatenate([up[P:], up[P:]], 0), "f_d": _chunks(down, FT),
    }


def kernel(**inputs):
    import numpy as _np
    import concourse.bacc as _bacc
    from concourse.bass_utils import run_bass_kernel_spmd as _run

    nc = _bacc.Bacc("TRN2", target_bir_lowering=False, num_devices=1)
    arrays, aps = {}, {}
    for name, a in _layouts(**{k: _np.asarray(v) for k, v in inputs.items()}).items():
        a = _np.ascontiguousarray(a)
        arrays[f"in_{name}_dram"] = a
        aps[name] = nc.dram_tensor(f"in_{name}_dram", a.shape, mybir.dt.from_np(a.dtype), kind="ExternalInput").ap()
    out = nc.dram_tensor("out_0_dram", (N, D), F32, kind="ExternalOutput").ap()
    gate_rows = nc.dram_tensor("gate_rows_dram", (EXPERTS, N), F32).ap()
    vit_kernel(nc, gate_rows=gate_rows, out=out, **aps)
    r = _run(nc, [arrays], core_ids=[0])
    return r.results[0]["out_0_dram"].reshape(IMAGES, POSITIONS, D)
```
